# Optimizing a Trainium2 kernel written in Bass

```python
import numpy as np
import jax
import jax.numpy as jnp

def _softmax(x, axis=-1):
    return jax.nn.softmax(x, axis=axis)

def _gelu(x):
    return jax.nn.gelu(x, approximate=True)

def _silu(x):
    return jax.nn.silu(x)

def _sigmoid(x):
    return jax.nn.sigmoid(x)

def _layernorm(x, axis=-1, eps=1e-05):
    m = jnp.mean(x, axis=axis, keepdims=True)
    v = jnp.var(x, axis=axis, keepdims=True)
    return (x - m) / jnp.sqrt(v + eps)

def _scatter_add(tgt, idx, src, axis=0):
    return tgt.at[idx].add(src)

def _segment_sum(src, seg, n):
    return jax.ops.segment_sum(src, seg, n)
kernel_name = 'mk_flamingo_gated_d4_seqx_r8_942a25'

def setup_inputs(seed: int=0):
    np.random.seed(seed)
    _w = jnp.asarray

    def _rec_inputs():
        import jax
        import jax.numpy as jnp
        _rk = jax.random.key(seed)
        x = -0.0002928 + 1 * jax.random.normal(jax.random.fold_in(_rk, 1), (32, 128, 128), jnp.float32)
        _lenS = 128 - jax.random.randint(jax.random.fold_in(_rk, 7), (32,), 0, max(1, 128 // 4) + 1, jnp.int32)
        _lenS2 = 128 - jax.random.randint(jax.random.fold_in(_rk, 8), (32,), 0, max(1, 128 // 4) + 1, jnp.int32)
        _ctx_1024P = jax.random.normal(jax.random.fold_in(_rk, 11), (32, 16, 128), jnp.float32)
        _ctx_1024c = jax.random.dirichlet(jax.random.fold_in(_rk, 511), 0.3 * jnp.ones((16,), jnp.float32), (32, 128))
        _ctx_1024t = jnp.einsum('bsk,bkd->bsd', _ctx_1024c, _ctx_1024P)
        _ctx_1024t = _ctx_1024t * jax.lax.rsqrt(jnp.mean(jnp.square(_ctx_1024t)) + 1e-12) * 0.953939
        ctx_1024 = -1.39393e-06 + 0.999914 * (_ctx_1024t + 0.3 * jax.random.normal(jax.random.fold_in(_rk, 611), (32, 128, 128), jnp.float32))
        _validS = jnp.arange(128)[None, :] < _lenS[:, None]
        _validS2 = jnp.arange(128)[None, :] < _lenS2[:, None]
        _causal = jnp.tril(jnp.ones((128, 128), dtype=bool))
        mask_BxSxS2_if1 = jnp.where(jnp.ones((32, 128, 128), dtype=bool), 1, 0).astype(jnp.int32)
        mask_1x1xSxS2_bf1 = jnp.ones((1, 1, 128, 128), dtype=bool)
        _g = jax.random.normal(jax.random.fold_in(_rk, 9001), (2, 4), jnp.float32)
        _g = jnp.sign(_g) * jnp.maximum(jnp.abs(_g), 1.0) + (_g == 0) * 1.0
        g_xattn = _g[0]
        g_ffn = _g[1]
        return (x, ctx_1024, mask_BxSxS2_if1, mask_1x1xSxS2_bf1, g_xattn, g_ffn)
    x, ctx_1024, mask_BxSxS2_if1, mask_1x1xSxS2_bf1, g_xattn, g_ffn = _rec_inputs()

    def _L0_xattn_setup():
        import jax, jax.numpy as jnp
        import numpy as np
        D_MODEL = 128
        HEADS = 16
        D_K = D_MODEL // HEADS
        key = jax.random.key(seed)
        ks = jax.random.split(key, 8)
        B, S = (2, 256)
        scale = 1.0 / np.sqrt(D_MODEL)
        return {'q': jax.random.normal(ks[0], (B, S, D_MODEL), dtype=jnp.float32), 'k': jax.random.normal(ks[1], (B, S, D_MODEL), dtype=jnp.float32), 'v': jax.random.normal(ks[2], (B, S, D_MODEL), dtype=jnp.float32), 'mask': jnp.ones((B, S, S), dtype=jnp.int32), 'w_q': jax.random.normal(ks[3], (D_MODEL, D_MODEL), dtype=jnp.float32) * scale, 'w_k': jax.random.normal(ks[4], (D_MODEL, D_MODEL), dtype=jnp.float32) * scale, 'w_v': jax.random.normal(ks[5], (D_MODEL, D_MODEL), dtype=jnp.float32) * scale, 'w_o': jax.random.normal(ks[6], (D_MODEL, D_MODEL), dtype=jnp.float32) * scale, 'b_o': jnp.zeros((D_MODEL,), dtype=jnp.float32)}
    _L0_xattn_all = _L0_xattn_setup()
    _L0_xattn_in = {k: v for k, v in _L0_xattn_all.items() if k in ('w_q', 'w_k', 'w_v', 'w_o', 'b_o')}
    del _L0_xattn_all

    def _L0_ffn_setup():
        import jax, jax.numpy as jnp
        import numpy as np
        DIM = 128
        INTER = 128
        N_EXPERTS = 8
        TOPK = 2
        N_SHARED = 2
        key = jax.random.key(seed)
        ks = jax.random.split(key, 10)
        s = 0.02
        return {'x': jax.random.normal(ks[0], (4, 256, DIM), dtype=jnp.float32), 'gate_w': jax.random.normal(ks[1], (N_EXPERTS, DIM), dtype=jnp.float32) * s, 'gate_bias': jax.random.normal(ks[2], (N_EXPERTS,), dtype=jnp.float32) * s, 'w1': jax.random.normal(ks[3], (N_EXPERTS, INTER, DIM), dtype=jnp.float32) * s, 'w3': jax.random.normal(ks[4], (N_EXPERTS, INTER, DIM), dtype=jnp.float32) * s, 'w2': jax.random.normal(ks[5], (N_EXPERTS, DIM, INTER), dtype=jnp.float32) * s, 'sw1': jax.random.normal(ks[6], (N_SHARED * INTER, DIM), dtype=jnp.float32) * s, 'sw3': jax.random.normal(ks[7], (N_SHARED * INTER, DIM), dtype=jnp.float32) * s, 'sw2': jax.random.normal(ks[8], (DIM, N_SHARED * INTER), dtype=jnp.float32) * s}
    _L0_ffn_all = _L0_ffn_setup()
    _L0_ffn_in = {k: v for k, v in _L0_ffn_all.items() if k in ('gate_w', 'gate_bias', 'w1', 'w3', 'w2', 'sw1', 'sw3', 'sw2')}
    del _L0_ffn_all

    def _L1_xattn_setup():
        import jax, jax.numpy as jnp
        import numpy as np
        H = 16
        D_MODEL = 128
        DK = D_MODEL // H
        NEG = -1000000000.0
        key = jax.random.key(seed)
        ks = jax.random.split(key, 12)
        B, S = (2, 256)
        s = 1.0 / np.sqrt(D_MODEL)
        inp = {'q': jax.random.normal(ks[0], (B, S, D_MODEL), jnp.float32), 'k': jax.random.normal(ks[1], (B, S, D_MODEL), jnp.float32), 'v': jax.random.normal(ks[2], (B, S, D_MODEL), jnp.float32), 'mask': jnp.ones((1, 1, S, S), dtype=bool), 'Wq': jax.random.normal(ks[3], (D_MODEL, D_MODEL), jnp.float32) * s, 'bq': jax.random.normal(ks[4], (D_MODEL,), jnp.float32) * 0.02, 'Wk': jax.random.normal(ks[5], (D_MODEL, D_MODEL), jnp.float32) * s, 'bk': jax.random.normal(ks[6], (D_MODEL,), jnp.float32) * 0.02, 'Wv': jax.random.normal(ks[7], (D_MODEL, D_MODEL), jnp.float32) * s, 'bv': jax.random.normal(ks[8], (D_MODEL,), jnp.float32) * 0.02, 'Wo': jax.random.normal(ks[9], (D_MODEL, D_MODEL), jnp.float32) * s, 'bo': jax.random.normal(ks[10], (D_MODEL,), jnp.float32) * 0.02}
        return inp
    _L1_xattn_all = _L1_xattn_setup()
    _L1_xattn_in = {k: v for k, v in _L1_xattn_all.items() if k in ('Wq', 'bq', 'Wk', 'bk', 'Wv', 'bv', 'Wo', 'bo')}
    del _L1_xattn_all

    def _L1_ffn_setup():
        import jax, jax.numpy as jnp
        import numpy as np
        B, T, DIM = (2, 256, 128)
        H, DH, E, K = (16, 64, 8, 2)
        key = jax.random.key(seed)
        ks = jax.random.split(key, 7)
        s = 0.02
        return {'x': jax.random.normal(ks[0], (B, T, DIM), jnp.float32), 'Wq': jax.random.normal(ks[1], (H, DH, DIM), jnp.float32) * s, 'Wk': jax.random.normal(ks[2], (H, DH, DIM), jnp.float32) * s, 'Wv': jax.random.normal(ks[3], (E, DH, DIM), jnp.float32) * s, 'Ws': jax.random.normal(ks[4], (H, E, DIM), jnp.float32) * s, 'Wd': jax.random.normal(ks[5], (H, E, DIM), jnp.float32) * s, 'Wo': jax.random.normal(ks[6], (E, DIM, DH), jnp.float32) * s}
    _L1_ffn_all = _L1_ffn_setup()
    _L1_ffn_in = {k: v for k, v in _L1_ffn_all.items() if k in ('Wq', 'Wk', 'Wv', 'Ws', 'Wd', 'Wo')}
    del _L1_ffn_all

    def _L2_xattn_setup():
        import jax, jax.numpy as jnp
        import numpy as np
        EPS_BACKEND = 1e-06
        NORM_EPS = 1e-06
        NUM_HEADS = 4

        def _mlstm_forward(q, k, v, ig_kernel, ig_bias, fg_kernel, fg_bias, outnorm_weight):
            B, S, E = q.shape
            NH = ig_bias.shape[0]
            DH = E // NH
            gate_input = jnp.concatenate([q, k, v], axis=-1)
            igate = gate_input @ ig_kernel + ig_bias
            fgate = gate_input @ fg_kernel + fg_bias
            qh = q.reshape(B, S, NH, DH).transpose(0, 2, 1, 3)
            kh = k.reshape(B, S, NH, DH).transpose(0, 2, 1, 3)
            vh = v.reshape(B, S, NH, DH).transpose(0, 2, 1, 3)
            ig = igate.transpose(0, 2, 1)
            fg = fgate.transpose(0, 2, 1)
            log_fg = jax.nn.log_sigmoid(fg)
            cums = jnp.concatenate([jnp.zeros((B, NH, 1), log_fg.dtype), jnp.cumsum(log_fg, axis=-1)], axis=-1)
            fg_mat = cums[..., :, None] - cums[..., None, :]
            mask = jnp.tril(jnp.ones((S + 1, S + 1), bool))
            fg_mat = jnp.where(mask, fg_mat, -jnp.inf)[..., 1:, 1:]
            log_D = fg_mat + ig[..., None, :]
            max_log_D = jnp.max(log_D, axis=-1, keepdims=True)
            D = jnp.exp(log_D - max_log_D)
            qk = jnp.einsum('bnsd,bntd->bnst', qh, kh) / jnp.sqrt(jnp.float32(DH))
            C = qk * D
            normalizer = jnp.maximum(jnp.abs(C.sum(-1, keepdims=True)), jnp.exp(-max_log_D))
            h = jnp.einsum('bnst,bntd->bnsd', C / (normalizer + EPS_BACKEND), vh)
            h = h.transpose(0, 2, 1, 3)
            mean = h.mean(-1, keepdims=True)
            var = h.var(-1, keepdims=True)
            hn = (h - mean) * jax.lax.rsqrt(var + NORM_EPS) * outnorm_weight
            return hn.reshape(B, S, E)
        key = jax.random.key(seed)
        ks = jax.random.split(key, 8)
        B, S, E, NH = (2, 256, 128, NUM_HEADS)
        DH = E // NH
        q = jax.random.normal(ks[0], (B, S, E), jnp.float32)
        k = jax.random.normal(ks[1], (B, S, E), jnp.float32)
        v = jax.random.normal(ks[2], (B, S, E), jnp.float32)
        ig_kernel = jax.random.normal(ks[3], (3 * E, NH), jnp.float32) * 0.02
        fg_kernel = jax.random.normal(ks[4], (3 * E, NH), jnp.float32) * 0.02
        ig_bias = jax.random.normal(ks[5], (NH,), jnp.float32) * 0.1
        fg_bias = jnp.linspace(3.0, 6.0, NH, dtype=jnp.float32)
        outnorm_weight = jnp.ones((NH, DH), jnp.float32)
        return {'q': q, 'k': k, 'v': v, 'ig_kernel': ig_kernel, 'ig_bias': ig_bias, 'fg_kernel': fg_kernel, 'fg_bias': fg_bias, 'outnorm_weight': outnorm_weight}
    _L2_xattn_all = _L2_xattn_setup()
    _L2_xattn_in = {k: v for k, v in _L2_xattn_all.items() if k in ('ig_kernel', 'ig_bias', 'fg_kernel', 'fg_bias', 'outnorm_weight')}
    del _L2_xattn_all

    def _L2_ffn_setup():
        import jax, jax.numpy as jnp
        import numpy as np
        B, S, D_MODEL, D_HIDDEN = (4, 256, 128, 512)

        def act_quant(x):
            scale = 127.0 / jnp.clip(jnp.max(jnp.abs(x), axis=-1, keepdims=True), 1e-05)
            return jnp.clip(jnp.round(x * scale), -128, 127) / scale

        def weight_quant(w):
            scale = 1.0 / jnp.clip(jnp.mean(jnp.abs(w)), 1e-05)
            return jnp.clip(jnp.round(w * scale), -1, 1) / scale

        def bit_linear(x, w):
            xq = x + jax.lax.stop_gradient(act_quant(x) - x)
            wq = w + jax.lax.stop_gradient(weight_quant(w) - w)
            return jnp.einsum('bsd,hd->bsh', xq, wq)

        def depthwise_conv1d(x_bcl, w, b):
            y = jax.lax.conv_general_dilated(x_bcl, w, window_strides=(1,), padding=[(1, 1)], dimension_numbers=('NCH', 'OIH', 'NCH'), feature_group_count=x_bcl.shape[1])
            return y + b[None, :, None]
        key = jax.random.key(seed)
        ks = jax.random.split(key, 5)
        lim1 = 1.0 / np.sqrt(D_MODEL)
        lim2 = 1.0 / np.sqrt(D_HIDDEN)
        limc = 1.0 / np.sqrt(3.0)
        return {'x': jax.random.normal(ks[0], (B, S, D_MODEL), dtype=jnp.float32), 'w1': jax.random.uniform(ks[1], (D_HIDDEN, D_MODEL), jnp.float32, -lim1, lim1), 'conv_w': jax.random.uniform(ks[2], (D_HIDDEN, 1, 3), jnp.float32, -limc, limc), 'conv_b': jax.random.uniform(ks[3], (D_HIDDEN,), jnp.float32, -limc, limc), 'w2': jax.random.uniform(ks[4], (D_MODEL, D_HIDDEN), jnp.float32, -lim2, lim2)}
    _L2_ffn_all = _L2_ffn_setup()
    _L2_ffn_in = {k: v for k, v in _L2_ffn_all.items() if k in ('w1', 'conv_w', 'conv_b', 'w2')}
    del _L2_ffn_all

    def _L3_xattn_setup():
        import jax, jax.numpy as jnp
        import numpy as np
        D_MODEL = 128
        D_FF = 512
        LN_EPS = 1e-05

        def _layer_norm(x, gamma, beta):
            mu = jnp.mean(x, axis=-1, keepdims=True)
            var = jnp.var(x, axis=-1, keepdims=True)
            return (x - mu) * jax.lax.rsqrt(var + LN_EPS) * gamma + beta
        key = jax.random.key(seed)
        ks = jax.random.split(key, 16)
        B, S, D, F = (4, 256, D_MODEL, D_FF)
        s = 0.02
        return {'queries': jax.random.normal(ks[0], (B, S, D), jnp.float32), 'keys': jax.random.normal(ks[1], (B, S, D), jnp.float32), 'values': jax.random.normal(ks[2], (B, S, D), jnp.float32), 'Wq': jax.random.normal(ks[3], (D, D), jnp.float32) * s, 'bq': jnp.zeros((D,), jnp.float32), 'Wk': jax.random.normal(ks[4], (D, D), jnp.float32) * s, 'bk': jnp.zeros((D,), jnp.float32), 'Wv': jax.random.normal(ks[5], (D, D), jnp.float32) * s, 'bv': jnp.zeros((D,), jnp.float32), 'Wo': jax.random.normal(ks[6], (D, D), jnp.float32) * s, 'bo': jnp.zeros((D,), jnp.float32), 'W1': jax.random.normal(ks[7], (D, F), jnp.float32) * s, 'b1': jnp.zeros((F,), jnp.float32), 'W2': jax.random.normal(ks[8], (F, D), jnp.float32) * s, 'b2': jnp.zeros((D,), jnp.float32), 'ln1_g': jnp.ones((D,), jnp.float32), 'ln1_b': jnp.zeros((D,), jnp.float32), 'ln2_g': jnp.ones((D,), jnp.float32), 'ln2_b': jnp.zeros((D,), jnp.float32)}
    _L3_xattn_all = _L3_xattn_setup()
    _L3_xattn_in = {k: v for k, v in _L3_xattn_all.items() if k in ('Wq', 'bq', 'Wk', 'bk', 'Wv', 'bv', 'Wo', 'bo', 'W1', 'b1', 'W2', 'b2', 'ln1_g', 'ln1_b', 'ln2_g', 'ln2_b')}
    del _L3_xattn_all

    def _L3_ffn_setup():
        import jax, jax.numpy as jnp
        import numpy as np
        DIM = 128
        N_EXPERTS = 16
        TOP_K = 4
        N_GROUP = 4
        TOPK_GROUP = 2
        MOE_INTER = 64
        SHARED_INTER = 256
        ROUTED_SCALE = 2.5

        def relu2(x):
            return jnp.square(jax.nn.relu(x))

        def _router(x2, gate_w, bias_e):
            T = x2.shape[0]
            logits = x2 @ gate_w.T
            scores = jax.nn.sigmoid(logits)
            sc = jax.lax.stop_gradient(scores + bias_e[None, :])
            grp = sc.reshape(T, N_GROUP, N_EXPERTS // N_GROUP)
            top2, _ = jax.lax.top_k(grp, 2)
            group_scores = top2.sum(-1)
            _, gidx = jax.lax.top_k(group_scores, TOPK_GROUP)
            rows = jnp.arange(T)[:, None]
            gmask = jnp.zeros((T, N_GROUP), dtype=sc.dtype).at[rows, gidx].set(1.0)
            smask = jnp.repeat(gmask, N_EXPERTS // N_GROUP, axis=1)
            masked = jnp.where(smask > 0, sc, 0.0)
            _, topk_idx = jax.lax.top_k(masked, TOP_K)
            topk_w = jnp.take_along_axis(scores, topk_idx, axis=1)
            topk_w = topk_w / (topk_w.sum(-1, keepdims=True) + 1e-20)
            topk_w = topk_w * ROUTED_SCALE
            return (topk_idx, topk_w)
        key = jax.random.key(seed)
        ks = jax.random.split(key, 6)
        hidden_states = jax.random.normal(ks[0], (2, 256, DIM), dtype=jnp.float32)
        gate_w = jax.random.normal(ks[1], (N_EXPERTS, DIM), dtype=jnp.float32) * 0.02
        bias_e = jnp.zeros((N_EXPERTS,), dtype=jnp.float32)
        up_w = jax.random.normal(ks[2], (N_EXPERTS, MOE_INTER, DIM), dtype=jnp.float32) * 0.02
        down_w = jax.random.normal(ks[3], (N_EXPERTS, DIM, MOE_INTER), dtype=jnp.float32) * 0.02
        shared_up = jax.random.normal(ks[4], (SHARED_INTER, DIM), dtype=jnp.float32) * 0.02
        shared_down = jax.random.normal(ks[5], (DIM, SHARED_INTER), dtype=jnp.float32) * 0.02
        return {'hidden_states': hidden_states, 'gate_w': gate_w, 'bias_e': bias_e, 'up_w': up_w, 'down_w': down_w, 'shared_up': shared_up, 'shared_down': shared_down}
    _L3_ffn_all = _L3_ffn_setup()
    _L3_ffn_in = {k: v for k, v in _L3_ffn_all.items() if k in ('gate_w', 'bias_e', 'up_w', 'down_w', 'shared_up', 'shared_down')}
    del _L3_ffn_all
    return {'x': x, 'ctx_1024': ctx_1024, 'mask_BxSxS2_if1': mask_BxSxS2_if1, 'mask_1x1xSxS2_bf1': mask_1x1xSxS2_bf1, 'g_xattn': g_xattn, 'g_ffn': g_ffn, 'L0_xattn_w_q': _L0_xattn_in['w_q'], 'L0_xattn_w_k': _L0_xattn_in['w_k'], 'L0_xattn_w_v': _L0_xattn_in['w_v'], 'L0_xattn_w_o': _L0_xattn_in['w_o'], 'L0_xattn_b_o': _L0_xattn_in['b_o'], 'L0_ffn_gate_w': _L0_ffn_in['gate_w'], 'L0_ffn_gate_bias': _L0_ffn_in['gate_bias'], 'L0_ffn_w1': _L0_ffn_in['w1'], 'L0_ffn_w3': _L0_ffn_in['w3'], 'L0_ffn_w2': _L0_ffn_in['w2'], 'L0_ffn_sw1': _L0_ffn_in['sw1'], 'L0_ffn_sw3': _L0_ffn_in['sw3'], 'L0_ffn_sw2': _L0_ffn_in['sw2'], 'L1_xattn_Wq': _L1_xattn_in['Wq'], 'L1_xattn_bq': _L1_xattn_in['bq'], 'L1_xattn_Wk': _L1_xattn_in['Wk'], 'L1_xattn_bk': _L1_xattn_in['bk'], 'L1_xattn_Wv': _L1_xattn_in['Wv'], 'L1_xattn_bv': _L1_xattn_in['bv'], 'L1_xattn_Wo': _L1_xattn_in['Wo'], 'L1_xattn_bo': _L1_xattn_in['bo'], 'L1_ffn_Wq': _L1_ffn_in['Wq'], 'L1_ffn_Wk': _L1_ffn_in['Wk'], 'L1_ffn_Wv': _L1_ffn_in['Wv'], 'L1_ffn_Ws': _L1_ffn_in['Ws'], 'L1_ffn_Wd': _L1_ffn_in['Wd'], 'L1_ffn_Wo': _L1_ffn_in['Wo'], 'L2_xattn_ig_kernel': _L2_xattn_in['ig_kernel'], 'L2_xattn_ig_bias': _L2_xattn_in['ig_bias'], 'L2_xattn_fg_kernel': _L2_xattn_in['fg_kernel'], 'L2_xattn_fg_bias': _L2_xattn_in['fg_bias'], 'L2_xattn_outnorm_weight': _L2_xattn_in['outnorm_weight'], 'L2_ffn_w1': _L2_ffn_in['w1'], 'L2_ffn_conv_w': _L2_ffn_in['conv_w'], 'L2_ffn_conv_b': _L2_ffn_in['conv_b'], 'L2_ffn_w2': _L2_ffn_in['w2'], 'L3_xattn_Wq': _L3_xattn_in['Wq'], 'L3_xattn_bq': _L3_xattn_in['bq'], 'L3_xattn_Wk': _L3_xattn_in['Wk'], 'L3_xattn_bk': _L3_xattn_in['bk'], 'L3_xattn_Wv': _L3_xattn_in['Wv'], 'L3_xattn_bv': _L3_xattn_in['bv'], 'L3_xattn_Wo': _L3_xattn_in['Wo'], 'L3_xattn_bo': _L3_xattn_in['bo'], 'L3_xattn_W1': _L3_xattn_in['W1'], 'L3_xattn_b1': _L3_xattn_in['b1'], 'L3_xattn_W2': _L3_xattn_in['W2'], 'L3_xattn_b2': _L3_xattn_in['b2'], 'L3_xattn_ln1_g': _L3_xattn_in['ln1_g'], 'L3_xattn_ln1_b': _L3_xattn_in['ln1_b'], 'L3_xattn_ln2_g': _L3_xattn_in['ln2_g'], 'L3_xattn_ln2_b': _L3_xattn_in['ln2_b'], 'L3_ffn_gate_w': _L3_ffn_in['gate_w'], 'L3_ffn_bias_e': _L3_ffn_in['bias_e'], 'L3_ffn_up_w': _L3_ffn_in['up_w'], 'L3_ffn_down_w': _L3_ffn_in['down_w'], 'L3_ffn_shared_up': _L3_ffn_in['shared_up'], 'L3_ffn_shared_down': _L3_ffn_in['shared_down']}

def reference(x, ctx_1024, mask_BxSxS2_if1, mask_1x1xSxS2_bf1, g_xattn, g_ffn, L0_xattn_w_q, L0_xattn_w_k, L0_xattn_w_v, L0_xattn_w_o, L0_xattn_b_o, L0_ffn_gate_w, L0_ffn_gate_bias, L0_ffn_w1, L0_ffn_w3, L0_ffn_w2, L0_ffn_sw1, L0_ffn_sw3, L0_ffn_sw2, L1_xattn_Wq, L1_xattn_bq, L1_xattn_Wk, L1_xattn_bk, L1_xattn_Wv, L1_xattn_bv, L1_xattn_Wo, L1_xattn_bo, L1_ffn_Wq, L1_ffn_Wk, L1_ffn_Wv, L1_ffn_Ws, L1_ffn_Wd, L1_ffn_Wo, L2_xattn_ig_kernel, L2_xattn_ig_bias, L2_xattn_fg_kernel, L2_xattn_fg_bias, L2_xattn_outnorm_weight, L2_ffn_w1, L2_ffn_conv_w, L2_ffn_conv_b, L2_ffn_w2, L3_xattn_Wq, L3_xattn_bq, L3_xattn_Wk, L3_xattn_bk, L3_xattn_Wv, L3_xattn_bv, L3_xattn_Wo, L3_xattn_bo, L3_xattn_W1, L3_xattn_b1, L3_xattn_W2, L3_xattn_b2, L3_xattn_ln1_g, L3_xattn_ln1_b, L3_xattn_ln2_g, L3_xattn_ln2_b, L3_ffn_gate_w, L3_ffn_bias_e, L3_ffn_up_w, L3_ffn_down_w, L3_ffn_shared_up, L3_ffn_shared_down):
    import jax
    import jax.numpy as jnp

    def _L0_xattn_ref(q, k, v, mask, w_q, w_k, w_v, w_o, b_o):
        import jax, jax.numpy as jnp
        import numpy as np
        D_MODEL = 128
        HEADS = 16
        D_K = D_MODEL // HEADS
        B, S, _ = q.shape

        def split_heads(x, w):
            y = jnp.einsum('bse,de->bsd', x, w)
            return y.reshape(B, S, HEADS, D_K).transpose(0, 2, 1, 3)
        qh, kh, vh = (split_heads(q, w_q), split_heads(k, w_k), split_heads(v, w_v))
        score = jnp.einsum('bhqd,bhkd->bhqk', qh, kh) / jnp.sqrt(jnp.float32(D_K))
        score = jnp.where(mask[:, None, :, :] == 0, -jnp.inf, score)
        attn = jax.nn.softmax(score, axis=-1)
        out = jnp.einsum('bhqk,bhkd->bhqd', attn, vh)
        out = out.transpose(0, 2, 1, 3).reshape(B, S, HEADS * D_K)
        return jnp.einsum('bsd,ed->bse', out, w_o) + b_o

    def _L0_ffn_ref(x, gate_w, gate_bias, w1, w3, w2, sw1, sw3, sw2):
        import jax, jax.numpy as jnp
        import numpy as np
        DIM = 128
        INTER = 128
        N_EXPERTS = 8
        TOPK = 2
        N_SHARED = 2
        shape = x.shape
        xt = x.reshape(-1, shape[-1])
        scores = jax.nn.softmax((xt @ gate_w.T).astype(jnp.float32), axis=-1)
        _, idx = jax.lax.top_k(scores + gate_bias, TOPK)
        weights = jnp.take_along_axis(scores, idx, axis=1).astype(x.dtype)
        y = jnp.zeros_like(xt)
        for e in range(N_EXPERTS):
            gate_e = jnp.sum(jnp.where(idx == e, weights, 0.0), axis=1)
            h = jax.nn.silu(xt @ w1[e].T) * (xt @ w3[e].T)
            y = y + gate_e[:, None] * (h @ w2[e].T)
        z = jax.nn.silu(xt @ sw1.T) * (xt @ sw3.T) @ sw2.T
        return (y + z).reshape(shape)

    def _L1_xattn_ref(q, k, v, mask, Wq, bq, Wk, bk, Wv, bv, Wo, bo):
        import jax, jax.numpy as jnp
        import numpy as np
        H = 16
        D_MODEL = 128
        DK = D_MODEL // H
        NEG = -1000000000.0
        B, S, _ = q.shape

        def proj(x, W, b):
            return (x @ W.T + b).reshape(B, -1, H, DK).transpose(0, 2, 1, 3)
        Q = proj(q, Wq, bq)
        K = proj(k, Wk, bk)
        V = proj(v, Wv, bv)
        scores = jnp.einsum('bhqd,bhkd->bhqk', Q, K) / jnp.sqrt(jnp.float32(DK))
        scores = jnp.where(mask, scores, NEG)
        attn = jax.nn.softmax(scores, axis=-1)
        out = jnp.einsum('bhqk,bhkd->bhqd', attn, V)
        out = out.transpose(0, 2, 1, 3).reshape(B, S, D_MODEL)
        return out @ Wo.T + bo

    def _L1_ffn_ref(x, Wq, Wk, Wv, Ws, Wd, Wo):
        import jax, jax.numpy as jnp
        import numpy as np
        B, T, DIM = (2, 256, 128)
        H, DH, E, K = (16, 64, 8, 2)
        scale = DH ** (-0.5)
        q = jnp.einsum('btc,hdc->bhtd', x, Wq)
        k = jnp.einsum('btc,hdc->bhtd', x, Wk)
        gate_v = jnp.einsum('btc,hec->bthe', x, Ws)
        w, sel = jax.lax.top_k(gate_v, K)
        wsig = jax.nn.sigmoid(w)
        oh = jax.nn.one_hot(sel, E, dtype=x.dtype)
        mix_v = jnp.einsum('bthk,bthke->bthe', wsig, oh)
        proj_v = jnp.einsum('btc,edc->bted', x, Wv)
        v = jnp.einsum('bthe,bted->bhtd', mix_v, proj_v)
        scores = jnp.einsum('bhid,bhjd->bhij', q * scale, k)
        probs = jax.nn.softmax(scores, axis=-1)
        attn = jnp.einsum('bhij,bhjd->bihd', probs, v)
        gate_o = jnp.einsum('btc,hec->bthe', x, Wd)
        _, sel_o = jax.lax.top_k(gate_o, K)
        mask_o = jax.nn.one_hot(sel_o, E, dtype=x.dtype).sum(axis=3)
        res = jnp.einsum('bthe,bthd,efd->bthf', mask_o, attn, Wo)
        return res.sum(axis=2)

    def _L2_xattn_ref(q, k, v, ig_kernel, ig_bias, fg_kernel, fg_bias, outnorm_weight):
        import jax, jax.numpy as jnp
        import numpy as np
        EPS_BACKEND = 1e-06
        NORM_EPS = 1e-06
        NUM_HEADS = 4

        def _mlstm_forward(q, k, v, ig_kernel, ig_bias, fg_kernel, fg_bias, outnorm_weight):
            B, S, E = q.shape
            NH = ig_bias.shape[0]
            DH = E // NH
            gate_input = jnp.concatenate([q, k, v], axis=-1)
            igate = gate_input @ ig_kernel + ig_bias
            fgate = gate_input @ fg_kernel + fg_bias
            qh = q.reshape(B, S, NH, DH).transpose(0, 2, 1, 3)
            kh = k.reshape(B, S, NH, DH).transpose(0, 2, 1, 3)
            vh = v.reshape(B, S, NH, DH).transpose(0, 2, 1, 3)
            ig = igate.transpose(0, 2, 1)
            fg = fgate.transpose(0, 2, 1)
            log_fg = jax.nn.log_sigmoid(fg)
            cums = jnp.concatenate([jnp.zeros((B, NH, 1), log_fg.dtype), jnp.cumsum(log_fg, axis=-1)], axis=-1)
            fg_mat = cums[..., :, None] - cums[..., None, :]
            mask = jnp.tril(jnp.ones((S + 1, S + 1), bool))
            fg_mat = jnp.where(mask, fg_mat, -jnp.inf)[..., 1:, 1:]
            log_D = fg_mat + ig[..., None, :]
            max_log_D = jnp.max(log_D, axis=-1, keepdims=True)
            D = jnp.exp(log_D - max_log_D)
            qk = jnp.einsum('bnsd,bntd->bnst', qh, kh) / jnp.sqrt(jnp.float32(DH))
            C = qk * D
            normalizer = jnp.maximum(jnp.abs(C.sum(-1, keepdims=True)), jnp.exp(-max_log_D))
            h = jnp.einsum('bnst,bntd->bnsd', C / (normalizer + EPS_BACKEND), vh)
            h = h.transpose(0, 2, 1, 3)
            mean = h.mean(-1, keepdims=True)
            var = h.var(-1, keepdims=True)
            hn = (h - mean) * jax.lax.rsqrt(var + NORM_EPS) * outnorm_weight
            return hn.reshape(B, S, E)
        return _mlstm_forward(q, k, v, ig_kernel, ig_bias, fg_kernel, fg_bias, outnorm_weight)

    def _L2_ffn_ref(x, w1, conv_w, conv_b, w2):
        import jax, jax.numpy as jnp
        import numpy as np
        B, S, D_MODEL, D_HIDDEN = (4, 256, 128, 512)

        def act_quant(x):
            scale = 127.0 / jnp.clip(jnp.max(jnp.abs(x), axis=-1, keepdims=True), 1e-05)
            return jnp.clip(jnp.round(x * scale), -128, 127) / scale

        def weight_quant(w):
            scale = 1.0 / jnp.clip(jnp.mean(jnp.abs(w)), 1e-05)
            return jnp.clip(jnp.round(w * scale), -1, 1) / scale

        def bit_linear(x, w):
            xq = x + jax.lax.stop_gradient(act_quant(x) - x)
            wq = w + jax.lax.stop_gradient(weight_quant(w) - w)
            return jnp.einsum('bsd,hd->bsh', xq, wq)

        def depthwise_conv1d(x_bcl, w, b):
            y = jax.lax.conv_general_dilated(x_bcl, w, window_strides=(1,), padding=[(1, 1)], dimension_numbers=('NCH', 'OIH', 'NCH'), feature_group_count=x_bcl.shape[1])
            return y + b[None, :, None]
        h = bit_linear(x, w1)
        h = depthwise_conv1d(h.transpose(0, 2, 1), conv_w, conv_b)
        h = h.transpose(0, 2, 1)
        h = jax.nn.silu(h)
        return bit_linear(h, w2)

    def _L3_xattn_ref(queries, keys, values, Wq, bq, Wk, bk, Wv, bv, Wo, bo, W1, b1, W2, b2, ln1_g, ln1_b, ln2_g, ln2_b):
        import jax, jax.numpy as jnp
        import numpy as np
        D_MODEL = 128
        D_FF = 512
        LN_EPS = 1e-05

        def _layer_norm(x, gamma, beta):
            mu = jnp.mean(x, axis=-1, keepdims=True)
            var = jnp.var(x, axis=-1, keepdims=True)
            return (x - mu) * jax.lax.rsqrt(var + LN_EPS) * gamma + beta
        Q = queries @ Wq + bq
        K = keys @ Wk + bk
        V = values @ Wv + bv
        scale = 1.0 / jnp.sqrt(jnp.float32(Q.shape[-1]))
        scores = jnp.einsum('bqd,bkd->bqk', Q, K) * scale
        attn_w = jax.nn.softmax(scores, axis=-1)
        attn = jnp.einsum('bqk,bkd->bqd', attn_w, V)
        merged = attn @ Wo + bo
        x = queries + keys + values
        x = _layer_norm(x + merged, ln1_g, ln1_b)
        h = jax.nn.relu(x @ W1 + b1) @ W2 + b2
        return _layer_norm(x + h, ln2_g, ln2_b)

    def _L3_ffn_ref(hidden_states, gate_w, bias_e, up_w, down_w, shared_up, shared_down):
        import jax, jax.numpy as jnp
        import numpy as np
        DIM = 128
        N_EXPERTS = 16
        TOP_K = 4
        N_GROUP = 4
        TOPK_GROUP = 2
        MOE_INTER = 64
        SHARED_INTER = 256
        ROUTED_SCALE = 2.5

        def relu2(x):
            return jnp.square(jax.nn.relu(x))

        def _router(x2, gate_w, bias_e):
            T = x2.shape[0]
            logits = x2 @ gate_w.T
            scores = jax.nn.sigmoid(logits)
            sc = jax.lax.stop_gradient(scores + bias_e[None, :])
            grp = sc.reshape(T, N_GROUP, N_EXPERTS // N_GROUP)
            top2, _ = jax.lax.top_k(grp, 2)
            group_scores = top2.sum(-1)
            _, gidx = jax.lax.top_k(group_scores, TOPK_GROUP)
            rows = jnp.arange(T)[:, None]
            gmask = jnp.zeros((T, N_GROUP), dtype=sc.dtype).at[rows, gidx].set(1.0)
            smask = jnp.repeat(gmask, N_EXPERTS // N_GROUP, axis=1)
            masked = jnp.where(smask > 0, sc, 0.0)
            _, topk_idx = jax.lax.top_k(masked, TOP_K)
            topk_w = jnp.take_along_axis(scores, topk_idx, axis=1)
            topk_w = topk_w / (topk_w.sum(-1, keepdims=True) + 1e-20)
            topk_w = topk_w * ROUTED_SCALE
            return (topk_idx, topk_w)
        B, S, D = hidden_states.shape
        x2 = hidden_states.reshape(-1, D)
        T = x2.shape[0]
        topk_idx, topk_w = _router(x2, gate_w, bias_e)
        rows = jnp.arange(T)[:, None]
        combine = jnp.zeros((T, N_EXPERTS), dtype=topk_w.dtype).at[rows, topk_idx].add(topk_w)

        def body(acc, inp):
            wu, wd, cw = inp
            y = relu2(x2 @ wu.T) @ wd.T
            return (acc + cw[:, None] * y, None)
        routed, _ = jax.lax.scan(body, jnp.zeros_like(x2), (up_w, down_w, combine.T))
        shared = relu2(x2 @ shared_up.T) @ shared_down.T
        out = routed + shared
        return out.reshape(B, S, D)
    x = x + jnp.tanh(g_xattn[0]) * _L0_xattn_ref(_layernorm(x, axis=-1), ctx_1024, ctx_1024, mask_BxSxS2_if1, L0_xattn_w_q, L0_xattn_w_k, L0_xattn_w_v, L0_xattn_w_o, L0_xattn_b_o)
    x = x + jnp.tanh(g_ffn[0]) * _L0_ffn_ref(_layernorm(x, axis=-1), L0_ffn_gate_w, L0_ffn_gate_bias, L0_ffn_w1, L0_ffn_w3, L0_ffn_w2, L0_ffn_sw1, L0_ffn_sw3, L0_ffn_sw2)
    x = x + jnp.tanh(g_xattn[1]) * _L1_xattn_ref(_layernorm(x, axis=-1), ctx_1024, ctx_1024, mask_1x1xSxS2_bf1, L1_xattn_Wq, L1_xattn_bq, L1_xattn_Wk, L1_xattn_bk, L1_xattn_Wv, L1_xattn_bv, L1_xattn_Wo, L1_xattn_bo)
    x = x + jnp.tanh(g_ffn[1]) * _L1_ffn_ref(_layernorm(x, axis=-1), L1_ffn_Wq, L1_ffn_Wk, L1_ffn_Wv, L1_ffn_Ws, L1_ffn_Wd, L1_ffn_Wo)
    x = x + jnp.tanh(g_xattn[2]) * _L2_xattn_ref(_layernorm(x, axis=-1), ctx_1024, ctx_1024, L2_xattn_ig_kernel, L2_xattn_ig_bias, L2_xattn_fg_kernel, L2_xattn_fg_bias, L2_xattn_outnorm_weight)
    x = x + jnp.tanh(g_ffn[2]) * _L2_ffn_ref(_layernorm(x, axis=-1), L2_ffn_w1, L2_ffn_conv_w, L2_ffn_conv_b, L2_ffn_w2)
    x = x + jnp.tanh(g_xattn[3]) * _L3_xattn_ref(_layernorm(x, axis=-1), ctx_1024, ctx_1024, L3_xattn_Wq, L3_xattn_bq, L3_xattn_Wk, L3_xattn_bk, L3_xattn_Wv, L3_xattn_bv, L3_xattn_Wo, L3_xattn_bo, L3_xattn_W1, L3_xattn_b1, L3_xattn_W2, L3_xattn_b2, L3_xattn_ln1_g, L3_xattn_ln1_b, L3_xattn_ln2_g, L3_xattn_ln2_b)
    x = x + jnp.tanh(g_ffn[3]) * _L3_ffn_ref(_layernorm(x, axis=-1), L3_ffn_gate_w, L3_ffn_bias_e, L3_ffn_up_w, L3_ffn_down_w, L3_ffn_shared_up, L3_ffn_shared_down)
    return x

_drawn_inputs = setup_inputs


def setup_inputs(seed=0):
    import zlib

    import numpy as np

    out = dict(_drawn_inputs(seed))
    spreads = {'L0_xattn_b_o': (0.0, 0.1),
     'L2_xattn_outnorm_weight': (1.0, 0.2),
     'L3_xattn_bq': (0.0, 0.8),
     'L3_xattn_bk': (0.0, 2.0),
     'L3_xattn_bv': (0.0, 0.8),
     'L3_xattn_bo': (0.0, 0.334),
     'L3_xattn_b1': (0.0, 1.064),
     'L3_xattn_b2': (0.0, 0.297),
     'L3_xattn_ln1_g': (1.0, 0.2),
     'L3_xattn_ln1_b': (0.0, 0.1),
     'L3_xattn_ln2_g': (1.0, 0.2),
     'L3_xattn_ln2_b': (0.0, 0.1),
     'L3_ffn_bias_e': (0.0, 0.718)}
    factors = {'g_ffn': 8.0,
     'L0_ffn_gate_w': 8.0,
     'L0_ffn_gate_bias': 8.0,
     'L0_ffn_w1': 8.0,
     'L0_ffn_w3': 8.0,
     'L0_ffn_w2': 8.0,
     'L0_ffn_sw1': 8.0,
     'L0_ffn_sw3': 8.0,
     'L0_ffn_sw2': 8.0,
     'L1_xattn_bq': 27.436,
     'L1_xattn_bk': 64.0,
     'L1_xattn_bv': 3.202,
     'L1_xattn_bo': 3.203,
     'L1_ffn_Wq': 8.0,
     'L1_ffn_Wk': 8.0,
     'L2_xattn_ig_bias': 64.0,
     'L2_xattn_fg_kernel': 3.794,
     'L3_xattn_Wq': 8.0,
     'L3_xattn_Wk': 8.0,
     'L3_xattn_Wv': 6.241,
     'L3_xattn_Wo': 4.856,
     'L3_ffn_gate_w': 8.0,
     'L3_ffn_up_w': 6.002,
     'L3_ffn_down_w': 5.551,
     'L3_ffn_shared_up': 3.738,
     'L3_ffn_shared_down': 3.354}
    for name, (base, spread) in spreads.items():
        noise = np.random.default_rng([zlib.crc32(name.encode()), seed]).standard_normal(out[name].shape)
        drawn = base * np.exp(spread * noise) if base else spread * noise
        out[name] = jnp.asarray(drawn.astype(out[name].dtype))
    for name, factor in factors.items():
        out[name] = (out[name] * factor).astype(out[name].dtype)
    return out
```

```python
from contextlib import ExitStack

import numpy as np
import concourse.bass as bass
from concourse import mybir

F32 = mybir.dt.float32
BF16 = mybir.dt.bfloat16
I32 = mybir.dt.int32
U8 = mybir.dt.uint8
ALU = mybir.AluOpType
ACT = mybir.ActivationFunctionType
AX = mybir.AxisListType

B, S, D = 32, 128, 128
G = 4
NG = B // G
T = G * S
H, DH = 16, 8
HQ = 4
NEG = -1.0e30
LN_EPS = 1e-5
E0, F0 = 8, 2
E1, D1 = 8, 64
NH2, DH2 = 4, 32
F2 = 512
F3 = 512
E3, I3 = 16, 64
ROUND = 1.5 * 2.0 ** 23
ENGINES = ("pe", "act", "dve", "pool")


class Done:

    def __init__(self, src, n):
        self.src, self.n = src, n


def flat(marks):
    for m in marks:
        if isinstance(m, Done):
            yield m
        elif m is not None:
            yield from flat(m)


class Flow:

    def __init__(self):
        self.steps = {e: [] for e in ENGINES}
        self.waited = {e: {} for e in ENGINES}

    def put(self, eng, step, *after):
        need = {}
        for m in flat(after):
            if m.n > self.waited[eng].get(m.src, -1):
                need[m.src] = max(need.get(m.src, -1), m.n)
        self.waited[eng].update(need)
        self.steps[eng].append((need, step))
        return Done(eng, len(self.steps[eng]))

    def count(self, eng):
        return len(self.steps[eng])


class Slots:

    def __init__(self, items):
        self.free = [(it, ()) for it in items]

    def take(self):
        return self.free.pop(0)

    def give(self, item, *marks):
        self.free.append((item, tuple(flat(marks))))


def weight_columns():
    sizes = dict(
        ident=128, causal=128, triu=128, head4=HQ, rev8=8, rev4=4, rev16=16, sel3=E3 // 2 * 128,
        gates=8,
        wq0=128, wk0=128, wv0=128, wo0=128, bo0=128,
        gw0=E0, gb0=E0, w1_0=(E0 + F0) * 128, w3_0=(E0 + F0) * 128, w2_0=(E0 + F0) * 128,
        wq1=128, bq1=1, wk1=128, bk1=1, wv1=128, bv1=128, wo1=128, bo1=128,
        sq1=H * D1, sk1=H * D1, sv1=E1 * D1, sg1=2 * H * E1, so1=E1 * D1 // 128 * 128,
        gk2=3 * 2 * NH2, gb2=2 * NH2, nw2=128, cw1=F2, conv=3 * F2, convb=F2, cw2=F2,
        wq3=128, bq3=1, wk3=128, bk3=1, wv3=128, bv3=128, wo3=128, bo3=128,
        f1_3=F3, fb1_3=F3 // 128, f2_3=F3, fb2_3=128, g1_3=128, b1_3=128, g2_3=128, b2_3=128,
        gw3=E3, gb3=E3, up3=10 * 128, down3=10 * 128,
    )
    at, cols = 0, {}
    for name, n in sizes.items():
        cols[name] = (at, n)
        at += n
    return cols, at


COLS, NCOLS = weight_columns()


def build(nc, x_in, ctx_in, ctxT_in, mask0_in, mask1_in, w_in, out):
    with ExitStack() as ctx:
        def sb(name, cols, dt=F32, parts=128):
            return ctx.enter_context(nc.sbuf_tensor(name, [parts, cols], dt))

        def sem(name):
            return ctx.enter_context(nc.semaphore(name))

        sems = {e: sem("s_" + e) for e in ENGINES}
        sems["in"] = sem("s_in")
        sems["out"] = sem("s_out")
        s_w = sem("s_w")
        s_step = sem("s_step")

        bank_tensors = [ctx.enter_context(nc.psum_tensor(f"bank{i}", [128, 512], F32)) for i in range(8)]
        banks = Slots([b[:, :] for b in bank_tensors])

        wt = sb("w_sb", NCOLS)

        def w(name, a=0, b=None):
            at, n = COLS[name]
            return wt[:, at + a:at + (n if b is None else b)]

        x_ld, c_ld, cT_ld = sb("x_ld", T), sb("c_ld", T), sb("cT_ld", T)
        m_ld = sb("m_ld", T, I32)
        m1_ld = sb("m1_ld", 128, U8)
        y_st = sb("y_st", T)
        identb, ones, causb = sb("identb", 128, BF16), sb("ones", 128), sb("causb", 128, BF16)
        mb1 = sb("mb1", 128, BF16)
        tg = sb("tg", 8)
        bk1m = sb("bk1m", HQ)
        w2b = sb("w2b", F2, BF16)
        wstat = sb("wstat", 8)
        wconv = w("conv")
        x, ctxN, ctxT = sb("x_sb", T), sb("ctxN", T), sb("ctxT_sb", T)
        mb0 = sb("mb0", T, BF16)
        xn, xnT = sb("xn", T), sb("xnT", T)
        qk = sb("qk", 2 * 8 * T)
        qA, kA = qk[:, 0:8 * T], qk[:, 8 * T:16 * T]
        va = sb("va", 3 * H * (D1 + 1))
        oa = sb("oa", 2 * 1024)
        oT = xnT
        pv1 = sb("pv1", G * E1 * D1)
        prod_mem = sb("prods", 3 * 1024)
        prods = Slots([prod_mem[:, i * 1024:(i + 1) * 1024] for i in range(3)])
        tmps = Slots([prod_mem[:, i * 512:(i + 1) * 512] for i in range(6)])
        Ps = Slots([sb(f"P{i}", 512)[:, :] for i in range(3)])
        PTs = Slots([sb(f"PT{i}", 512)[:, :] for i in range(3)])
        gs, gm, gt = sb("gs", 1024), sb("gm", 1024), sb("gt", 1024)
        gw1_, gw2_ = oa[:, 0:1024], oa[:, 1024:2048]
        small = sb("small", 1024)
        shifts = Slots([(sb(f"nm{i}", 8)[:, :], sb(f"nh{i}", 8, BF16)[:, :], sb(f"nl{i}", 8, BF16)[:, :])
                        for i in range(4)])
        r2 = va[:, 0:G * F2 // 2].bitcast(BF16)
        r2T = va[:, G * F2 // 2:G * F2].bitcast(BF16)
        xqT = sb("xqT", G * 130)

        def b3(ap, n=G):
            return ap.rearrange("p (b c) -> p b c", b=n)

        def bc(ap, axis, n):
            a = ap.unsqueeze(axis)
            shape = list(a.shape)
            shape[axis] = n
            return a.broadcast_to(shape)

        ident = w("ident")
        flow = Flow()

        def pe(step, *after):
            return flow.put("pe", step, *after)

        def act(step, *after):
            return flow.put("act", step, *after)

        def dve(step, *after):
            return flow.put("dve", step, *after)

        def pool(step, *after):
            return flow.put("pool", step, *after)

        load_w = Done("w", 32)
        t_ones = dve(lambda e: e.memset(ones[:, :], 1.0))
        t_idb = dve(lambda e: e.tensor_copy(identb[:, :], ident), load_w)
        dve(lambda e: e.tensor_copy(causb[:, :], w("causal")))
        dve(lambda e: e.tensor_scalar(mb1[:, :], m1_ld[:, :], 0.0, NEG, ALU.is_equal, ALU.mult))
        act(lambda e: e.activation(tg[:, :], w("gates"), ACT.Tanh), load_w)
        dve(lambda e: e.tensor_scalar(bk1m[:, :], w("head4"), w("bk1"), None, ALU.mult))
        pool(lambda e: e.memset(xqT[:, :], 0.0))

        def ternary(name, at):
            t1 = dve(lambda e: e.tensor_reduce(wstat[:, at + 1:at + 2], w(name), AX.X, ALU.add,
                                               apply_absolute_value=True), load_w)
            bank, was = banks.take()
            t2 = pe(lambda e: e.matmul(bank[:, 0:1], ones[:, :], wstat[:, at + 1:at + 2], start=True, stop=True),
                    t1, t_ones, was)
            t3 = dve(lambda e: e.tensor_scalar(wstat[:, at:at + 1], bank[:, 0:1], 1.0 / (D * F2), 1e-5,
                                               ALU.mult, ALU.max), t2)
            banks.give(bank, t3)
            t4 = dve(lambda e: e.reciprocal(wstat[:, at + 2:at + 3], wstat[:, at:at + 1]), t3)
            t5 = dve(lambda e: e.tensor_scalar(w(name), w(name), wstat[:, at + 2:at + 3], ROUND,
                                               ALU.mult, ALU.add), t4)
            t6 = dve(lambda e: e.tensor_scalar(w(name), w(name), ROUND, 1.0, ALU.subtract, ALU.min), t5)
            return dve(lambda e: e.tensor_scalar(w(name), w(name), -1.0, None, ALU.max), t6)

        t_q1 = ternary("cw1", 0)
        t_q2 = ternary("cw2", 4)
        for k in range(3):
            dve(lambda e, k=k: e.scalar_tensor_tensor(wconv[:, k * F2:(k + 1) * F2], w("cw1"), wstat[:, 0:1],
                                                      w("conv", k * F2, (k + 1) * F2), ALU.mult, ALU.mult), t_q1)
        dve(lambda e: e.tensor_copy(w2b[:, :], w("cw2")), t_q2)
        setup, flow = flow, Flow()
        banks = Slots([b[:, :] for b in bank_tensors])

        loads, stored = Done("in", 64), Done("out", 16)
        t_x = dve(lambda e: e.tensor_copy(x[:, :], x_ld[:, :]), loads)
        t_c = act(lambda e: e.activation(ctxN[:, :], c_ld[:, :], ACT.Copy), loads)
        t_cT = act(lambda e: e.activation(ctxT[:, :], cT_ld[:, :], ACT.Copy))
        t_m = dve(lambda e: e.tensor_scalar(mb0[:, :], m_ld[:, :], 0.0, NEG, ALU.is_equal, ALU.mult))
        t_copied = [t_x, t_c, t_cT, t_m]

        smalls = Slots([small[:, 64 * i:64 * i + 64] for i in range(16)])

        def rstd(ve, eps_div, n, *after):
            t1_, w1 = smalls.take()
            y_, w2 = smalls.take()
            t1, y = t1_[:, 0:n], y_[:, 0:n]
            m = dve(lambda e: e.memset(t1, -0.5), w1, w2, *after)
            a = dve(lambda e: e.tensor_scalar(ve, ve, eps_div[0], eps_div[1], ALU.mult, ALU.add))
            p = pool(lambda e: e.tensor_tensor(y, ve, t1, ALU.pow), a, m)
            c = dve(lambda e: e.tensor_tensor(t1, y, y, ALU.mult), p)
            c = dve(lambda e: e.tensor_tensor(t1, t1, ve, ALU.mult), c)
            c = dve(lambda e: e.tensor_scalar(t1, t1, -0.5, 1.5, ALU.mult, ALU.add), c)
            c = dve(lambda e: e.tensor_tensor(ve, y, t1, ALU.mult), c)
            smalls.give(t1_, c)
            smalls.give(y_, c)
            return c

        def layernorm(src, dst, *after):
            st_, w1 = smalls.take()
            mv_, w2 = smalls.take()
            st, mv = b3(st_[:, 0:6 * G]), mv_[:, 0:2 * G].rearrange("p (b c) -> p b c", c=2)
            s3, d3 = b3(src), b3(dst)
            for b in range(G):
                t = dve(lambda e, b=b: e.bn_stats(st[:, b, :], s3[:, b, :]), *after, w1, w2)
            dve(lambda e: e.memset(st_[:, 60:64], 1.0), t)
            for b in range(G):
                t2 = dve(lambda e, b=b: e.bn_aggr(mv[:, b, :], st[:, b, :]))
            t3 = rstd(mv[:, :, 1], (1.0, LN_EPS), G, t2)
            for b in range(G):
                t4 = dve(lambda e, b=b: e.tensor_scalar(d3[:, b, :], s3[:, b, :], mv[:, b, 0:1], mv[:, b, 1:2],
                                                        ALU.subtract, ALU.mult), t3)
            smalls.give(st_, t4)
            smalls.give(mv_, t4)
            return t4

        def turn(src, dst, *after):
            bank, was = banks.take()

            def step(e):
                for b in range(G):
                    r = e.transpose(bank[:, b * 128:(b + 1) * 128], src[:, b * 128:(b + 1) * 128], ident)
                return r
            t = pe(step, *after, was)
            t = act(lambda e: e.activation(dst, bank, ACT.Copy), t)
            banks.give(bank, t)
            return t

        def gated_add(layer, bank, *after):
            t = dve(lambda e: e.scalar_tensor_tensor(x[:, :], bank, tg[:, layer:layer + 1], x[:, :],
                                                     ALU.mult, ALU.add), *after)
            banks.give(bank, t)
            return t

        def project(weight, src, *after):
            bank, was = banks.take()
            return bank, pe(lambda e: e.matmul(bank, weight, src, start=True, stop=True), *after, was)

        def attend(n, scores, scale, clamp, values, between=None):
            live = {}

            def start(u):
                bank, was = banks.take()
                live[u] = dict(S=bank, t=scores(u, bank, was))
                m = live[u]
                m["sh"], was = shifts.take()
                nm, nh, nl = (a[:, 0:HQ] for a in m["sh"])
                t = dve(lambda e: e.tensor_reduce(nm, b3(bank), AX.X, ALU.max, negate=True), m["t"], was)
                if clamp:
                    t = dve(lambda e: e.tensor_scalar(nm, nm, -NEG / 10, None, ALU.min), t)
                t = dve(lambda e: e.tensor_copy(nh, nm), t)
                m["t"] = dve(lambda e: e.tensor_tensor(nl, nm, nh, ALU.subtract), t)

            def shift_exp(u):
                m = live[u]
                bank, (nm, nh, nl) = m["S"], m["sh"]

                def step(e):
                    for part in (nh, nl):
                        r = e.matmul(bank, identb[:, :], bc(part[:, 0:HQ], 2, 128), start=False, stop=True,
                                     skip_group_check=True)
                    return r
                t = pe(step, m["t"])
                shifts.give(m["sh"], t)
                m["P"], was = Ps.take()
                P = m["P"]
                m["t"] = act(lambda e: e.activation(P, bank, ACT.Exp, scale=scale), t, was)
                banks.give(bank, m["t"])

            def turn_map(u):
                m = live[u]
                P = m["P"]
                bank, was = banks.take()

                def step(e):
                    for j in range(HQ):
                        r = e.transpose(bank[:, j * 128:(j + 1) * 128], P[:, j * 128:(j + 1) * 128], ident)
                    return r
                t = pe(step, m["t"], was)
                Ps.give(P, t)
                m["PT"], was = PTs.take()
                PT = m["PT"]
                m["t"] = act(lambda e: e.activation(PT, bank, ACT.Copy), t, was)
                banks.give(bank, m["t"])

            def finish(u):
                m = live.pop(u)
                PTs.give(m["PT"], values(u, m["PT"], m["t"]))

            for s in range(n + 3):
                if s < n:
                    start(s)
                if 0 <= s - 1 < n:
                    shift_exp(s - 1)
                if 0 <= s - 2 < n:
                    turn_map(s - 2)
                if 0 <= s - 3 < n:
                    finish(s - 3)
                if between and s < n:
                    between(s)

        def small_head_attention(layer, wq, bq, wk, bk, wv, bv, wo, bo, mask, clamp, t_mask, t_x):
            t_n = layernorm(x[:, :], xn[:, :], t_x)
            t_nT = turn(xn, xnT[:, :], t_n)
            kb, t_k = project(w(wk), ctxT[:, :], t_cT, t_x)
            km = kA[:, 0:HQ * T].rearrange("p (b j t) -> p b j t", b=G, j=HQ)
            for j in range(HQ):
                t_km = act(lambda e, j=j: e.activation(km[:, :, j, :], b3(kb), ACT.Identity,
                                                       scale=w("head4", j, j + 1),
                                                       bias=0.0 if bk is None else bk[:, j:j + 1]), t_k)
            banks.give(kb, t_km)
            vb, was = banks.take()

            def v_step(e):
                for b in range(G):
                    o = vb[:, b * 128:(b + 1) * 128]
                    r = e.matmul(o, ctxT[:, b * 128:(b + 1) * 128], w(wv), start=True, stop=bv is None)
                    if bv is not None:
                        r = e.matmul(o, ones[0:1, :], w(bv)[0:1, :], start=False, stop=True)
                return r
            t_v = pe(v_step, was)
            v4 = va[:, 0:G * H * (DH + 1)].rearrange("p (b h d) -> p b h d", b=G, h=H)
            t_va = [pool(lambda e: e.memset(v4[:, :, :, DH], 1.0), t_x),
                    dve(lambda e: e.tensor_copy(v4[:, :, :, 0:DH].rearrange("p b h d -> p (b h) d"),
                                                vb.rearrange("p (n d) -> p n d", d=DH)), t_v)]
            banks.give(vb, t_va)
            qb, t_q = project(w(wq), xnT[:, :], t_nT)
            t_qT = act(lambda e: e.activation(qA[:, 0:T], qb, ACT.Identity, bias=0.0 if bq is None else w(bq)), t_q)
            banks.give(qb, t_qT)

            def scores(u, bank, was):
                b, r = divmod(u, 4)
                rows = slice(32 * r, 32 * r + 32)

                def step(e):
                    e.matmul(bank, qA[rows, b * 128:(b + 1) * 128], km[rows, b, :, :], start=True, stop=False,
                             skip_group_check=True)
                    return e.matmul(bank, identb[:, :], bc(mask(b), 1, HQ), start=False, stop=True,
                                    skip_group_check=True)
                return pe(step, t_qT, t_km, t_mask, was)

            per = {}
            y_bank = {}

            def values(u, PT, t):
                b, r = divmod(u, 4)
                if r == 0:
                    per["O"], per["was"] = banks.take()
                O = per["O"]

                def step(e):
                    for j in range(HQ):
                        h = HQ * r + j
                        m = e.matmul(O[:, h * 9:h * 9 + 9], PT[:, j * 128:(j + 1) * 128], v4[:, b, h, :],
                                     start=True, stop=True)
                    return m
                t_pv = pe(step, t, t_va, per["was"])
                if r == 3:
                    o3 = O[:, 0:H * 9].rearrange("p (h d) -> p h d", h=H)
                    rec, was = smalls.take()
                    t1 = dve(lambda e: e.reciprocal(rec[:, 0:H], o3[:, :, DH]), t_pv, was)
                    on = oa[:, b * 128:(b + 1) * 128].rearrange("p (h d) -> p h d", h=H)
                    t2 = dve(lambda e: e.tensor_tensor(on, o3[:, :, 0:DH], bc(rec[:, 0:H], 2, DH), ALU.mult), t1)
                    smalls.give(rec, t2)
                    banks.give(O, t2)
                    y_bank["t"] = t2
                return t_pv

            attend(G * H // HQ, scores, DH ** -0.5, clamp, values)
            t_oT = turn(oa, oT[:, :], y_bank["t"])
            yb, was = banks.take()

            def y_step(e):
                for b in range(G):
                    o = yb[:, b * 128:(b + 1) * 128]
                    e.matmul(o, oT[:, b * 128:(b + 1) * 128], w(wo), start=True, stop=False)
                    r = e.matmul(o, ones[0:1, :], w(bo)[0:1, :], start=False, stop=True)
                return r
            return gated_add(layer, yb, pe(y_step, t_oT, was))

        def top(src, work1, work2, mask, n, width, k, rev, *after):
            s3 = src.rearrange("p (n e) -> p n e", e=width)
            a3 = work1.rearrange("p (n e) -> p n e", e=width)
            r_, wr = tops.take()
            r = r_[:, 0:n]
            cur, t = s3, list(after) + [wr]
            cur_flat = src
            for i in range(k):
                t1 = dve(lambda e, c=cur: e.tensor_reduce(r, c, AX.X, ALU.max), t)
                t2 = dve(lambda e, c=cur: e.tensor_tensor(a3, c, bc(r, 2, width), ALU.is_equal), t1)
                t3 = dve(lambda e: e.tensor_tensor(a3, a3, bc(rev, 1, n), ALU.mult), t2)
                t4 = dve(lambda e: e.tensor_reduce(r, a3, AX.X, ALU.max), t3)
                t5 = dve(lambda e: e.tensor_tensor(a3, a3, bc(r, 2, width), ALU.is_equal), t4)
                if i < k - 1:
                    t = dve(lambda e, c=cur_flat: e.scalar_tensor_tensor(work2, work1, -3.0e38, c, ALU.mult, ALU.add), t5)
                if i == 0:
                    t_m = dve(lambda e: e.tensor_copy(mask, work1), t5)
                else:
                    t_m = dve(lambda e: e.tensor_tensor(mask, mask, work1, ALU.add), t5)
                t = [t, t_m]
                cur, cur_flat = work2.rearrange("p (n e) -> p n e", e=width), work2
            tops.give(r_, t_m)
            return t_m

        tops = Slots([sb(f"top{i}", 128)[:, :] for i in range(2)])

        t_x = small_head_attention(0, "wq0", None, "wk0", None, "wv0", None, "wo0", "bo0",
                                   lambda b: mb0[:, b * 128:(b + 1) * 128], True, t_m, t_x)

        def widen(sel, gT, *after):
            bank, was = banks.take()
            return bank, pe(lambda e: e.matmul(bank, sel, gT, start=True, stop=True), *after, was)

        def turn_gates(src, width, dst, *after):
            bank, was = banks.take()

            def step(e):
                for b in range(G):
                    r = e.transpose(bank[0:width, b * 128:(b + 1) * 128], src[:, b * width:(b + 1) * width], ident)
                return r
            t = pe(step, *after, was)
            t = act(lambda e: e.activation(dst[0:width, 0:T], bank[0:width, :], ACT.Copy), t)
            banks.give(bank, t)
            return t

        def sum_tiles(layer, tiles, hT, weight, *after):
            yb, was = banks.take()

            def step(e):
                for b in range(G):
                    for n in range(tiles):
                        r = e.matmul(yb[:, b * 128:(b + 1) * 128], hT[:, n * T + b * 128:n * T + (b + 1) * 128],
                                     w(weight, n * 128, (n + 1) * 128), start=(n == 0), stop=(n == tiles - 1))
                return r
            return gated_add(layer, yb, pe(step, *after, was))

        def mixture0(t_x):
            t_n = layernorm(x[:, :], xn[:, :], t_x)
            t_nT = turn(xn, xnT[:, :], t_n)
            lb, was = banks.take()

            def l_step(e):
                for b in range(G):
                    r = e.matmul(lb[:, b * E0:(b + 1) * E0], xnT[:, b * 128:(b + 1) * 128], w("gw0"),
                                 start=True, stop=True)
                return r
            t_l = pe(l_step, t_nT, was)
            ne = G * E0
            l3 = lb[:, 0:ne].rearrange("p (b e) -> p b e", b=G)
            sc, sb_ = gs[:, 0:ne], gs[:, ne:2 * ne]
            sc3, sb3 = (a.rearrange("p (b e) -> p b e", b=G) for a in (sc, sb_))
            mx, was = smalls.take()
            t = dve(lambda e: e.tensor_reduce(mx[:, 0:G], l3, AX.X, ALU.max), t_l, was)
            t = dve(lambda e: e.tensor_tensor(sc3, l3, bc(mx[:, 0:G], 2, E0), ALU.subtract), t)
            banks.give(lb, t)
            t = act(lambda e: e.activation(sc, sc, ACT.Exp), t)
            t = dve(lambda e: e.tensor_reduce(mx[:, 0:G], sc3, AX.X, ALU.add), t)
            t = dve(lambda e: e.reciprocal(mx[:, 0:G], mx[:, 0:G]), t)
            t = dve(lambda e: e.tensor_tensor(sc3, sc3, bc(mx[:, 0:G], 2, E0), ALU.mult), t)
            smalls.give(mx, t)
            t = dve(lambda e: e.tensor_tensor(sb3, sc3, bc(w("gb0"), 1, G), ALU.add), t)
            t = top(sb_, gw1_[:, 0:ne], gw2_[:, 0:ne], gm[:, 0:ne], G, E0, 2, w("rev8"), t)
            t = dve(lambda e: e.scalar_tensor_tensor(sc, sc, 0.5, gm[:, 0:ne], ALU.mult, ALU.mult), t)
            t_g = turn_gates(sc, E0, gt, t)
            t_h = []
            order = list(range(E0, E0 + F0)) + list(range(E0))
            for n in order:
                a, t_a = project(w("w1_0", n * 128, (n + 1) * 128), xnT[:, :], t_nT)
                c, t_c3 = project(w("w3_0", n * 128, (n + 1) * 128), xnT[:, :], t_nT)
                th, was = tmps.take()
                t = act(lambda e, th=th, a=a: e.activation(th, a, ACT.Tanh, scale=0.5), t_a, was)
                t = dve(lambda e, th=th, a=a: e.scalar_tensor_tensor(th, th, 1.0, a, ALU.add, ALU.mult), t)
                banks.give(a, t)
                h = qk[:, n * T:(n + 1) * T]
                if n >= E0:
                    t = dve(lambda e, th=th, c=c, h=h: e.scalar_tensor_tensor(h, th, 0.5, c, ALU.mult, ALU.mult), t, t_c3)
                    banks.give(c, t)
                else:
                    t = dve(lambda e, th=th, c=c: e.tensor_tensor(th, th, c, ALU.mult), t, t_c3)
                    banks.give(c, t)
                    g, t_w = widen(ident[0:E0, n:n + 1].broadcast_to((E0, 128)), gt[0:E0, 0:T], t_g)
                    t = dve(lambda e, th=th, g=g, h=h: e.tensor_tensor(h, th, g, ALU.mult), t, t_w)
                    banks.give(g, t)
                tmps.give(th, t)
                t_h.append(t)
            return sum_tiles(4, E0 + F0, qk, "w2_0", t_h)

        t_x = mixture0(t_x)

        t_x = small_head_attention(1, "wq1", "bq1", "wk1", bk1m, "wv1", "bv1", "wo1", "bo1",
                                   lambda b: mb1[:, :], False, None, t_x)

        def switched_attention(t_x):
            t_n = layernorm(x[:, :], xn[:, :], t_x)
            t_nT = turn(xn, xnT[:, :], t_n)
            NGATE = 2 * H * E1
            for half in range(G // 2):
                gb, was = banks.take()

                def g_step(e, gb=gb, half=half):
                    for i in range(2):
                        b = 2 * half + i
                        r = e.matmul(gb[:, i * NGATE:(i + 1) * NGATE], xnT[:, b * 128:(b + 1) * 128], w("sg1"),
                                     start=True, stop=True)
                    return r
                t = pe(g_step, t_nT, was)
                t_g = act(lambda e, gb=gb, half=half: e.activation(gs[:, half * 512:half * 512 + 512], gb, ACT.Copy), t)
                banks.give(gb, t_g)
            for b in range(G):
                pb_, was = banks.take()
                t = pe(lambda e, b=b, o=pb_: e.matmul(o, xnT[:, b * 128:(b + 1) * 128], w("sv1"), start=True, stop=True),
                       t_nT, was)
                t_pv = act(lambda e, b=b, o=pb_: e.activation(pv1[:, b * 512:(b + 1) * 512], o, ACT.Copy, scale=0.5), t)
                banks.give(pb_, t_pv)
            t_top = top(gs[:, :], gw1_[:, :], gw2_[:, :], gm[:, :], 2 * G * H, E1, 2, w("rev8"), t_g)
            t = act(lambda e: e.activation(gt[:, :], gs[:, :], ACT.Tanh, scale=0.5), t_g)
            t_mix = dve(lambda e: e.scalar_tensor_tensor(gt[:, :], gt[:, :], 1.0, gm[:, :], ALU.add, ALU.mult), t, t_top)
            mix = gt[:, :].rearrange("p (b s h e) -> p b s h e", b=G, s=2, h=H)
            sel = gm[:, :].rearrange("p (b s h e) -> p b s h e", b=G, s=2, h=H)
            t_qk = []
            for n in range(8):
                for wn, dst in (("sq1", qA), ("sk1", kA)):
                    bank, t = project(w(wn, n * 128, (n + 1) * 128), xnT[:, :], t_nT)
                    t = act(lambda e, n=n, dst=dst, bank=bank: e.activation(dst[:, n * T:(n + 1) * T], bank, ACT.Copy), t)
                    banks.give(bank, t)
                    t_qk.append(t)
            v4 = va[:, :].rearrange("p (b h d) -> p b h d", b=3, h=H)
            t_one = pool(lambda e: e.memset(v4[:, :, :, D1], 1.0), t_x)
            t_v = {b: [t_one] for b in range(G)}
            turn_of = [0]

            def mixed(out_, in0, in1, shape, *after):
                pr, was = prods.take()
                p4 = pr.rearrange(*shape[0], **shape[1])
                eng = pool if turn_of[0] % 5 in (1, 3) else dve
                turn_of[0] += 1
                t = eng(lambda e: e.tensor_tensor(p4, in0, in1, ALU.mult), *after, was)
                t = dve(lambda e: e.tensor_reduce(out_, p4, AX.X, ALU.add), t)
                prods.give(pr, t)
                return t

            pv4 = pv1[:, :].rearrange("p (b e d) -> p b d e", b=G, e=E1)

            def mix_values(b, h):
                t_v[b].append(mixed(v4[:, b % 3, h:h + 2, 0:D1], bc(mix[:, b, 0, h:h + 2, :], 2, D1),
                                    bc(pv4[:, b, :, :], 1, 2), (("p (h d e) -> p h d e",), dict(h=2, e=E1)),
                                    t_mix, t_pv, t_pvs.get(b - 3)))

            t_pvs = {}
            o4 = oa[:, :].rearrange("p (b h d) -> p b d h", b=2, h=H)
            t_o = {b: [] for b in range(G)}
            U = qk_u[:, :]
            u4 = U.rearrange("p (b e d) -> p b e d", b=G, e=E1)
            t_u = {b: [] for b in range(G)}

            def mix_outputs(b, ex):
                t_u[b].append(mixed(u4[:, b, ex, :], o4[:, b % 2, :, :], bc(sel[:, b, 1, :, ex], 1, D1),
                                    (("p (d h) -> p d h",), dict(h=H)), t_o[b]))

            def scores(u, bank, was):
                b, g = divmod(u, 4)
                rows = slice(64 * (g % 2), 64 * (g % 2) + 64)

                def step(e):
                    for j in range(HQ):
                        c = (HQ * (g // 2) + j) * T + b * 128
                        r = e.matmul(bank[:, j * 128:(j + 1) * 128], qA[rows, c:c + 128], kA[rows, c:c + 128],
                                     start=(j == 0), stop=True, skip_group_check=True)
                    return r
                return pe(step, t_qk, was)

            def values(u, PT, t):
                b, g = divmod(u, 4)
                O, was = banks.take()

                def step(e):
                    for j in range(HQ):
                        r = e.matmul(O[:, j * 65:j * 65 + 65], PT[:, j * 128:(j + 1) * 128], v4[:, b % 3, 8 * (g // 2) + 2 * j + g % 2, :],
                                     start=True, stop=True)
                    return r
                t_p = t_pvs[b] = pe(step, t, t_v[b], was)
                o3 = O[:, 0:HQ * 65].rearrange("p (h d) -> p h d", h=HQ)
                rec, was = smalls.take()
                t1 = dve(lambda e: e.reciprocal(rec[:, 0:HQ], o3[:, :, D1]), t_p, was)
                dst = oa[:, :].rearrange("p (b g j r d) -> p b g j r d", b=2, g=2, j=HQ, r=2)[:, b % 2, g // 2, :, g % 2, :]
                t2 = dve(lambda e: e.tensor_tensor(dst, o3[:, :, 0:D1], bc(rec[:, 0:HQ], 2, D1), ALU.mult), t1, t_u.get(b - 2))
                smalls.give(rec, t2)
                banks.give(O, t2)
                t_o[b].append(t2)
                return t_p

            for h in range(0, H, 2):
                mix_values(0, h)

            def between(s):
                b, g = divmod(s, 4)
                if b + 1 < G:
                    mix_values(b + 1, 4 * g)
                    mix_values(b + 1, 4 * g + 2)
                if s >= 7:
                    bo, k = divmod(s - 7, 4)
                    mix_outputs(bo, 2 * k)
                    mix_outputs(bo, 2 * k + 1)

            attend(G * 4, scores, D1 ** -0.5, False, values, between)
            for k in range(9 * 2, G * E1):
                mix_outputs(*divmod(k, E1))
            uT = U2[:, :]
            t_uT = []
            for b in range(G):
                bank, was = banks.take()

                def step(e, b=b, bank=bank):
                    for n in range(4):
                        c = b * 512 + n * 128
                        r = e.transpose(bank[:, n * 128:(n + 1) * 128], U[:, c:c + 128], ident)
                    return r
                t = pe(step, t_u[b], was)
                t_uT.append(act(lambda e, b=b, bank=bank: e.activation(uT[:, b * 512:(b + 1) * 512], bank, ACT.Copy), t,
                                t_qk))
                banks.give(bank, t_uT[-1])
            yb, was = banks.take()

            def y_step(e):
                for b in range(G):
                    for n in range(4):
                        r = e.matmul(yb[:, b * 128:(b + 1) * 128], uT[:, b * 512 + n * 128:b * 512 + (n + 1) * 128],
                                     w("so1", n * 128, (n + 1) * 128), start=(n == 0), stop=(n == 3))
                return r
            return gated_add(5, yb, pe(y_step, t_uT, was))

        qk_u = sb("qk_u", G * E1 * D1)
        U2 = pv1
        t_x = switched_attention(t_x)

        def mlstm(t_x):
            t_n = layernorm(x[:, :], xn[:, :], t_x)
            t_nT = turn(xn, xnT[:, :], t_n)
            gb, was = banks.take()
            NGK = 2 * NH2

            def g_step(e):
                for b in range(G):
                    o = gb[:, b * NGK:(b + 1) * NGK]
                    e.matmul(o, xnT[:, b * 128:(b + 1) * 128], w("gk2", 0, NGK), start=True, stop=False)
                    for part in (1, 2):
                        e.matmul(o, ctxT[:, b * 128:(b + 1) * 128], w("gk2", part * NGK, (part + 1) * NGK),
                                 start=False, stop=False)
                    r = e.matmul(o, ones[0:1, :], w("gb2")[0:1, :], start=False, stop=True)
                return r
            t_g = pe(g_step, t_nT, was)
            n = G * NH2
            g4 = gb[:, 0:G * NGK].rearrange("p (b k h) -> p b k h", b=G, k=2)
            ab, lf, ig, cum, av, mneg = (gs[:, i * n:(i + 1) * n] for i in range(6))
            v3 = {k: a.rearrange("p (b h) -> p b h", b=G) for k, a in
                  dict(ab=ab, lf=lf, ig=ig, cum=cum, av=av).items()}
            t = act(lambda e: e.activation(v3["ab"], g4[:, :, 1, :], ACT.Abs), t_g)
            t = act(lambda e: e.activation(ab, ab, ACT.Exp, scale=-1.0), t)
            t_s = act(lambda e: e.activation(ab, ab, ACT.Ln, bias=1.0), t)
            t = dve(lambda e: e.tensor_copy(v3["ig"], g4[:, :, 0, :]), t_g, t_s)
            t = dve(lambda e: e.tensor_scalar(v3["lf"], g4[:, :, 1, :], 0.0, None, ALU.min), t)
            banks.give(gb, t)
            t = dve(lambda e: e.tensor_tensor(lf, lf, ab, ALU.subtract), t, t_s)
            cb, was = banks.take()
            t = pe(lambda e: e.matmul(cb[:, 0:n], w("triu"), lf, start=True, stop=True), t, was)
            t = dve(lambda e: e.tensor_copy(cum, cb[:, 0:n]), t)
            banks.give(cb, t)
            t_a = dve(lambda e: e.tensor_tensor(av, ig, cum, ALU.subtract), t)
            v4 = va[:, 0:G * NH2 * (DH2 + 1)].rearrange("p (b h d) -> p b h d", b=G, h=NH2)
            t_va = [pool(lambda e: e.memset(v4[:, :, :, DH2], 1.0), t_x),
                    act(lambda e: e.activation(v4[:, :, :, 0:DH2].rearrange("p b h d -> p (b h) d"),
                                               ctxN[:, :].rearrange("p (n d) -> p n d", d=DH2), ACT.Copy), t_x)]
            hn = oa[:, 0:T]
            t_h = []
            live = {}

            def decay(h):
                m = live[h] = {}
                dg, was = tmps.take()
                for b in range(G):
                    t = dve(lambda e, b=b: e.tensor_scalar(dg[:, b * 128:(b + 1) * 128], ident,
                                                           av[:, b * NH2 + h:b * NH2 + h + 1], None, ALU.mult), t_a, was)
                A, was = banks.take()

                def a_step(e):
                    e.matmul(A, ones[:, :], dg[:, 0:512], start=True, stop=False, skip_group_check=True)
                    return e.matmul(A, identb[:, :], bc(causb[:, :], 1, G), start=False, stop=True,
                                    skip_group_check=True)
                t = pe(a_step, t, was)
                tmps.give(dg, t)
                nm = mneg[:, h * G:(h + 1) * G]
                t = dve(lambda e: e.tensor_reduce(nm, b3(A), AX.X, ALU.max, negate=True), t)
                m.update(A=A, t=t, nm=nm)

            def decay2(h):
                m = live[h]
                A, nm = m["A"], m["nm"]
                t = pe(lambda e: e.matmul(A, ident, bc(nm, 2, 128), start=False, stop=True,
                                          skip_group_check=True), m["t"])
                Pd, was = Ps.take()
                t_D = act(lambda e: e.activation(Pd, A, ACT.Exp), t, was)
                banks.give(A, t_D)
                Q, was = banks.take()

                def q_step(e):
                    rows = slice(32 * h, 32 * h + 32)
                    for b in range(G):
                        r = e.matmul(Q[:, b * 128:(b + 1) * 128], xnT[rows, b * 128:(b + 1) * 128],
                                     ctxT[rows, b * 128:(b + 1) * 128], start=True, stop=True)
                    return r
                t = pe(q_step, t_nT, was)
                t = dve(lambda e: e.scalar_tensor_tensor(Pd, Q, DH2 ** -0.5, Pd, ALU.mult, ALU.mult), t, t_D)
                banks.give(Q, t)
                m.update(P=Pd, t=t)

            def weigh(h):
                m = live.pop(h)
                Pd = m["P"]
                bank, was = banks.take()

                def t_step(e):
                    for b in range(G):
                        r = e.transpose(bank[:, b * 128:(b + 1) * 128], Pd[:, b * 128:(b + 1) * 128], ident)
                    return r
                t = pe(t_step, m["t"], was)
                Ps.give(Pd, t)
                PT, was = PTs.take()
                t = act(lambda e: e.activation(PT, bank, ACT.Copy), t, was)
                banks.give(bank, t)
                O, was = banks.take()

                def o_step(e):
                    for b in range(G):
                        r = e.matmul(O[:, b * 33:b * 33 + 33], PT[:, b * 128:(b + 1) * 128], v4[:, b, h, :],
                                     start=True, stop=True)
                    return r
                t = pe(o_step, t, t_va, was)
                PTs.give(PT, t)
                o3 = O[:, 0:G * 33].rearrange("p (b d) -> p b d", b=G)
                nr, was = smalls.take()
                e4, s4 = nr[:, 0:G], nr[:, G:2 * G]
                cu = v3["cum"][:, :, h]
                t1 = dve(lambda e: e.tensor_tensor(e4, m["nm"], cu, ALU.subtract), was)
                t1 = act(lambda e: e.activation(e4, e4, ACT.Exp), t1)
                t2 = dve(lambda e: e.tensor_scalar(s4, o3[:, :, DH2], -1.0, None, ALU.mult), t)
                t2 = dve(lambda e: e.tensor_tensor(s4, s4, o3[:, :, DH2], ALU.max), t2)
                t2 = dve(lambda e: e.tensor_tensor(s4, s4, e4, ALU.max), t2, t1)
                t2 = dve(lambda e: e.tensor_scalar(s4, s4, 1e-6, None, ALU.add), t2)
                t2 = dve(lambda e: e.reciprocal(s4, s4), t2)
                t2 = dve(lambda e: e.tensor_tensor(hn.rearrange("p (b h d) -> p b h d", b=G, h=NH2)[:, :, h, :],
                                                   o3[:, :, 0:DH2], bc(s4, 2, DH2), ALU.mult), t2)
                smalls.give(nr, t2)
                banks.give(O, t2)
                t_h.append(t2)

            for s in range(NH2 + 2):
                if s < NH2:
                    decay(s)
                if 0 <= s - 1 < NH2:
                    decay2(s - 1)
                if 0 <= s - 2 < NH2:
                    weigh(s - 2)
            h3 = hn.rearrange("p (n d) -> p n d", d=DH2)
            mn, was = smalls.take()
            vr, was2 = smalls.take()
            sq, was3 = tmps.take()
            t = dve(lambda e: e.tensor_reduce(mn[:, 0:n], h3, AX.X, ALU.add), t_h, was, was2, was3)
            t = dve(lambda e: e.tensor_scalar(mn[:, 0:n], mn[:, 0:n], 1.0 / DH2, None, ALU.mult), t)
            t = dve(lambda e: e.tensor_tensor(h3, h3, bc(mn[:, 0:n], 2, DH2), ALU.subtract), t)
            t = dve(lambda e: e.tensor_tensor(sq, hn, hn, ALU.mult), t)
            t = dve(lambda e: e.tensor_reduce(vr[:, 0:n], sq.rearrange("p (n d) -> p n d", d=DH2), AX.X, ALU.add), t)
            tmps.give(sq, t)
            t = rstd(vr[:, 0:n], (1.0 / DH2, 1e-6), n, t)
            t = dve(lambda e: e.tensor_tensor(h3, h3, bc(vr[:, 0:n], 2, DH2), ALU.mult), t)
            smalls.give(mn, t)
            smalls.give(vr, t)
            t = dve(lambda e: e.tensor_tensor(b3(hn), b3(hn), bc(w("nw2"), 1, G), ALU.mult), t)
            return dve(lambda e: e.scalar_tensor_tensor(x[:, :], hn, tg[:, 2:3], x[:, :], ALU.mult, ALU.add), t)

        t_x = mlstm(t_x)

        def conv_ffn(t_x):
            t_n = layernorm(x[:, :], xn[:, :], t_x)
            am_, was = smalls.take()
            am, sc = am_[:, 0:G], am_[:, G:2 * G]
            t = dve(lambda e: e.tensor_reduce(am, b3(xn[:, :]), AX.X, ALU.max, apply_absolute_value=True), t_n, was)
            t = dve(lambda e: e.tensor_scalar(am, am, 1e-5, None, ALU.max), t)
            t = dve(lambda e: e.reciprocal(sc, am), t)
            t = dve(lambda e: e.tensor_scalar(sc, sc, 127.0, None, ALU.mult), t)
            t = dve(lambda e: e.tensor_scalar(am, am, 1.0 / 127.0, None, ALU.mult), t)
            x3 = b3(xn[:, :])
            for b in range(G):
                t1 = dve(lambda e, b=b: e.tensor_scalar(x3[:, b, :], x3[:, b, :], sc[:, b:b + 1], ROUND,
                                                        ALU.mult, ALU.add), t)
            t1 = dve(lambda e: e.tensor_scalar(xn[:, :], xn[:, :], ROUND, 127.0, ALU.subtract, ALU.min), t1)
            for b in range(G):
                t2 = dve(lambda e, b=b: e.tensor_scalar(x3[:, b, :], x3[:, b, :], -128.0, am[:, b:b + 1],
                                                        ALU.max, ALU.mult), t1)
            smalls.give(am_, t2)
            bank, was = banks.take()

            def t_step(e):
                for b in range(G):
                    r = e.transpose(bank[:, b * 128:(b + 1) * 128], xn[:, b * 128:(b + 1) * 128], ident)
                return r
            t = pe(t_step, t2, was)
            q3 = xqT[:, :].rearrange("p (b t) -> p b t", t=130)
            t_q = act(lambda e: e.activation(q3[:, :, 1:129], b3(bank), ACT.Copy), t)
            banks.give(bank, t_q)
            yb, yw = banks.take()
            live = {}
            h2 = oa[:, 0:G * F2]
            sc2_, was_s = smalls.take()
            t_y = []

            def hidden(b):
                hb, was = banks.take()

                def step(e):
                    for k in range(3):
                        e.matmul(hb, q3[:, b, k:k + 128], wconv[:, k * F2:(k + 1) * F2], start=(k == 0), stop=False)
                    return e.matmul(hb, ones[0:1, :], w("convb")[0:1, :], start=False, stop=True)
                t = pe(step, t_q, was)
                h = h2[:, b * F2:(b + 1) * F2]
                th, was = tmps.take()
                t = act(lambda e: e.activation(th, hb, ACT.Tanh, scale=0.5), t, was)
                t = dve(lambda e: e.scalar_tensor_tensor(h, th, 1.0, hb, ALU.add, ALU.mult), t)
                banks.give(hb, t)
                tmps.give(th, t)
                a, s, o = (sc2_[:, k * G + b:k * G + b + 1] for k in range(3))
                t = dve(lambda e: e.tensor_reduce(a, h, AX.X, ALU.max, apply_absolute_value=True), t, was_s)
                t = dve(lambda e: e.tensor_scalar(a, a, 2e-5, None, ALU.max), t)
                t = dve(lambda e: e.reciprocal(s, a), t)
                t = dve(lambda e: e.tensor_scalar(s, s, 127.0, None, ALU.mult), t)
                t1 = dve(lambda e: e.tensor_scalar(a, a, 0.5 / 127.0, wstat[:, 4:5], ALU.mult, ALU.mult), t)
                live[b, "o"] = dve(lambda e: e.tensor_scalar(o, a, tg[:, 6:7], None, ALU.mult), t1)
                t = dve(lambda e: e.tensor_scalar(h, h, s, ROUND, ALU.mult, ALU.add), t)
                t = dve(lambda e: e.tensor_scalar(h, h, ROUND, 127.0, ALU.subtract, ALU.min), t)
                live[b] = dve(lambda e: e.tensor_scalar(r2[:, b * F2:(b + 1) * F2], h, -128.0, None, ALU.max), t)

            def second(b):
                bank, was = banks.take()
                bb = bank[:, 0:256].bitcast(BF16)

                def step(e):
                    for n in range(4):
                        r = e.transpose(bb[:, n * 128:(n + 1) * 128], r2[:, b * F2 + n * 128:b * F2 + (n + 1) * 128],
                                        identb[:, :])
                    return r
                t = pe(step, live[b], was)
                t = act(lambda e: e.activation(r2T[:, b * F2:(b + 1) * F2], bb, ACT.Copy), t)
                banks.give(bank, t)

                def y_step(e):
                    for n in range(4):
                        r = e.matmul(yb[:, b * 128:(b + 1) * 128], r2T[:, b * F2 + n * 128:b * F2 + (n + 1) * 128],
                                     w2b[:, n * 128:(n + 1) * 128], start=(n == 0), stop=(n == 3))
                    return r
                t_y.append(pe(y_step, t, yw))

            for s in range(G + 1):
                if s < G:
                    hidden(s)
                if s >= 1:
                    second(s - 1)
            xx = b3(x[:, :])
            for b in range(G):
                t = dve(lambda e, b=b: e.scalar_tensor_tensor(xx[:, b, :], yb[:, b * 128:(b + 1) * 128],
                                                              sc2_[:, 2 * G + b:2 * G + b + 1], xx[:, b, :],
                                                              ALU.mult, ALU.add), t_y, live[b, "o"])
            banks.give(yb, t)
            smalls.give(sc2_, t)
            return t

        t_x = conv_ffn(t_x)

        def wide_attention(t_x):
            t_n = layernorm(x[:, :], xn[:, :], t_x)
            t_nT = turn(xn, xnT[:, :], t_n)
            kb, t = project(w("wk3"), ctxT[:, :], t_x)
            t_k = act(lambda e: e.activation(kA[:, 0:T], kb, ACT.Identity, bias=w("bk3")), t)
            banks.give(kb, t_k)
            qb, t = project(w("wq3"), xnT[:, :], t_nT)
            t_q = act(lambda e: e.activation(qA[:, 0:T], qb, ACT.Identity, bias=w("bq3")), t)
            banks.give(qb, t_q)
            vb, was = banks.take()

            def v_step(e):
                for b in range(G):
                    o = vb[:, b * 128:(b + 1) * 128]
                    e.matmul(o, ctxT[:, b * 128:(b + 1) * 128], w("wv3"), start=True, stop=False)
                    r = e.matmul(o, ones[0:1, :], w("bv3")[0:1, :], start=False, stop=True)
                return r
            t = pe(v_step, was)
            v3 = va[:, 0:G * (D + 1)].rearrange("p (b d) -> p b d", b=G)
            t_va = [pool(lambda e: e.memset(v3[:, :, D], 1.0), t_x),
                    dve(lambda e: e.tensor_copy(v3[:, :, 0:D], b3(vb)), t)]
            banks.give(vb, t_va)

            def scores(u, bank, was):
                def step(e):
                    for b in range(G):
                        c = slice(b * 128, (b + 1) * 128)
                        r = e.matmul(bank[:, c], qA[:, c], kA[:, c], start=(b == 0), stop=True, skip_group_check=True)
                    return r
                return pe(step, t_q, t_k, was)

            res = {}

            def values(u, PT, t):
                t_on = []
                for half in range(2):
                    O, was = banks.take()

                    def step(e, O=O, half=half):
                        for i in range(2):
                            b = 2 * half + i
                            r = e.matmul(O[:, i * 129:i * 129 + 129], PT[:, b * 128:(b + 1) * 128], v3[:, b, :],
                                         start=True, stop=True)
                        return r
                    t_p = pe(step, t, t_va, was)
                    o3 = O[:, 0:258].rearrange("p (b d) -> p b d", b=2)
                    rec, was = smalls.take()
                    t1 = dve(lambda e, o3=o3, rec=rec: e.reciprocal(rec[:, 0:2], o3[:, :, D]), t_p, was)
                    t2 = dve(lambda e, o3=o3, rec=rec, half=half: e.tensor_tensor(
                        oa[:, half * 256:half * 256 + 256].rearrange("p (b d) -> p b d", b=2), o3[:, :, 0:D],
                        bc(rec[:, 0:2], 2, D), ALU.mult), t1)
                    smalls.give(rec, t2)
                    banks.give(O, t2)
                    t_on.append(t2)
                res["t"] = t_on
                return t_p

            attend(1, scores, D ** -0.5, False, values)
            t_oT = turn(oa, oT[:, :], res["t"])
            yb, was = banks.take()

            def y_step(e):
                for b in range(G):
                    o = yb[:, b * 128:(b + 1) * 128]
                    e.matmul(o, oT[:, b * 128:(b + 1) * 128], w("wo3"), start=True, stop=False)
                    r = e.matmul(o, ones[0:1, :], w("bo3")[0:1, :], start=False, stop=True)
                return r
            t_y = pe(y_step, t_oT, was)
            t = dve(lambda e: e.scalar_tensor_tensor(xn[:, :], ctxN[:, :], 2.0, xn[:, :], ALU.mult, ALU.add), t_nT)
            t = dve(lambda e: e.tensor_tensor(xn[:, :], xn[:, :], yb, ALU.add), t, t_y)
            banks.give(yb, t)
            t = layernorm(xn[:, :], xn[:, :], t)
            t = dve(lambda e: e.tensor_tensor(b3(xn[:, :]), b3(xn[:, :]), bc(w("g1_3"), 1, G), ALU.mult), t)
            t = dve(lambda e: e.tensor_tensor(b3(xn[:, :]), b3(xn[:, :]), bc(w("b1_3"), 1, G), ALU.add), t)
            t_nT = turn(xn, xnT[:, :], t)
            t_h = []
            for n in range(F3 // 128):
                bank, t = project(w("f1_3", n * 128, (n + 1) * 128), xnT[:, :], t_nT)
                t = act(lambda e, n=n, bank=bank: e.activation(qk[:, (2 + n) * T:(3 + n) * T], bank, ACT.Relu,
                                                               bias=w("fb1_3", n, n + 1)), t)
                banks.give(bank, t)
                t_h.append(t)
            zb, was = banks.take()

            def f_step(e, zb=zb):
                for b in range(G):
                    o = zb[:, b * 128:(b + 1) * 128]
                    for n in range(F3 // 128):
                        e.matmul(o, qk[:, (2 + n) * T + b * 128:(2 + n) * T + (b + 1) * 128],
                                 w("f2_3", n * 128, (n + 1) * 128), start=(n == 0), stop=False)
                    r = e.matmul(o, ones[0:1, :], w("fb2_3")[0:1, :], start=False, stop=True)
                return r
            t_y = pe(f_step, t_h, was)
            t = dve(lambda e, zb=zb: e.tensor_tensor(xn[:, :], xn[:, :], zb, ALU.add), t_y)
            banks.give(zb, t)
            t = layernorm(xn[:, :], xn[:, :], t)
            t = dve(lambda e: e.tensor_tensor(b3(xn[:, :]), b3(xn[:, :]), bc(w("g2_3"), 1, G), ALU.mult), t)
            t = dve(lambda e: e.tensor_tensor(b3(xn[:, :]), b3(xn[:, :]), bc(w("b2_3"), 1, G), ALU.add), t)
            return dve(lambda e: e.scalar_tensor_tensor(x[:, :], xn[:, :], tg[:, 3:4], x[:, :], ALU.mult, ALU.add), t)

        t_x = wide_attention(t_x)

        def mixture3(t_x):
            t_n = layernorm(x[:, :], xn[:, :], t_x)
            t_nT = turn(xn, xnT[:, :], t_n)
            lb, was = banks.take()

            def l_step(e):
                for b in range(G):
                    r = e.matmul(lb[:, b * E3:(b + 1) * E3], xnT[:, b * 128:(b + 1) * 128], w("gw3"),
                                 start=True, stop=True)
                return r
            t_l = pe(l_step, t_nT, was)
            ne, ng = G * E3, G * 4
            sc, sb_, mk, pr, w1_, w2_, gmk, gw = (gs[:, i * ne:(i + 1) * ne] for i in range(8))
            t = act(lambda e: e.activation(sc, lb[:, 0:ne], ACT.Exp, scale=-1.0), t_l)
            banks.give(lb, t)
            t = dve(lambda e: e.tensor_scalar(sc, sc, 1.0, None, ALU.add), t)
            t = dve(lambda e: e.reciprocal(sc, sc), t)
            t = dve(lambda e: e.tensor_tensor(sb_.rearrange("p (b e) -> p b e", b=G),
                                              sc.rearrange("p (b e) -> p b e", b=G), bc(w("gb3"), 1, G), ALU.add), t)
            t = top(sb_, w1_, w2_, mk, ng, 4, 2, w("rev4"), t)
            t = dve(lambda e: e.tensor_tensor(pr, mk, sb_, ALU.mult), t)
            r1, was = smalls.take()
            t = dve(lambda e: e.tensor_reduce(r1[:, 0:ng], pr.rearrange("p (g e) -> p g e", e=4), AX.X, ALU.add), t, was)
            t = top(r1[:, 0:ng], w1_[:, 0:ng], w2_[:, 0:ng], gmk[:, 0:ng], G, 4, 2, w("rev4"), t)
            smalls.give(r1, t)
            t = dve(lambda e: e.tensor_tensor(sb_.rearrange("p (g e) -> p g e", e=4),
                                              sb_.rearrange("p (g e) -> p g e", e=4), bc(gmk[:, 0:ng], 2, 4), ALU.mult), t)
            t = top(sb_, w1_, w2_, mk, G, E3, 4, w("rev16"), t)
            t = dve(lambda e: e.tensor_tensor(sc, sc, mk, ALU.mult), t)
            r2_, was = smalls.take()
            sc3 = sc.rearrange("p (b e) -> p b e", b=G)
            t = dve(lambda e: e.tensor_reduce(r2_[:, 0:G], sc3, AX.X, ALU.add), t, was)
            t = dve(lambda e: e.tensor_scalar(r2_[:, 0:G], r2_[:, 0:G], 1e-20, None, ALU.add), t)
            t = dve(lambda e: e.reciprocal(r2_[:, 0:G], r2_[:, 0:G]), t)
            t = dve(lambda e: e.tensor_scalar(r2_[:, 0:G], r2_[:, 0:G], 2.5, None, ALU.mult), t)
            t = dve(lambda e: e.tensor_tensor(sc3, sc3, bc(r2_[:, 0:G], 2, E3), ALU.mult), t)
            smalls.give(r2_, t)
            t_g = turn_gates(sc, E3, gt, t)
            t_h = []
            for n in list(range(8, 10)) + list(range(8)):
                a, t_a = project(w("up3", n * 128, (n + 1) * 128), xnT[:, :], t_nT)
                th, was = tmps.take()
                h = qk[:, n * T:(n + 1) * T]
                t = act(lambda e, th=th, a=a: e.activation(th, a, ACT.Relu), t_a, was)
                dst = h if n >= 8 else th
                t = dve(lambda e, th=th, a=a, dst=dst: e.tensor_tensor(dst, th, a, ALU.mult), t)
                banks.give(a, t)
                if n < 8:
                    g, t_w = widen(w("sel3", n * 128, (n + 1) * 128)[0:E3, :], gt[0:E3, 0:T], t_g)
                    t = dve(lambda e, th=th, g=g, h=h: e.tensor_tensor(h, th, g, ALU.mult), t, t_w)
                    banks.give(g, t)
                tmps.give(th, t)
                t_h.append(t)
            yb, was = banks.take()

            def step(e):
                for b in range(G):
                    for n in range(10):
                        r = e.matmul(yb[:, b * 128:(b + 1) * 128], qk[:, n * T + b * 128:n * T + (b + 1) * 128],
                                     w("down3", n * 128, (n + 1) * 128), start=(n == 0), stop=(n == 9))
                return r
            t = pe(step, t_h, was)
            t_y = dve(lambda e: e.scalar_tensor_tensor(y_st[:, :], yb, tg[:, 7:8], x[:, :], ALU.mult, ALU.add),
                      t, stored)
            banks.give(yb, t_y)
            return t_y

        t_y = mixture3(t_x)

        base = {e: setup.count(e) for e in ENGINES}
        turn_count = {e: flow.count(e) for e in ENGINES}
        base.update({"in": 0, "out": 0})
        turn_count.update({"in": 64, "out": 16})

        def value(src, n, i):
            return i * turn_count[src] + (base[src] + n)

        def program(name):
            def run(eng):
                for need, step in setup.steps[name]:
                    for src, n in need.items():
                        eng.wait_ge(s_w if src == "w" else sems[src], n)
                    step(eng).then_inc(sems[name], 1)
                with eng.Fori(0, NG) as i:
                    for src in ENGINES:
                        eng.wait_ge(sems[src], value(src, 0, i))
                    for need, step in flow.steps[name]:
                        for src, n in need.items():
                            eng.wait_ge(sems[src], value(src, n, i))
                        step(eng).then_inc(sems[name], 1)
            return run

        block = ctx.enter_context(nc.Block())
        block.tensor(program("pe"))
        block.scalar(program("act"))
        block.vector(program("dve"))
        block.gpsimd(program("pool"))

        @block.sync
        def _(sp):
            def load(i):
                rows = bass.ds(i * G, G)
                for dst, src in ((x_ld, x_in), (c_ld, ctx_in), (m_ld, mask0_in)):
                    sp.dma_start(b3(dst[:, :]), src[rows, :, :].rearrange("b t c -> t b c")).then_inc(sems["in"], 16)
                sp.dma_start(cT_ld[:, :], ctxT_in[:, bass.ds(i * T, T)]).then_inc(sems["in"], 16)

            sp.sem_inc(sems["out"], 16)
            sp.dma_start(m1_ld[:, :], mask1_in).then_inc(s_w, 16)
            load(0)
            sp.dma_start(wt[:, :], w_in).then_inc(s_w, 16)

            def turn_(i, last):
                for t in t_copied:
                    sp.wait_ge(sems[t.src], value(t.src, t.n, i))
                    sp.sem_inc(s_step, 1)
                if not last:
                    load(i + 1)
                sp.wait_ge(sems[t_y.src], value(t_y.src, t_y.n, i))
                sp.sem_inc(s_step, 1)
                sp.dma_start(out[bass.ds(i * G, G), :, :].rearrange("b t c -> t b c"), b3(y_st[:, :]))\
                  .then_inc(sems["out"], 16)

            with sp.Fori(0, NG - 1) as i:
                turn_(i, False)
            turn_(NG - 1, True)
            sp.wait_ge(sems["out"], 16 * (NG + 1))


def pack_weights(v):
    def row(a):
        return np.broadcast_to(np.asarray(a).reshape(1, -1), (128, np.asarray(a).size))

    def col(a):
        a = np.asarray(a)
        return a.reshape(-1, 128).T

    def tiles(a):
        a = np.asarray(a)
        return a.reshape(-1, 128, a.shape[1]).transpose(1, 0, 2).reshape(128, -1)

    p = np.arange(128)
    sel3 = np.zeros((128, E3 // 2, 128), np.float32)
    for n in range(E3 // 2):
        sel3[2 * n, n, 0:64] = 1.0
        sel3[2 * n + 1, n, 64:128] = 1.0
    f = {k: np.asarray(a) for k, a in v.items()}
    parts = dict(
        ident=np.eye(128, dtype=np.float32),
        causal=np.where(p[None, :] <= p[:, None], 0.0, NEG).astype(np.float32),
        triu=(p[:, None] <= p[None, :]).astype(np.float32),
        head4=((p[:, None] // DH) % HQ == np.arange(HQ)[None, :]).astype(np.float32),
        rev8=row(np.arange(8, 0, -1, dtype=np.float32)), rev4=row(np.arange(4, 0, -1, dtype=np.float32)),
        rev16=row(np.arange(16, 0, -1, dtype=np.float32)),
        sel3=sel3.reshape(128, -1),
        gates=row(np.concatenate([f["g_xattn"], f["g_ffn"]])),
        wq0=f["L0_xattn_w_q"].T, wk0=f["L0_xattn_w_k"].T, wv0=f["L0_xattn_w_v"].T, wo0=f["L0_xattn_w_o"].T,
        bo0=row(f["L0_xattn_b_o"]),
        gw0=f["L0_ffn_gate_w"].T, gb0=row(f["L0_ffn_gate_bias"]),
        w1_0=np.concatenate([f["L0_ffn_w1"].reshape(-1, D), f["L0_ffn_sw1"]]).T,
        w3_0=np.concatenate([f["L0_ffn_w3"].reshape(-1, D), f["L0_ffn_sw3"]]).T,
        w2_0=tiles(np.concatenate([f["L0_ffn_w2"].transpose(0, 2, 1).reshape(-1, D), f["L0_ffn_sw2"].T])),
        wq1=f["L1_xattn_Wq"].T, bq1=col(f["L1_xattn_bq"]), wk1=f["L1_xattn_Wk"].T, bk1=col(f["L1_xattn_bk"]),
        wv1=f["L1_xattn_Wv"].T, bv1=row(f["L1_xattn_bv"]), wo1=f["L1_xattn_Wo"].T, bo1=row(f["L1_xattn_bo"]),
        sq1=f["L1_ffn_Wq"].reshape(-1, D).T, sk1=f["L1_ffn_Wk"].reshape(-1, D).T,
        sv1=f["L1_ffn_Wv"].reshape(-1, D).T,
        sg1=np.concatenate([f["L1_ffn_Ws"].reshape(-1, D), f["L1_ffn_Wd"].reshape(-1, D)]).T,
        so1=tiles(f["L1_ffn_Wo"].transpose(0, 2, 1).reshape(-1, D)),
        gk2=np.stack([np.concatenate([f["L2_xattn_ig_kernel"][k * 128:(k + 1) * 128],
                                      f["L2_xattn_fg_kernel"][k * 128:(k + 1) * 128]], axis=1)
                      for k in range(3)], axis=1).reshape(128, -1),
        gb2=row(np.concatenate([f["L2_xattn_ig_bias"], f["L2_xattn_fg_bias"]])),
        nw2=row(f["L2_xattn_outnorm_weight"]),
        cw1=f["L2_ffn_w1"].T, conv=row(f["L2_ffn_conv_w"].reshape(F2, 3).T), convb=row(f["L2_ffn_conv_b"]),
        cw2=tiles(f["L2_ffn_w2"].T),
        wq3=f["L3_xattn_Wq"], bq3=col(f["L3_xattn_bq"]), wk3=f["L3_xattn_Wk"], bk3=col(f["L3_xattn_bk"]),
        wv3=f["L3_xattn_Wv"], bv3=row(f["L3_xattn_bv"]), wo3=f["L3_xattn_Wo"], bo3=row(f["L3_xattn_bo"]),
        f1_3=f["L3_xattn_W1"], fb1_3=col(f["L3_xattn_b1"]), f2_3=tiles(f["L3_xattn_W2"]),
        fb2_3=row(f["L3_xattn_b2"]), g1_3=row(f["L3_xattn_ln1_g"]), b1_3=row(f["L3_xattn_ln1_b"]),
        g2_3=row(f["L3_xattn_ln2_g"]), b2_3=row(f["L3_xattn_ln2_b"]),
        gw3=f["L3_ffn_gate_w"].T, gb3=row(f["L3_ffn_bias_e"]),
        up3=np.concatenate([f["L3_ffn_up_w"].reshape(-1, D), f["L3_ffn_shared_up"]]).T,
        down3=tiles(np.concatenate([f["L3_ffn_down_w"].transpose(0, 2, 1).reshape(-1, D), f["L3_ffn_shared_down"].T])),
    )
    packed = np.empty((128, NCOLS), np.float32)
    for name, (at, n) in COLS.items():
        packed[:, at:at + n] = parts[name]
    return packed


def kernel(**inputs):
    import concourse.bacc as bacc
    from concourse.bass_utils import run_bass_kernel_spmd

    nc = bacc.Bacc("TRN2", target_bir_lowering=False, num_devices=1)
    ctx = np.asarray(inputs["ctx_1024"])
    arrays = {
        "x": np.asarray(inputs["x"]),
        "ctx": ctx,
        "ctxT": np.ascontiguousarray(ctx.transpose(2, 0, 1).reshape(D, B * S)),
        "mask0": np.asarray(inputs["mask_BxSxS2_if1"]),
        "mask1": np.asarray(inputs["mask_1x1xSxS2_bf1"]).reshape(S, S).view(np.uint8),
        "weights": pack_weights(inputs),
    }
    arrays = {k: np.ascontiguousarray(a) for k, a in arrays.items()}
    args = [nc.dram_tensor(k, a.shape, mybir.dt.from_np(a.dtype), kind="ExternalInput").ap() for k, a in arrays.items()]
    out = nc.dram_tensor("out", (B, S, D), F32, kind="ExternalOutput").ap()
    build(nc, *args, out)
    r = run_bass_kernel_spmd(nc, [arrays], core_ids=[0])
    return r.results[0]["out"]
```

```python
from contextlib import ExitStack

import numpy as np
import concourse.bass as bass
from concourse import mybir

F32 = mybir.dt.float32
BF16 = mybir.dt.bfloat16
I32 = mybir.dt.int32
U8 = mybir.dt.uint8
ALU = mybir.AluOpType
ACT = mybir.ActivationFunctionType
AX = mybir.AxisListType

B, S, D = 32, 128, 128
G = 2
LANES = 2
TURNS = B // (G * LANES)
T = G * S
H, DH = 16, 8
HQ = 4
POOL_OF, POOL_TURNS = 5, (1, 3)
NEG = -1.0e30
LN_EPS = 1e-5
E0, F0 = 8, 2
E1, D1 = 8, 64
NH2, DH2 = 4, 32
F2 = 512
F3 = 512
E3, I3 = 16, 64
ROUND = 1.5 * 2.0 ** 23
ENGINES = ("pe", "act", "dve", "pool")


class Done:

    def __init__(self, src, n):
        self.src, self.n = src, n


def flat(marks):
    for m in marks:
        if isinstance(m, Done):
            yield m
        elif m is not None:
            yield from flat(m)


class Flow:

    def __init__(self):
        self.steps = {e: [] for e in ENGINES}
        self.waited = {e: {} for e in ENGINES}

    def put(self, eng, us, step, *after):
        need = {}
        for m in flat(after):
            if m.n > self.waited[eng].get(m.src, -1):
                need[m.src] = max(need.get(m.src, -1), m.n)
        self.waited[eng].update(need)
        self.steps[eng].append((need, step, us))
        return Done(eng, len(self.steps[eng]))


def interleave(flows):
    queues = {e: [] for e in ENGINES}
    value = [{e: [0] for e in ENGINES} for _ in flows]
    done = [{e: [0.0] for e in ENGINES} for _ in flows]
    free = {e: 0.0 for e in ENGINES}
    while True:
        best = None
        for k, f in enumerate(flows):
            for e in ENGINES:
                n = len(done[k][e]) - 1
                if n == len(f.steps[e]):
                    continue
                need, step, us = f.steps[e][n]
                if any(src in ENGINES and m >= len(done[k][src]) for src, m in need.items()):
                    continue
                ready = max([done[k][src][m] + 0.1 for src, m in need.items() if src in ENGINES], default=0.0)
                start = max(ready, free[e])
                if best is None or (start, ready) < best[:2]:
                    best = (start, ready, k, e)
        if best is None:
            return queues, value
        start, _, k, e = best
        need, step, us = flows[k].steps[e][len(done[k][e]) - 1]
        queues[e].append((k, need, step))
        value[k][e].append(len(queues[e]))
        free[e] = start + us
        done[k][e].append(free[e])


class Slots:

    def __init__(self, items):
        self.free = [(it, ()) for it in items]

    def take(self):
        return self.free.pop(0)

    def give(self, item, *marks):
        self.free.append((item, tuple(flat(marks))))


def weight_columns():
    sizes = dict(
        ident=128, causal=128, triu=128, head16=H, rev8=8, rev4=4, rev16=16, rows=512, pick0=E0,
        gates=8,
        wq0=128, wk0=128, wv0=128, wo0=128,
        gw0=E0, gb0=E0, w1_0=(E0 + F0) * 128, w3_0=(E0 + F0) * 128, w2_0=(E0 + F0) * 128,
        wq1=128, bq1=1, wk1=128, bk1=1, wv1=128, wo1=128,
        sq1=H * D1, sk1=H * D1, sv1=E1 * D1, sg1=2 * H * E1, so1=E1 * D1 // 128 * 128,
        gk2=3 * 2 * NH2, gb2=2 * NH2, nw2=128, cw1=F2, conv=3 * F2, cw2=F2,
        wq3=128, bq3=1, wk3=128, bk3=1, wv3=128, wo3=128,
        f1_3=F3, fb1_3=F3 // 128, f2_3=F3, g1_3=128, b1_3=128, g2_3=128, b2_3=128,
        gw3=E3, gb3=E3, up3=10 * 128, down3=10 * 128,
    )
    at, cols = 0, {}
    for name, n in sizes.items():
        cols[name] = (at, n)
        at += n
    return cols, at


COLS, NCOLS = weight_columns()
BIAS_ROWS = dict(bo0=(0, 0), bv1=(0, 128), bo1=(0, 256), bv3=(0, 384), bo3=(32, 0), fb2_3=(32, 128), convb=(64, 0))


def build(nc, x_in, ctx_in, ctxT_in, mask0_in, mask1_in, w_in, pick_in, out):
    with ExitStack() as ctx:
        def sb(name, cols, dt=F32, parts=128):
            return ctx.enter_context(nc.sbuf_tensor(name, [parts, cols], dt))

        def sem(name):
            return ctx.enter_context(nc.semaphore(name))

        sems = {e: sem("s_" + e) for e in ENGINES}
        s_w = sem("s_w")
        s_step = sem("s_step")
        for k in range(LANES):
            sems["ctx", k] = sem(f"s_ctx{k}")
            sems["x", k] = sem(f"s_x{k}")
            sems["out", k] = sem(f"s_out{k}")

        bank_tensors = [ctx.enter_context(nc.psum_tensor(f"bank{i}", [128, 512], F32)) for i in range(8)]
        wt = sb("w_sb", NCOLS)

        def w(name, a=0, b=None):
            at, n = COLS[name]
            return wt[:, at + a:at + (n if b is None else b)]

        m1_ld = sb("m1_ld", 128, U8)
        identb, ones, causb = sb("identb", 128, BF16), sb("ones", 128), sb("causb", 128, BF16)
        mb1 = sb("mb1", 128, BF16)
        tg = sb("tg", 8)
        bq1s = sb("bq1s", 2)
        wstat = sb("wstat", 8)
        wconv = w("conv")
        w2b = w("cw1", 0, F2 // 2).bitcast(BF16)
        ident = w("ident")
        pick0b = sb("pick0b", E0, BF16)
        pick3b = sb("pick3b", E3 // 2 * 128, BF16, 3 * E3)

        def b3(ap, n=G):
            return ap.rearrange("p (b c) -> p b c", b=n)

        def bc(ap, axis, n):
            a = ap.unsqueeze(axis)
            shape = list(a.shape)
            shape[axis] = n
            return a.broadcast_to(shape)

        def add_bias(e, acc, name):
            row, col = BIAS_ROWS[name]
            n = acc.shape[1]
            at = COLS["rows"][0] + col
            return e.matmul(acc, ones[row:row + 1, :], wt[row:row + 1, at:at + n], start=False, stop=True)

        qks = [sb(f"qk_{k}", 2 * 8 * T) for k in range(LANES)]
        pick_ld = qks[0][0:3 * E3, 0:E3 // 2 * 128]

        flow = Flow()
        banks = Slots([b[:, :] for b in bank_tensors])

        def pe(step, *after):
            return flow.put("pe", 0.5, step, *after)

        def act(step, *after):
            return flow.put("act", 0.5, step, *after)

        def dve(step, *after):
            return flow.put("dve", 0.5, step, *after)

        load_w = Done("w", 48)
        t_ones = dve(lambda e: e.memset(ones[:, :], 1.0))
        t_idb = dve(lambda e: e.tensor_copy(identb[:, :], ident), load_w)
        dve(lambda e: e.tensor_copy(causb[:, :], w("causal")))
        dve(lambda e: e.tensor_scalar(mb1[:, :], m1_ld[:, :], 0.0, NEG, ALU.is_equal, ALU.mult))
        act(lambda e: e.activation(tg[:, :], w("gates"), ACT.Tanh), load_w)
        dve(lambda e: e.tensor_scalar(bq1s[:, 0:1], w("bq1"), DH ** -0.5, None, ALU.mult))
        dve(lambda e: e.tensor_scalar(bq1s[:, 1:2], w("bq3"), D ** -0.5, None, ALU.mult))

        def ternary(name, at):
            t1 = dve(lambda e: e.tensor_reduce(wstat[:, at + 1:at + 2], w(name), AX.X, ALU.add,
                                               apply_absolute_value=True), load_w)
            bank, was = banks.take()
            t2 = pe(lambda e: e.matmul(bank[:, 0:1], ones[:, :], wstat[:, at + 1:at + 2], start=True, stop=True),
                    t1, t_ones, was)
            t3 = dve(lambda e: e.tensor_scalar(wstat[:, at:at + 1], bank[:, 0:1], 1.0 / (D * F2), 1e-5,
                                               ALU.mult, ALU.max), t2)
            banks.give(bank, t3)
            t4 = dve(lambda e: e.reciprocal(wstat[:, at + 2:at + 3], wstat[:, at:at + 1]), t3)
            t5 = dve(lambda e: e.tensor_scalar(w(name), w(name), wstat[:, at + 2:at + 3], ROUND,
                                               ALU.mult, ALU.add), t4)
            t6 = dve(lambda e: e.tensor_scalar(w(name), w(name), ROUND, 1.0, ALU.subtract, ALU.min), t5)
            return dve(lambda e: e.tensor_scalar(w(name), w(name), -1.0, None, ALU.max), t6)

        t_q1 = ternary("cw1", 0)
        t_q2 = ternary("cw2", 4)
        for k in range(3):
            t_cw1 = dve(lambda e, k=k: e.scalar_tensor_tensor(wconv[:, k * F2:(k + 1) * F2], w("cw1"), wstat[:, 0:1],
                                                      w("conv", k * F2, (k + 1) * F2), ALU.mult, ALU.mult), t_q1)
        dve(lambda e: e.tensor_copy(w2b, w("cw2")), t_q2, t_cw1)
        dve(lambda e: e.tensor_copy(pick0b[:, :], w("pick0")))
        t_pick = dve(lambda e: e.tensor_copy(pick3b[:, :], pick_ld))
        setup = flow

        xs, ctxs, ctxTs, masks, ys = [], [], [], [], []

        def lane(k):
            def sb_(name, cols, dt=F32):
                return sb(f"{name}_{k}", cols, dt)

            flow = Flow()
            banks = Slots([b[:, :] for b in bank_tensors[4 * k:4 * k + 4]])
            m_ld = sb_("m_ld", T, I32)
            y_st = w("cw2", k * T, (k + 1) * T)
            x, ctxN, ctxT = sb_("x", T), sb_("ctxN", T), sb_("ctxT", T)
            xs.append(x[:, :])
            ctxs.append(ctxN[:, :])
            ctxTs.append(ctxT[:, :])
            masks.append(m_ld[:, :])
            ys.append(y_st)
            mb0 = sb_("mb0", T, BF16)
            xn, xnT = sb_("xn", T), sb_("xnT", T)
            qk = qks[k]
            qA, kA = qk[:, 0:8 * T], qk[:, 8 * T:16 * T]
            va = sb_("va", G * H * (D1 + 1))
            oa = sb_("oa", G * H * D1)
            oT = xnT
            pv1 = sb_("pv1", G * E1 * D1)
            mixed1 = sb_("mixed1", E1 * D1)
            prod_mem = sb_("prods", 2 * 1024)
            prods = Slots([prod_mem[:, i * 1024:(i + 1) * 1024] for i in range(2)])
            tmps = Slots([prod_mem[:, i * 512:(i + 1) * 512] for i in range(4)])
            Ps = Slots([sb_(f"P{i}", 512)[:, :] for i in range(2)])
            PTs = Slots([sb_(f"PT{i}", 512)[:, :] for i in range(2)])
            gs, gm, gt = (sb_(n, G * 256) for n in ("gs", "gm", "gt"))
            gw1_, gw2_ = oa[:, 0:G * 256], oa[:, G * 256:2 * G * 256]
            smalls = Slots([sb_(f"small{i}", 32)[:, :] for i in range(8)])
            shifts = Slots([sb_(f"nm{i}", 8)[:, :] for i in range(3)])
            tops = Slots([sb_(f"top{i}", 64)[:, :] for i in range(1)])
            gpart, gateT = sb_("gpart", G * 128, BF16), sb_("gateT", T, BF16)
            r2 = va[:, 0:G * F2 // 2].bitcast(BF16)
            r2T = va[:, G * F2 // 2:G * F2].bitcast(BF16)
            xqT = gt[:, 0:G * 130]

            def pe(step, *after, us=0.45):
                return flow.put("pe", us, step, *after)

            def act(step, *after, us=0.45):
                return flow.put("act", us, step, *after)

            def dve(step, *after, us=0.25):
                return flow.put("dve", us, step, *after)

            def pool(step, *after, us=0.6):
                return flow.put("pool", us, step, *after)

            loads = [Done(("x", k), 16)]
            t_c = Done(("ctx", k), 48)
            stored = Done(("out", k), 16)
            t_x = loads
            t_m = dve(lambda e: e.tensor_scalar(mb0[:, :], m_ld[:, :], 0.0, NEG, ALU.is_equal, ALU.mult), t_c)
            dve(lambda e: e.memset(gpart[:, :], 0.0))

            def rstd(ve, eps_div, n, *after):
                t1_, w1 = smalls.take()
                y_, w2 = smalls.take()
                t1, y = t1_[:, 0:n], y_[:, 0:n]
                m = dve(lambda e: e.memset(t1, -0.5), w1, w2, *after)
                a = dve(lambda e: e.tensor_scalar(ve, ve, eps_div[0], eps_div[1], ALU.mult, ALU.add))
                p = pool(lambda e: e.tensor_tensor(y, ve, t1, ALU.pow), a, m)
                c = dve(lambda e: e.tensor_tensor(t1, y, y, ALU.mult), p)
                c = dve(lambda e: e.tensor_tensor(t1, t1, ve, ALU.mult), c)
                c = dve(lambda e: e.tensor_scalar(t1, t1, -0.5, 1.5, ALU.mult, ALU.add), c)
                c = dve(lambda e: e.tensor_tensor(ve, y, t1, ALU.mult), c)
                smalls.give(t1_, c)
                smalls.give(y_, c)
                return c

            def layernorm(src, dst, *after):
                st_, w1 = smalls.take()
                mv_, w2 = smalls.take()
                st, mv = b3(st_[:, 0:6 * G]), mv_[:, 0:2 * G].rearrange("p (b c) -> p b c", c=2)
                s3, d3 = b3(src), b3(dst)
                for b in range(G):
                    t = dve(lambda e, b=b: e.bn_stats(st[:, b, :], s3[:, b, :]), *after, w1, w2)
                dve(lambda e: e.memset(st_[:, 28:32], 1.0), t)
                for b in range(G):
                    t2 = dve(lambda e, b=b: e.bn_aggr(mv[:, b, :], st[:, b, :]))
                t3 = rstd(mv[:, :, 1], (1.0, LN_EPS), G, t2)
                for b in range(G):
                    t4 = dve(lambda e, b=b: e.tensor_scalar(d3[:, b, :], s3[:, b, :], mv[:, b, 0:1], mv[:, b, 1:2],
                                                            ALU.subtract, ALU.mult), t3)
                smalls.give(st_, t4)
                smalls.give(mv_, t4)
                return t4

            def turn(src, dst, *after):
                bank, was = banks.take()

                def step(e):
                    for b in range(G):
                        r = e.transpose(bank[:, b * 128:(b + 1) * 128], src[:, b * 128:(b + 1) * 128], ident)
                    return r
                t = pe(step, *after, was)
                t = act(lambda e: e.activation(dst, bank[:, 0:T], ACT.Copy), t)
                banks.give(bank, t)
                return t

            def gated_add(layer, bank, *after):
                t = dve(lambda e: e.scalar_tensor_tensor(x[:, :], bank[:, 0:T], tg[:, layer:layer + 1], x[:, :],
                                                         ALU.mult, ALU.add), *after)
                banks.give(bank, t)
                return t

            def project(weight, src, *after):
                bank, was = banks.take()
                return bank, pe(lambda e: e.matmul(bank[:, 0:T], weight, src, start=True, stop=True), *after, was)

            def attend(n, maps, scores, clamp, values, between=None):
                live = {}
                cols = maps * 128

                def start(u):
                    bank, was = banks.take()
                    nm, was_m = shifts.take()
                    P, was_P = Ps.take()
                    t = scores(u, bank, was)
                    t = dve(lambda e: e.tensor_reduce(nm[:, 0:maps], b3(bank[:, 0:cols], maps), AX.X, ALU.max,
                                                      negate=True), t, was_m, us=0.6)
                    if clamp:
                        t = dve(lambda e: e.tensor_scalar(nm[:, 0:maps], nm[:, 0:maps], -NEG / 10, None, ALU.min),
                                t, us=0.07)

                    def step(e):
                        for j in range(maps):
                            c = slice(j * 128, (j + 1) * 128)
                            r = e.activation(P[:, c], bank[:, c], ACT.Exp, bias=nm[:, j:j + 1])
                        return r
                    t = act(step, t, was_P, us=0.3 * maps)
                    shifts.give(nm, t)
                    banks.give(bank, t)
                    live[u] = P, t

                def turn_map(u):
                    P, t = live[u]
                    bank, was = banks.take()
                    PT, was_PT = PTs.take()

                    def step(e):
                        for j in range(maps):
                            r = e.transpose(bank[:, j * 128:(j + 1) * 128], P[:, j * 128:(j + 1) * 128], ident)
                        return r
                    t = pe(step, t, was, us=0.22 * maps)
                    Ps.give(P, t)
                    t = act(lambda e: e.activation(PT[:, 0:cols], bank[:, 0:cols], ACT.Copy), t, was_PT, us=0.55)
                    banks.give(bank, t)
                    live[u] = PT, t

                def finish(u):
                    PT, t = live.pop(u)
                    PTs.give(PT, values(u, PT, t))

                for s in range(n + 2):
                    if s < n:
                        start(s)
                    if 0 <= s - 1 < n:
                        turn_map(s - 1)
                    if 0 <= s - 2 < n:
                        finish(s - 2)
                    if between and s < n:
                        between(s)

            def small_head_attention(layer, wq, bq, wk, bk, wv, bv, wo, bo, mask, clamp, t_mask, t_x):
                t_n = layernorm(x[:, :], xn[:, :], t_x)
                kb, t_k = project(w(wk), ctxT[:, :], t_c, t_x)
                kT_, was = tmps.take()
                kT = kT_[:, 0:T]
                t_k = act(lambda e: e.activation(kT, kb[:, 0:T], ACT.Identity, bias=0.0 if bk is None else bk), t_k, was)
                banks.give(kb, t_k)
                km = qk[:, :].rearrange("p (b h t) -> p b h t", b=G, h=H)
                t_km = []
                for r in range(H // HQ):
                    def keep(e, r=r):
                        for h in range(HQ * r, HQ * r + HQ):
                            m = e.tensor_scalar(km[:, :, h, :], b3(kT), w("head16", h, h + 1), None, ALU.mult)
                        return m
                    t_km.append(dve(keep, t_k, us=0.8))
                tmps.give(kT_, t_km[-1])
                t_nT = turn(xn, xnT[:, :], t_n)
                qT = gs[:, 0:T]
                vb, was = banks.take()

                def v_step(e):
                    for b in range(G):
                        o = vb[:, b * 128:(b + 1) * 128]
                        r = e.matmul(o, ctxT[:, b * 128:(b + 1) * 128], w(wv), start=True, stop=bv is None)
                        if bv is not None:
                            r = add_bias(e, o, bv)
                    return r
                t_v = pe(v_step, was, t_c, t_x)
                v4 = va[:, 0:G * H * (DH + 1)].rearrange("p (b h d) -> p b h d", b=G, h=H)
                t_va = [dve(lambda e: e.memset(v4[:, :, :, DH], 1.0), t_x),
                        dve(lambda e: e.tensor_copy(v4[:, :, :, 0:DH].rearrange("p b h d -> p (b h) d"),
                                                    vb[:, 0:T].rearrange("p (n d) -> p n d", d=DH)), t_v)]
                banks.give(vb, t_va)
                qb, t_q = project(w(wq), xnT[:, :], t_nT)
                t_qT = act(lambda e: e.activation(qT, qb[:, 0:T], ACT.Identity, scale=DH ** -0.5,
                                                        bias=0.0 if bq is None else bq), t_q)
                banks.give(qb, t_qT)

                def scores(u, bank, was):
                    b, r = divmod(u, 4)

                    def step(e):
                        e.matmul(bank, qT[:, b * 128:(b + 1) * 128], km[:, b, HQ * r:HQ * r + HQ, :], start=True, stop=False,
                                 skip_group_check=True)
                        return e.matmul(bank, identb[:, :], bc(mask(b), 1, HQ), start=False, stop=True,
                                        skip_group_check=True)
                    return pe(step, t_qT, t_km[r], t_mask, was, us=1.07)

                per = {}
                y_bank = {}

                def values(u, PT, t):
                    b, r = divmod(u, 4)
                    if r == 0:
                        per["O"], per["was"] = banks.take()
                    O = per["O"]

                    def step(e):
                        for j in range(HQ):
                            h = HQ * r + j
                            m = e.matmul(O[:, h * 9:h * 9 + 9], PT[:, j * 128:(j + 1) * 128], v4[:, b, h, :],
                                         start=True, stop=True)
                        return m
                    t_pv = pe(step, t, t_va, per["was"], us=0.87)
                    if r == 3:
                        o3 = O[:, 0:H * 9].rearrange("p (h d) -> p h d", h=H)
                        rec, was = smalls.take()
                        t1 = dve(lambda e: e.reciprocal(rec[:, 0:H], o3[:, :, DH]), t_pv, was)
                        on = oa[:, b * 128:(b + 1) * 128].rearrange("p (h d) -> p h d", h=H)
                        t2 = dve(lambda e: e.tensor_tensor(on, o3[:, :, 0:DH], bc(rec[:, 0:H], 2, DH), ALU.mult), t1)
                        smalls.give(rec, t2)
                        banks.give(O, t2)
                        y_bank["t"] = t2
                    return t_pv

                attend(G * H // HQ, HQ, scores, clamp, values)
                t_oT = turn(oa, oT[:, :], y_bank["t"])
                yb, was = banks.take()

                def y_step(e):
                    for b in range(G):
                        o = yb[:, b * 128:(b + 1) * 128]
                        e.matmul(o, oT[:, b * 128:(b + 1) * 128], w(wo), start=True, stop=False)
                        r = add_bias(e, o, bo)
                    return r
                return gated_add(layer, yb, pe(y_step, t_oT, was))

            def top(src, work1, work2, mask, n, width, k, rev, *after):
                s3 = src.rearrange("p (n e) -> p n e", e=width)
                a3 = work1.rearrange("p (n e) -> p n e", e=width)
                r_, wr = tops.take()
                r = r_[:, 0:n]
                cur, t = s3, list(after) + [wr]
                cur_flat = src
                for i in range(k):
                    t1 = dve(lambda e, c=cur: e.tensor_reduce(r, c, AX.X, ALU.max), t)
                    t2 = dve(lambda e, c=cur: e.tensor_tensor(a3, c, bc(r, 2, width), ALU.is_equal), t1)
                    t3 = dve(lambda e: e.tensor_tensor(a3, a3, bc(rev, 1, n), ALU.mult), t2)
                    t4 = dve(lambda e: e.tensor_reduce(r, a3, AX.X, ALU.max), t3)
                    t5 = dve(lambda e: e.tensor_tensor(a3, a3, bc(r, 2, width), ALU.is_equal), t4)
                    if i < k - 1:
                        t = dve(lambda e, c=cur_flat: e.scalar_tensor_tensor(work2, work1, -3.0e38, c, ALU.mult, ALU.add), t5)
                    if i == 0:
                        t_m = dve(lambda e: e.tensor_copy(mask, work1), t5)
                    else:
                        t_m = dve(lambda e: e.tensor_tensor(mask, mask, work1, ALU.add), t5)
                    t = [t, t_m]
                    cur, cur_flat = work2.rearrange("p (n e) -> p n e", e=width), work2
                tops.give(r_, t_m)
                return t_m

            t_x = small_head_attention(0, "wq0", None, "wk0", None, "wv0", None, "wo0", "bo0",
                                       lambda b: mb0[:, b * 128:(b + 1) * 128], True, t_m, t_x)

            def widen(sel, gT, *after):
                bank, was = banks.take()
                return bank, pe(lambda e: e.matmul(bank[:, 0:T], sel, gT, start=True, stop=True), *after, was)

            def turn_gates(src, width, *after):
                n = 3 * width
                parts = b3(gpart[:, :])[:, :, 0:n].rearrange("p b (k e) -> p b k e", k=3)
                s3 = src.rearrange("p (b e) -> p b e", b=G)
                t = after
                for i in range(3):
                    t = dve(lambda e, i=i: e.tensor_copy(parts[:, :, i, :], s3), t, us=0.1)
                    if i < 2:
                        t = dve(lambda e, i=i: e.tensor_tensor(s3, s3, parts[:, :, i, :], ALU.subtract), t, us=0.1)
                bank, was = banks.take()
                bb = bank[:, 0:T // 2].bitcast(BF16)

                def step(e):
                    for b in range(G):
                        c = slice(b * 128, (b + 1) * 128)
                        r = e.transpose(bb[:, c], gpart[:, c], identb[:, :])
                    return r
                t = pe(step, t, was)
                t = act(lambda e: e.activation(gateT[0:n, :], bb[0:n, :], ACT.Copy), t)
                banks.give(bank, t)
                return t

            def sum_tiles(layer, tiles, hT, weight, *after):
                yb, was = banks.take()

                def step(e):
                    for b in range(G):
                        for n in range(tiles):
                            r = e.matmul(yb[:, b * 128:(b + 1) * 128], hT[:, n * T + b * 128:n * T + (b + 1) * 128],
                                         w(weight, n * 128, (n + 1) * 128), start=(n == 0), stop=(n == tiles - 1))
                    return r
                return gated_add(layer, yb, pe(step, *after, was, us=4.4))

            def mixture0(t_x):
                t_n = layernorm(x[:, :], xn[:, :], t_x)
                t_nT = turn(xn, xnT[:, :], t_n)
                lb, was = banks.take()

                def l_step(e):
                    for b in range(G):
                        r = e.matmul(lb[:, b * E0:(b + 1) * E0], xnT[:, b * 128:(b + 1) * 128], w("gw0"),
                                     start=True, stop=True)
                    return r
                t_l = pe(l_step, t_nT, was)
                ne = G * E0
                l3 = lb[:, 0:ne].rearrange("p (b e) -> p b e", b=G)
                sc, sb_ = gs[:, 0:ne], gs[:, ne:2 * ne]
                sc3, sb3 = (a.rearrange("p (b e) -> p b e", b=G) for a in (sc, sb_))
                mx, was = smalls.take()
                t = dve(lambda e: e.tensor_reduce(mx[:, 0:G], l3, AX.X, ALU.max), t_l, was)
                t = dve(lambda e: e.tensor_tensor(sc3, l3, bc(mx[:, 0:G], 2, E0), ALU.subtract), t)
                banks.give(lb, t)
                t = act(lambda e: e.activation(sc, sc, ACT.Exp), t)
                t = dve(lambda e: e.tensor_reduce(mx[:, 0:G], sc3, AX.X, ALU.add), t)
                t = dve(lambda e: e.reciprocal(mx[:, 0:G], mx[:, 0:G]), t)
                t = dve(lambda e: e.tensor_tensor(sc3, sc3, bc(mx[:, 0:G], 2, E0), ALU.mult), t)
                smalls.give(mx, t)
                t = dve(lambda e: e.tensor_tensor(sb3, sc3, bc(w("gb0"), 1, G), ALU.add), t)
                t = top(sb_, gw1_[:, 0:ne], gw2_[:, 0:ne], gm[:, 0:ne], G, E0, 2, w("rev8"), t)
                t = dve(lambda e: e.scalar_tensor_tensor(sc, sc, 0.5, gm[:, 0:ne], ALU.mult, ALU.mult), t)
                t_g = turn_gates(sc, E0, t)
                t_h = []
                order = list(range(E0, E0 + F0)) + list(range(E0))
                for n in order:
                    a_, t_a = project(w("w1_0", n * 128, (n + 1) * 128), xnT[:, :], t_nT)
                    c_, t_c3 = project(w("w3_0", n * 128, (n + 1) * 128), xnT[:, :], t_nT)
                    th_, was = tmps.take()
                    a, c, th = a_[:, 0:T], c_[:, 0:T], th_[:, 0:T]
                    t = act(lambda e, th=th, a=a: e.activation(th, a, ACT.Tanh, scale=0.5), t_a, was)
                    t = dve(lambda e, th=th, a=a: e.scalar_tensor_tensor(th, th, 1.0, a, ALU.add, ALU.mult), t)
                    banks.give(a_, t)
                    h = qk[:, n * T:(n + 1) * T]
                    if n >= E0:
                        t = dve(lambda e, th=th, c=c, h=h: e.scalar_tensor_tensor(h, th, 0.5, c, ALU.mult, ALU.mult), t, t_c3)
                        banks.give(c_, t)
                    else:
                        t = dve(lambda e, th=th, c=c: e.tensor_tensor(th, th, c, ALU.mult), t, t_c3)
                        banks.give(c_, t)
                        g_, t_w = widen(pick0b[0:3 * E0, n:n + 1].broadcast_to((3 * E0, 128)), gateT[0:3 * E0, :], t_g)
                        t = dve(lambda e, th=th, g=g_[:, 0:T], h=h: e.tensor_tensor(h, th, g, ALU.mult), t, t_w)
                        banks.give(g_, t)
                    tmps.give(th_, t)
                    t_h.append(t)
                return sum_tiles(4, E0 + F0, qk, "w2_0", t_h)

            t_x = mixture0(t_x)

            t_x = small_head_attention(1, "wq1", bq1s[:, 0:1], "wk1", w("bk1"), "wv1", "bv1", "wo1", "bo1",
                                       lambda b: mb1[:, :], False, None, t_x)

            def switched_attention(t_x):
                t_n = layernorm(x[:, :], xn[:, :], t_x)
                t_nT = turn(xn, xnT[:, :], t_n)
                NGATE = 2 * H * E1
                for half in range(G // 2):
                    gb, was = banks.take()

                    def g_step(e, gb=gb, half=half):
                        for i in range(2):
                            b = 2 * half + i
                            r = e.matmul(gb[:, i * NGATE:(i + 1) * NGATE], xnT[:, b * 128:(b + 1) * 128], w("sg1"),
                                         start=True, stop=True)
                        return r
                    t = pe(g_step, t_nT, was)
                    t_g = act(lambda e, gb=gb, half=half: e.activation(gs[:, half * 512:half * 512 + 512], gb, ACT.Copy), t)
                    banks.give(gb, t_g)
                for b in range(G):
                    pb_, was = banks.take()
                    t = pe(lambda e, b=b, o=pb_: e.matmul(o, xnT[:, b * 128:(b + 1) * 128], w("sv1"), start=True, stop=True),
                           t_nT, was)
                    t_pv = act(lambda e, b=b, o=pb_: e.activation(pv1[:, b * 512:(b + 1) * 512], o, ACT.Copy, scale=0.5), t)
                    banks.give(pb_, t_pv)
                t_top = top(gs[:, :], gw1_[:, :], gw2_[:, :], gm[:, :], 2 * G * H, E1, 2, w("rev8"), t_g)
                t = act(lambda e: e.activation(gt[:, :], gs[:, :], ACT.Tanh, scale=0.5), t_g)
                t_mix = dve(lambda e: e.scalar_tensor_tensor(gt[:, :], gt[:, :], 1.0, gm[:, :], ALU.add, ALU.mult), t, t_top)
                mix = gt[:, :].rearrange("p (b s h e) -> p b s h e", b=G, s=2, h=H)
                sel = gm[:, :].rearrange("p (b s h e) -> p b s h e", b=G, s=2, h=H)
                t_qk = []
                for n in range(8):
                    for wn, dst in (("sq1", qA), ("sk1", kA)):
                        bank, t = project(w(wn, n * 128, (n + 1) * 128), xnT[:, :], t_nT)
                        t = act(lambda e, n=n, dst=dst, bank=bank: e.activation(
                            dst[:, n * T:(n + 1) * T], bank[:, 0:T], ACT.Copy, scale=D1 ** -0.5 if dst is qA else 1.0), t)
                        banks.give(bank, t)
                        t_qk.append(t)
                v4 = va[:, :].rearrange("p (b h d) -> p b h d", b=G, h=H)
                t_one = dve(lambda e: e.memset(v4[:, :, :, D1], 1.0), t_x)
                t_v = {b: [t_one] for b in range(G)}
                turn_of = [0]

                def mixed(out_, in0, in1, shape, *after):
                    pr, was = prods.take()
                    p4 = pr.rearrange(*shape[0], **shape[1])
                    on_pool = turn_of[0] % POOL_OF in POOL_TURNS
                    turn_of[0] += 1
                    t = (pool if on_pool else dve)(lambda e: e.tensor_tensor(p4, in0, in1, ALU.mult), *after, was,
                                                   us=3.3 if on_pool else 1.15)
                    t = dve(lambda e: e.tensor_reduce(out_, p4, AX.X, ALU.add), t, us=1.15)
                    prods.give(pr, t)
                    return t

                pv4 = pv1[:, :].rearrange("p (b e d) -> p b d e", b=G, e=E1)

                def mix_values(b, h):
                    t_v[b].append(mixed(v4[:, b, h:h + 2, 0:D1], bc(mix[:, b, 0, h:h + 2, :], 2, D1),
                                        bc(pv4[:, b, :, :], 1, 2), (("p (h d e) -> p h d e",), dict(h=2, e=E1)),
                                        t_mix, t_pv))

                o4 = oa[:, :].rearrange("p (b h d) -> p b d h", b=G, h=H)
                t_o = {b: [] for b in range(G)}
                U = mixed1[:, :]
                u3 = U.rearrange("p (e d) -> p e d", e=E1)
                t_u = []
                uT = pv1[:, :]
                t_uT = []

                def mix_outputs(b):
                    t = []
                    for ex in range(E1):
                        t.append(mixed(u3[:, ex, :], o4[:, b, :, :], bc(sel[:, b, 1, :, ex], 1, D1),
                                       (("p (d h) -> p d h",), dict(h=H)), t_o[b], t_u))
                    bank, was = banks.take()

                    def step(e):
                        for n in range(4):
                            r = e.transpose(bank[:, n * 128:(n + 1) * 128], U[:, n * 128:(n + 1) * 128], ident)
                        return r
                    t_u.append(pe(step, t, was))
                    t = act(lambda e: e.activation(uT[:, b * 512:(b + 1) * 512], bank, ACT.Copy), t_u[-1], t_v[b], us=0.6)
                    banks.give(bank, t)
                    t_uT.append(t)

                def scores(u, bank, was):
                    b, g = divmod(u, 4)
                    rows = slice(64 * (g % 2), 64 * (g % 2) + 64)

                    def step(e):
                        for j in range(HQ):
                            c = (HQ * (g // 2) + j) * T + b * 128
                            r = e.matmul(bank[:, j * 128:(j + 1) * 128], qA[rows, c:c + 128], kA[rows, c:c + 128],
                                         start=(j == 0), stop=True, skip_group_check=True)
                        return r
                    return pe(step, t_qk, was, us=0.87)

                def values(u, PT, t):
                    b, g = divmod(u, 4)
                    O, was = banks.take()

                    def step(e):
                        for j in range(HQ):
                            r = e.matmul(O[:, j * 65:j * 65 + 65], PT[:, j * 128:(j + 1) * 128], v4[:, b, 8 * (g // 2) + 2 * j + g % 2, :],
                                         start=True, stop=True)
                        return r
                    t_p = pe(step, t, t_v[b], was, us=0.87)
                    o3 = O[:, 0:HQ * 65].rearrange("p (h d) -> p h d", h=HQ)
                    rec, was = smalls.take()
                    t1 = dve(lambda e: e.reciprocal(rec[:, 0:HQ], o3[:, :, D1]), t_p, was)
                    dst = oa[:, :].rearrange("p (b g j r d) -> p b g j r d", b=G, g=2, j=HQ, r=2)[:, b, g // 2, :, g % 2, :]
                    t2 = dve(lambda e: e.tensor_tensor(dst, o3[:, :, 0:D1], bc(rec[:, 0:HQ], 2, D1), ALU.mult), t1)
                    smalls.give(rec, t2)
                    banks.give(O, t2)
                    t_o[b].append(t2)
                    return t_p

                for h in range(0, H, 2):
                    mix_values(0, h)

                def between(s):
                    b, g = divmod(s, 4)
                    if b + 1 < G:
                        mix_values(b + 1, 4 * g)
                        mix_values(b + 1, 4 * g + 2)

                attend(G * H // HQ, HQ, scores, False, values, between)
                for b in range(G):
                    mix_outputs(b)
                yb, was = banks.take()

                def y_step(e):
                    for b in range(G):
                        for n in range(4):
                            r = e.matmul(yb[:, b * 128:(b + 1) * 128], uT[:, b * 512 + n * 128:b * 512 + (n + 1) * 128],
                                         w("so1", n * 128, (n + 1) * 128), start=(n == 0), stop=(n == 3))
                    return r
                return gated_add(5, yb, pe(y_step, t_uT, was, us=1.8))

            t_x = switched_attention(t_x)

            def mlstm(t_x):
                t_n = layernorm(x[:, :], xn[:, :], t_x)
                t_nT = turn(xn, xnT[:, :], t_n)
                gb, was = banks.take()
                NGK = 2 * NH2

                def g_step(e):
                    for b in range(G):
                        o = gb[:, b * NGK:(b + 1) * NGK]
                        e.matmul(o, xnT[:, b * 128:(b + 1) * 128], w("gk2", 0, NGK), start=True, stop=False)
                        for part in (1, 2):
                            e.matmul(o, ctxT[:, b * 128:(b + 1) * 128], w("gk2", part * NGK, (part + 1) * NGK),
                                     start=False, stop=False)
                        r = e.matmul(o, ones[0:1, :], w("gb2")[0:1, :], start=False, stop=True)
                    return r
                t_g = pe(g_step, t_nT, was)
                n = G * NH2
                g4 = gb[:, 0:G * NGK].rearrange("p (b k h) -> p b k h", b=G, k=2)
                ab, lf, ig, cum, av, mneg = (gs[:, i * n:(i + 1) * n] for i in range(6))
                v3 = {k: a.rearrange("p (b h) -> p b h", b=G) for k, a in
                      dict(ab=ab, lf=lf, ig=ig, cum=cum, av=av).items()}
                t = act(lambda e: e.activation(v3["ab"], g4[:, :, 1, :], ACT.Abs), t_g)
                t = act(lambda e: e.activation(ab, ab, ACT.Exp, scale=-1.0), t)
                t_s = act(lambda e: e.activation(ab, ab, ACT.Ln, bias=1.0), t)
                t = dve(lambda e: e.tensor_copy(v3["ig"], g4[:, :, 0, :]), t_g, t_s)
                t = dve(lambda e: e.tensor_scalar(v3["lf"], g4[:, :, 1, :], 0.0, None, ALU.min), t)
                banks.give(gb, t)
                t = dve(lambda e: e.tensor_tensor(lf, lf, ab, ALU.subtract), t, t_s)
                cb, was = banks.take()
                t = pe(lambda e: e.matmul(cb[:, 0:n], w("triu"), lf, start=True, stop=True), t, was)
                t = dve(lambda e: e.tensor_copy(cum, cb[:, 0:n]), t)
                banks.give(cb, t)
                t_a = dve(lambda e: e.tensor_tensor(av, ig, cum, ALU.subtract), t)
                v4 = va[:, 0:G * NH2 * (DH2 + 1)].rearrange("p (b h d) -> p b h d", b=G, h=NH2)
                t_va = [dve(lambda e: e.memset(v4[:, :, :, DH2], 1.0), t_x),
                        act(lambda e: e.activation(v4[:, :, :, 0:DH2].rearrange("p b h d -> p (b h) d"),
                                                   ctxN[:, :].rearrange("p (n d) -> p n d", d=DH2), ACT.Copy), t_x)]
                hn = oa[:, 0:T]
                t_h = []
                live = {}

                def decay(h):
                    m = live[h] = {}
                    dg, was = tmps.take()
                    for b in range(G):
                        t = dve(lambda e, b=b: e.tensor_scalar(dg[:, b * 128:(b + 1) * 128], ident,
                                                               av[:, b * NH2 + h:b * NH2 + h + 1], None, ALU.mult), t_a, was)
                    A_, was = banks.take()
                    A = A_[:, 0:T]

                    def a_step(e):
                        e.matmul(A, ones[:, :], dg[:, 0:T], start=True, stop=False, skip_group_check=True)
                        return e.matmul(A, identb[:, :], bc(causb[:, :], 1, G), start=False, stop=True,
                                        skip_group_check=True)
                    t = pe(a_step, t, was)
                    tmps.give(dg, t)
                    nm = mneg[:, h * G:(h + 1) * G]
                    t = dve(lambda e: e.tensor_reduce(nm, b3(A), AX.X, ALU.max, negate=True), t)
                    m.update(A=A_, t=t, nm=nm)

                def decay2(h):
                    m = live[h]
                    A_, nm = m["A"], m["nm"]
                    A = A_[:, 0:T]
                    t = pe(lambda e: e.matmul(A, ident, bc(nm, 2, 128), start=False, stop=True,
                                              skip_group_check=True), m["t"])
                    Pd, was = Ps.take()
                    t_D = act(lambda e: e.activation(Pd[:, 0:T], A, ACT.Exp), t, was)
                    banks.give(A_, t_D)
                    Q, was = banks.take()

                    def q_step(e):
                        rows = slice(32 * h, 32 * h + 32)
                        for b in range(G):
                            r = e.matmul(Q[:, b * 128:(b + 1) * 128], xnT[rows, b * 128:(b + 1) * 128],
                                         ctxT[rows, b * 128:(b + 1) * 128], start=True, stop=True)
                        return r
                    t = pe(q_step, t_nT, was)
                    t = dve(lambda e: e.scalar_tensor_tensor(Pd[:, 0:T], Q[:, 0:T], DH2 ** -0.5, Pd[:, 0:T], ALU.mult, ALU.mult), t, t_D)
                    banks.give(Q, t)
                    m.update(P=Pd, t=t)

                def weigh(h):
                    m = live.pop(h)
                    Pd = m["P"]
                    bank, was = banks.take()

                    def t_step(e):
                        for b in range(G):
                            r = e.transpose(bank[:, b * 128:(b + 1) * 128], Pd[:, b * 128:(b + 1) * 128], ident)
                        return r
                    t = pe(t_step, m["t"], was)
                    Ps.give(Pd, t)
                    PT, was = PTs.take()
                    t = act(lambda e: e.activation(PT[:, 0:T], bank[:, 0:T], ACT.Copy), t, was)
                    banks.give(bank, t)
                    O, was = banks.take()

                    def o_step(e):
                        for b in range(G):
                            r = e.matmul(O[:, b * 33:b * 33 + 33], PT[:, b * 128:(b + 1) * 128], v4[:, b, h, :],
                                         start=True, stop=True)
                        return r
                    t = pe(o_step, t, t_va, was)
                    PTs.give(PT, t)
                    o3 = O[:, 0:G * 33].rearrange("p (b d) -> p b d", b=G)
                    nr, was = smalls.take()
                    e4, s4 = nr[:, 0:G], nr[:, G:2 * G]
                    cu = v3["cum"][:, :, h]
                    t1 = dve(lambda e: e.tensor_tensor(e4, m["nm"], cu, ALU.subtract), was)
                    t1 = act(lambda e: e.activation(e4, e4, ACT.Exp), t1)
                    t2 = dve(lambda e: e.tensor_scalar(s4, o3[:, :, DH2], -1.0, None, ALU.mult), t)
                    t2 = dve(lambda e: e.tensor_tensor(s4, s4, o3[:, :, DH2], ALU.max), t2)
                    t2 = dve(lambda e: e.tensor_tensor(s4, s4, e4, ALU.max), t2, t1)
                    t2 = dve(lambda e: e.tensor_scalar(s4, s4, 1e-6, None, ALU.add), t2)
                    t2 = dve(lambda e: e.reciprocal(s4, s4), t2)
                    t2 = dve(lambda e: e.tensor_tensor(hn.rearrange("p (b h d) -> p b h d", b=G, h=NH2)[:, :, h, :],
                                                       o3[:, :, 0:DH2], bc(s4, 2, DH2), ALU.mult), t2)
                    smalls.give(nr, t2)
                    banks.give(O, t2)
                    t_h.append(t2)

                for s in range(NH2 + 2):
                    if s < NH2:
                        decay(s)
                    if 0 <= s - 1 < NH2:
                        decay2(s - 1)
                    if 0 <= s - 2 < NH2:
                        weigh(s - 2)
                h3 = hn.rearrange("p (n d) -> p n d", d=DH2)
                mn, was = smalls.take()
                vr, was2 = smalls.take()
                sq_, was3 = tmps.take()
                sq = sq_[:, 0:T]
                t = dve(lambda e: e.tensor_reduce(mn[:, 0:n], h3, AX.X, ALU.add), t_h, was, was2, was3)
                t = dve(lambda e: e.tensor_scalar(mn[:, 0:n], mn[:, 0:n], 1.0 / DH2, None, ALU.mult), t)
                t = dve(lambda e: e.tensor_tensor(h3, h3, bc(mn[:, 0:n], 2, DH2), ALU.subtract), t)
                t = dve(lambda e: e.tensor_tensor(sq, hn, hn, ALU.mult), t)
                t = dve(lambda e: e.tensor_reduce(vr[:, 0:n], sq.rearrange("p (n d) -> p n d", d=DH2), AX.X, ALU.add), t)
                tmps.give(sq_, t)
                t = rstd(vr[:, 0:n], (1.0 / DH2, 1e-6), n, t)
                t = dve(lambda e: e.tensor_tensor(h3, h3, bc(vr[:, 0:n], 2, DH2), ALU.mult), t)
                smalls.give(mn, t)
                smalls.give(vr, t)
                t = dve(lambda e: e.tensor_tensor(b3(hn), b3(hn), bc(w("nw2"), 1, G), ALU.mult), t)
                return dve(lambda e: e.scalar_tensor_tensor(x[:, :], hn, tg[:, 2:3], x[:, :], ALU.mult, ALU.add), t)

            t_x = mlstm(t_x)

            def conv_ffn(t_x):
                q3 = xqT.rearrange("p (b t) -> p b t", t=130)
                t_pad = dve(lambda e: e.memset(q3[:, :, 0:130:129], 0.0), t_x)
                t_n = layernorm(x[:, :], xn[:, :], t_x)
                am_, was = smalls.take()
                am, sc = am_[:, 0:G], am_[:, G:2 * G]
                t = dve(lambda e: e.tensor_reduce(am, b3(xn[:, :]), AX.X, ALU.max, apply_absolute_value=True), t_n, was)
                t = dve(lambda e: e.tensor_scalar(am, am, 1e-5, None, ALU.max), t)
                t = dve(lambda e: e.reciprocal(sc, am), t)
                t = dve(lambda e: e.tensor_scalar(sc, sc, 127.0, None, ALU.mult), t)
                t = dve(lambda e: e.tensor_scalar(am, am, 1.0 / 127.0, None, ALU.mult), t)
                x3 = b3(xn[:, :])
                for b in range(G):
                    t1 = dve(lambda e, b=b: e.tensor_scalar(x3[:, b, :], x3[:, b, :], sc[:, b:b + 1], ROUND,
                                                            ALU.mult, ALU.add), t)
                t1 = dve(lambda e: e.tensor_scalar(xn[:, :], xn[:, :], ROUND, 127.0, ALU.subtract, ALU.min), t1)
                for b in range(G):
                    t2 = dve(lambda e, b=b: e.tensor_scalar(x3[:, b, :], x3[:, b, :], -128.0, am[:, b:b + 1],
                                                            ALU.max, ALU.mult), t1)
                smalls.give(am_, t2)
                bank, was = banks.take()

                def t_step(e):
                    for b in range(G):
                        r = e.transpose(bank[:, b * 128:(b + 1) * 128], xn[:, b * 128:(b + 1) * 128], ident)
                    return r
                t = pe(t_step, t2, was)
                t_q = act(lambda e: e.activation(q3[:, :, 1:129], b3(bank[:, 0:T]), ACT.Copy), t)
                banks.give(bank, t_q)
                yb, yw = banks.take()
                live = {}
                h2 = oa[:, 0:G * F2]
                sc2_, was_s = smalls.take()
                t_y = []

                def hidden(b):
                    hb, was = banks.take()

                    def step(e):
                        for k in range(3):
                            e.matmul(hb, q3[:, b, k:k + 128], wconv[:, k * F2:(k + 1) * F2], start=(k == 0), stop=False)
                        return add_bias(e, hb, "convb")
                    t = pe(step, t_q, t_pad, was, us=3.4)
                    h = h2[:, b * F2:(b + 1) * F2]
                    th, was = tmps.take()
                    t = act(lambda e: e.activation(th, hb, ACT.Tanh, scale=0.5), t, was)
                    t = dve(lambda e: e.scalar_tensor_tensor(h, th, 1.0, hb, ALU.add, ALU.mult), t)
                    banks.give(hb, t)
                    tmps.give(th, t)
                    a, s, o = (sc2_[:, k * G + b:k * G + b + 1] for k in range(3))
                    t = dve(lambda e: e.tensor_reduce(a, h, AX.X, ALU.max, apply_absolute_value=True), t, was_s)
                    t = dve(lambda e: e.tensor_scalar(a, a, 2e-5, None, ALU.max), t)
                    t = dve(lambda e: e.reciprocal(s, a), t)
                    t = dve(lambda e: e.tensor_scalar(s, s, 127.0, None, ALU.mult), t)
                    t1 = dve(lambda e: e.tensor_scalar(a, a, 0.5 / 127.0, wstat[:, 4:5], ALU.mult, ALU.mult), t)
                    live[b, "o"] = dve(lambda e: e.tensor_scalar(o, a, tg[:, 6:7], None, ALU.mult), t1)
                    t = dve(lambda e: e.tensor_scalar(h, h, s, ROUND, ALU.mult, ALU.add), t)
                    t = dve(lambda e: e.tensor_scalar(h, h, ROUND, 127.0, ALU.subtract, ALU.min), t)
                    live[b] = dve(lambda e: e.tensor_scalar(r2[:, b * F2:(b + 1) * F2], h, -128.0, None, ALU.max), t)

                def second(b):
                    bank, was = banks.take()
                    bb = bank[:, 0:256].bitcast(BF16)

                    def step(e):
                        for n in range(4):
                            r = e.transpose(bb[:, n * 128:(n + 1) * 128], r2[:, b * F2 + n * 128:b * F2 + (n + 1) * 128],
                                            identb[:, :])
                        return r
                    t = pe(step, live[b], was)
                    t = act(lambda e: e.activation(r2T[:, b * F2:(b + 1) * F2], bb, ACT.Copy), t)
                    banks.give(bank, t)

                    def y_step(e):
                        for n in range(4):
                            r = e.matmul(yb[:, b * 128:(b + 1) * 128], r2T[:, b * F2 + n * 128:b * F2 + (n + 1) * 128],
                                         w2b[:, n * 128:(n + 1) * 128], start=(n == 0), stop=(n == 3))
                        return r
                    t_y.append(pe(y_step, t, yw))

                for s in range(G + 1):
                    if s < G:
                        hidden(s)
                    if s >= 1:
                        second(s - 1)
                xx = b3(x[:, :])
                for b in range(G):
                    t = dve(lambda e, b=b: e.scalar_tensor_tensor(xx[:, b, :], yb[:, b * 128:(b + 1) * 128],
                                                                  sc2_[:, 2 * G + b:2 * G + b + 1], xx[:, b, :],
                                                                  ALU.mult, ALU.add), t_y, live[b, "o"])
                banks.give(yb, t)
                smalls.give(sc2_, t)
                return t

            t_x = conv_ffn(t_x)

            def wide_attention(t_x):
                t_n = layernorm(x[:, :], xn[:, :], t_x)
                t_nT = turn(xn, xnT[:, :], t_n)
                kb, t = project(w("wk3"), ctxT[:, :], t_x)
                t_kp = t
                t_k = act(lambda e: e.activation(kA[:, 0:T], kb[:, 0:T], ACT.Identity, bias=w("bk3")), t)
                banks.give(kb, t_k)
                qb, t = project(w("wq3"), xnT[:, :], t_nT)
                t_q = act(lambda e: e.activation(qA[:, 0:T], qb[:, 0:T], ACT.Identity, scale=D ** -0.5,
                                                        bias=bq1s[:, 1:2]), t)
                banks.give(qb, t_q)
                vb, was = banks.take()

                def v_step(e):
                    for b in range(G):
                        o = vb[:, b * 128:(b + 1) * 128]
                        e.matmul(o, ctxT[:, b * 128:(b + 1) * 128], w("wv3"), start=True, stop=False)
                        r = add_bias(e, o, "bv3")
                    return r
                t_vp = t = pe(v_step, was)
                v3 = va[:, 0:G * (D + 1)].rearrange("p (b d) -> p b d", b=G)
                t_va = [dve(lambda e: e.memset(v3[:, :, D], 1.0), t_x),
                        dve(lambda e: e.tensor_copy(v3[:, :, 0:D], b3(vb[:, 0:T])), t)]
                banks.give(vb, t_va)

                def scores(u, bank, was):
                    def step(e):
                        for b in range(G):
                            c = slice(b * 128, (b + 1) * 128)
                            r = e.matmul(bank[:, c], qA[:, c], kA[:, c], start=(b == 0), stop=True, skip_group_check=True)
                        return r
                    return pe(step, t_q, t_k, was)

                res = {}

                def values(u, PT, t):
                    t_on = []
                    for half in range(G // 2):
                        O, was = banks.take()

                        def step(e, O=O, half=half):
                            for i in range(2):
                                b = 2 * half + i
                                r = e.matmul(O[:, i * 129:i * 129 + 129], PT[:, b * 128:(b + 1) * 128], v3[:, b, :],
                                             start=True, stop=True)
                            return r
                        t_p = pe(step, t, t_va, was)
                        o3 = O[:, 0:258].rearrange("p (b d) -> p b d", b=2)
                        rec, was = smalls.take()
                        t1 = dve(lambda e, o3=o3, rec=rec: e.reciprocal(rec[:, 0:2], o3[:, :, D]), t_p, was)
                        t2 = dve(lambda e, o3=o3, rec=rec, half=half: e.tensor_tensor(
                            oa[:, half * 256:half * 256 + 256].rearrange("p (b d) -> p b d", b=2), o3[:, :, 0:D],
                            bc(rec[:, 0:2], 2, D), ALU.mult), t1)
                        smalls.give(rec, t2)
                        banks.give(O, t2)
                        t_on.append(t2)
                    res["t"] = t_on
                    return t_p

                attend(1, G, scores, False, values)
                t_oT = turn(oa, oT[:, :], res["t"])
                yb, was = banks.take()

                def y_step(e):
                    for b in range(G):
                        o = yb[:, b * 128:(b + 1) * 128]
                        e.matmul(o, oT[:, b * 128:(b + 1) * 128], w("wo3"), start=True, stop=False)
                        r = add_bias(e, o, "bo3")
                    return r
                t_y = pe(y_step, t_oT, was)
                t = t_cn = dve(lambda e: e.scalar_tensor_tensor(xn[:, :], ctxN[:, :], 2.0, xn[:, :], ALU.mult, ALU.add), t_nT)
                t = dve(lambda e: e.tensor_tensor(xn[:, :], xn[:, :], yb[:, 0:T], ALU.add), t, t_y)
                banks.give(yb, t)
                t = layernorm(xn[:, :], xn[:, :], t)
                t = dve(lambda e: e.tensor_tensor(b3(xn[:, :]), b3(xn[:, :]), bc(w("g1_3"), 1, G), ALU.mult), t)
                t = dve(lambda e: e.tensor_tensor(b3(xn[:, :]), b3(xn[:, :]), bc(w("b1_3"), 1, G), ALU.add), t)
                t_nT = turn(xn, xnT[:, :], t)
                t_h = []
                for n in range(F3 // 128):
                    bank, t = project(w("f1_3", n * 128, (n + 1) * 128), xnT[:, :], t_nT)
                    t = act(lambda e, n=n, bank=bank: e.activation(qk[:, (2 + n) * T:(3 + n) * T], bank[:, 0:T], ACT.Relu,
                                                                   bias=w("fb1_3", n, n + 1)), t)
                    banks.give(bank, t)
                    t_h.append(t)
                zb, was = banks.take()

                def f_step(e, zb=zb):
                    for b in range(G):
                        o = zb[:, b * 128:(b + 1) * 128]
                        for n in range(F3 // 128):
                            e.matmul(o, qk[:, (2 + n) * T + b * 128:(2 + n) * T + (b + 1) * 128],
                                     w("f2_3", n * 128, (n + 1) * 128), start=(n == 0), stop=False)
                        r = add_bias(e, o, "fb2_3")
                    return r
                t_y = pe(f_step, t_h, was, us=2.2)
                t = dve(lambda e, zb=zb: e.tensor_tensor(xn[:, :], xn[:, :], zb[:, 0:T], ALU.add), t_y)
                banks.give(zb, t)
                t = layernorm(xn[:, :], xn[:, :], t)
                t = dve(lambda e: e.tensor_tensor(b3(xn[:, :]), b3(xn[:, :]), bc(w("g2_3"), 1, G), ALU.mult), t)
                t = dve(lambda e: e.tensor_tensor(b3(xn[:, :]), b3(xn[:, :]), bc(w("b2_3"), 1, G), ALU.add), t)
                return [t_vp, t_kp, t_cn], dve(lambda e: e.scalar_tensor_tensor(x[:, :], xn[:, :], tg[:, 3:4], x[:, :], ALU.mult, ALU.add), t)

            t_ctx, t_x = wide_attention(t_x)

            def mixture3(t_x):
                t_n = layernorm(x[:, :], xn[:, :], t_x)
                t_nT = turn(xn, xnT[:, :], t_n)
                lb, was = banks.take()

                def l_step(e):
                    for b in range(G):
                        r = e.matmul(lb[:, b * E3:(b + 1) * E3], xnT[:, b * 128:(b + 1) * 128], w("gw3"),
                                     start=True, stop=True)
                    return r
                t_l = pe(l_step, t_nT, was)
                ne, ng = G * E3, G * 4
                sc, sb_, mk, pr, w1_, w2_, gmk, gw = (gs[:, i * ne:(i + 1) * ne] for i in range(8))
                t = act(lambda e: e.activation(sc, lb[:, 0:ne], ACT.Exp, scale=-1.0), t_l)
                banks.give(lb, t)
                t = dve(lambda e: e.tensor_scalar(sc, sc, 1.0, None, ALU.add), t)
                t = dve(lambda e: e.reciprocal(sc, sc), t)
                t = dve(lambda e: e.tensor_tensor(sb_.rearrange("p (b e) -> p b e", b=G),
                                                  sc.rearrange("p (b e) -> p b e", b=G), bc(w("gb3"), 1, G), ALU.add), t)
                t = top(sb_, w1_, w2_, mk, ng, 4, 2, w("rev4"), t)
                t = dve(lambda e: e.tensor_tensor(pr, mk, sb_, ALU.mult), t)
                r1, was = smalls.take()
                t = dve(lambda e: e.tensor_reduce(r1[:, 0:ng], pr.rearrange("p (g e) -> p g e", e=4), AX.X, ALU.add), t, was)
                t = top(r1[:, 0:ng], w1_[:, 0:ng], w2_[:, 0:ng], gmk[:, 0:ng], G, 4, 2, w("rev4"), t)
                smalls.give(r1, t)
                t = dve(lambda e: e.tensor_tensor(sb_.rearrange("p (g e) -> p g e", e=4),
                                                  sb_.rearrange("p (g e) -> p g e", e=4), bc(gmk[:, 0:ng], 2, 4), ALU.mult), t)
                t = top(sb_, w1_, w2_, mk, G, E3, 4, w("rev16"), t)
                t = dve(lambda e: e.tensor_tensor(sc, sc, mk, ALU.mult), t)
                r2_, was = smalls.take()
                sc3 = sc.rearrange("p (b e) -> p b e", b=G)
                t = dve(lambda e: e.tensor_reduce(r2_[:, 0:G], sc3, AX.X, ALU.add), t, was)
                t = dve(lambda e: e.tensor_scalar(r2_[:, 0:G], r2_[:, 0:G], 1e-20, None, ALU.add), t)
                t = dve(lambda e: e.reciprocal(r2_[:, 0:G], r2_[:, 0:G]), t)
                t = dve(lambda e: e.tensor_scalar(r2_[:, 0:G], r2_[:, 0:G], 2.5, None, ALU.mult), t)
                t = dve(lambda e: e.tensor_tensor(sc3, sc3, bc(r2_[:, 0:G], 2, E3), ALU.mult), t)
                smalls.give(r2_, t)
                t_g = turn_gates(sc, E3, t)
                t_h = []
                for n in list(range(8, 10)) + list(range(8)):
                    a_, t_a = project(w("up3", n * 128, (n + 1) * 128), xnT[:, :], t_nT)
                    th_, was = tmps.take()
                    a, th = a_[:, 0:T], th_[:, 0:T]
                    h = qk[:, n * T:(n + 1) * T]
                    t = act(lambda e, th=th, a=a: e.activation(th, a, ACT.Relu), t_a, was)
                    dst = h if n >= 8 else th
                    t = dve(lambda e, th=th, a=a, dst=dst: e.tensor_tensor(dst, th, a, ALU.mult), t)
                    banks.give(a_, t)
                    if n < 8:
                        g_, t_w = widen(pick3b[:, n * 128:(n + 1) * 128], gateT[0:3 * E3, :], t_g)
                        t = dve(lambda e, th=th, g=g_[:, 0:T], h=h: e.tensor_tensor(h, th, g, ALU.mult), t, t_w)
                        banks.give(g_, t)
                    tmps.give(th_, t)
                    t_h.append(t)
                yb, was = banks.take()

                def step(e):
                    for b in range(G):
                        for n in range(10):
                            r = e.matmul(yb[:, b * 128:(b + 1) * 128], qk[:, n * T + b * 128:n * T + (b + 1) * 128],
                                         w("down3", n * 128, (n + 1) * 128), start=(n == 0), stop=(n == 9))
                    return r
                t = pe(step, t_h, was, us=4.4)
                t_y = dve(lambda e: e.scalar_tensor_tensor(y_st, yb[:, 0:T], tg[:, 7:8], x[:, :], ALU.mult, ALU.add),
                          t, stored)
                banks.give(yb, t_y)
                return t_y

            t_y = mixture3(t_x)
            return flow, t_m, t_ctx, t_y

        lanes = [lane(k) for k in range(LANES)]
        queues, values_ = interleave([ln[0] for ln in lanes])
        base = {e: len(setup.steps[e]) for e in ENGINES}
        per_turn = {e: len(queues[e]) for e in ENGINES}
        for k in range(LANES):
            for what, n in (("ctx", 48), ("x", 16), ("out", 16)):
                base[what, k], per_turn[what, k] = 0, n

        def value(src, n, i):
            return i * per_turn[src] + (base[src] + n)

        def in_turn(k, src, n):
            return values_[k][src][n] if src in ENGINES else n

        def program(name):
            def run(eng):
                for need, step, _ in setup.steps[name]:
                    for src, n in need.items():
                        eng.wait_ge(s_w if src == "w" else sems[src], n)
                    step(eng).then_inc(sems[name], 1)
                with eng.Fori(0, TURNS) as i:
                    waited = {}
                    for src in ENGINES:
                        if base[src]:
                            eng.wait_ge(sems[src], value(src, 0, i))
                    for k, need, step in queues[name]:
                        for src, n in need.items():
                            m = in_turn(k, src, n)
                            if m > waited.get(src, 0):
                                waited[src] = m
                                eng.wait_ge(sems[src], value(src, m, i))
                        step(eng).then_inc(sems[name], 1)
            return run

        block = ctx.enter_context(nc.Block())
        block.tensor(program("pe"))
        block.scalar(program("act"))
        block.vector(program("dve"))
        block.gpsimd(program("pool"))

        @block.sync
        def _(sp):
            def seqs(i, k):
                return bass.ds((i * LANES + k) * G, G)

            def wait(k, t, i):
                sp.wait_ge(sems[t.src], value(t.src, in_turn(k, t.src, t.n), i))
                sp.sem_inc(s_step, 1)

            def load_ctx(i, k):
                for dst, src in ((ctxs[k], ctx_in), (masks[k], mask0_in)):
                    sp.dma_start(b3(dst), src[seqs(i, k), :, :].rearrange("b t c -> t b c"))\
                      .then_inc(sems["ctx", k], 16)
                sp.dma_start(ctxTs[k], ctxT_in[:, bass.ds((i * LANES + k) * T, T)]).then_inc(sems["ctx", k], 16)

            def load_x(i, k):
                sp.dma_start(b3(xs[k]), x_in[seqs(i, k), :, :].rearrange("b t c -> t b c"))\
                  .then_inc(sems["x", k], 16)

            sp.dma_start(m1_ld[:, :], mask1_in).then_inc(s_w, 16)
            for k in range(LANES):
                sp.sem_inc(sems["out", k], 16)
                load_x(0, k)
                load_ctx(0, k)
            sp.dma_start(pick_ld, pick_in).then_inc(s_w, 16)
            sp.dma_start(wt[:, :], w_in).then_inc(s_w, 16)

            def turn_(i, last):
                if not last:
                    for k, (_, t_m, t_ctx, _) in enumerate(lanes):
                        for t in flat([t_m, t_ctx]):
                            wait(k, t, i)
                        load_ctx(i + 1, k)
                for k, (_, _, _, t_y) in enumerate(lanes):
                    wait(k, t_y, i)
                    if not last:
                        load_x(i + 1, k)
                    sp.dma_start(out[seqs(i, k), :, :].rearrange("b t c -> t b c"), b3(ys[k]))\
                      .then_inc(sems["out", k], 16)

            with sp.Fori(0, TURNS - 1) as i:
                turn_(i, False)
            turn_(TURNS - 1, True)
            for k in range(LANES):
                sp.wait_ge(sems["out", k], 16 * (TURNS + 1))


def pack_weights(v):
    def row(a):
        return np.broadcast_to(np.asarray(a).reshape(1, -1), (128, np.asarray(a).size))

    def col(a):
        a = np.asarray(a)
        return a.reshape(-1, 128).T

    def tiles(a):
        a = np.asarray(a)
        return a.reshape(-1, 128, a.shape[1]).transpose(1, 0, 2).reshape(128, -1)

    p = np.arange(128)
    f = {k: np.asarray(a) for k, a in v.items()}
    parts = dict(
        ident=np.eye(128, dtype=np.float32),
        causal=np.where(p[None, :] <= p[:, None], 0.0, NEG).astype(np.float32),
        triu=(p[:, None] <= p[None, :]).astype(np.float32),
        head16=(p[:, None] // DH == np.arange(H)[None, :]).astype(np.float32),
        rev8=row(np.arange(8, 0, -1, dtype=np.float32)), rev4=row(np.arange(4, 0, -1, dtype=np.float32)),
        rev16=row(np.arange(16, 0, -1, dtype=np.float32)),
        rows=np.zeros((128, 512), np.float32), pick0=np.tile(np.eye(E0, dtype=np.float32), (128 // E0, 1)),
        gates=row(np.concatenate([f["g_xattn"], f["g_ffn"]])),
        wq0=f["L0_xattn_w_q"].T, wk0=f["L0_xattn_w_k"].T, wv0=f["L0_xattn_w_v"].T, wo0=f["L0_xattn_w_o"].T,
        gw0=f["L0_ffn_gate_w"].T, gb0=row(f["L0_ffn_gate_bias"]),
        w1_0=np.concatenate([f["L0_ffn_w1"].reshape(-1, D), f["L0_ffn_sw1"]]).T,
        w3_0=np.concatenate([f["L0_ffn_w3"].reshape(-1, D), f["L0_ffn_sw3"]]).T,
        w2_0=tiles(np.concatenate([f["L0_ffn_w2"].transpose(0, 2, 1).reshape(-1, D), f["L0_ffn_sw2"].T])),
        wq1=f["L1_xattn_Wq"].T, bq1=col(f["L1_xattn_bq"]), wk1=f["L1_xattn_Wk"].T, bk1=col(f["L1_xattn_bk"]),
        wv1=f["L1_xattn_Wv"].T, wo1=f["L1_xattn_Wo"].T,
        sq1=f["L1_ffn_Wq"].reshape(-1, D).T, sk1=f["L1_ffn_Wk"].reshape(-1, D).T,
        sv1=f["L1_ffn_Wv"].reshape(-1, D).T,
        sg1=np.concatenate([f["L1_ffn_Ws"].reshape(-1, D), f["L1_ffn_Wd"].reshape(-1, D)]).T,
        so1=tiles(f["L1_ffn_Wo"].transpose(0, 2, 1).reshape(-1, D)),
        gk2=np.stack([np.concatenate([f["L2_xattn_ig_kernel"][k * 128:(k + 1) * 128],
                                      f["L2_xattn_fg_kernel"][k * 128:(k + 1) * 128]], axis=1)
                      for k in range(3)], axis=1).reshape(128, -1),
        gb2=row(np.concatenate([f["L2_xattn_ig_bias"], f["L2_xattn_fg_bias"]])),
        nw2=row(f["L2_xattn_outnorm_weight"]),
        cw1=f["L2_ffn_w1"].T, conv=row(f["L2_ffn_conv_w"].reshape(F2, 3).T),
        cw2=tiles(f["L2_ffn_w2"].T),
        wq3=f["L3_xattn_Wq"], bq3=col(f["L3_xattn_bq"]), wk3=f["L3_xattn_Wk"], bk3=col(f["L3_xattn_bk"]),
        wv3=f["L3_xattn_Wv"], wo3=f["L3_xattn_Wo"],
        f1_3=f["L3_xattn_W1"], fb1_3=col(f["L3_xattn_b1"]), f2_3=tiles(f["L3_xattn_W2"]),
        g1_3=row(f["L3_xattn_ln1_g"]), b1_3=row(f["L3_xattn_ln1_b"]),
        g2_3=row(f["L3_xattn_ln2_g"]), b2_3=row(f["L3_xattn_ln2_b"]),
        gw3=f["L3_ffn_gate_w"].T, gb3=row(f["L3_ffn_bias_e"]),
        up3=np.concatenate([f["L3_ffn_up_w"].reshape(-1, D), f["L3_ffn_shared_up"]]).T,
        down3=tiles(np.concatenate([f["L3_ffn_down_w"].transpose(0, 2, 1).reshape(-1, D), f["L3_ffn_shared_down"].T])),
    )
    packed = np.empty((128, NCOLS), np.float32)
    for name, (at, n) in COLS.items():
        packed[:, at:at + n] = parts[name]
    rows = dict(bo0=f["L0_xattn_b_o"], bv1=f["L1_xattn_bv"], bo1=f["L1_xattn_bo"], bv3=f["L3_xattn_bv"],
                bo3=f["L3_xattn_bo"], fb2_3=f["L3_xattn_b2"], convb=f["L2_ffn_conv_b"])
    for name, (r, c) in BIAS_ROWS.items():
        at = COLS["rows"][0] + c
        packed[r, at:at + rows[name].size] = rows[name]
    return packed


def kernel(**inputs):
    import concourse.bacc as bacc
    from concourse.bass_utils import run_bass_kernel_spmd

    nc = bacc.Bacc("TRN2", target_bir_lowering=False, num_devices=1)
    ctx = np.asarray(inputs["ctx_1024"])
    arrays = {
        "x": np.asarray(inputs["x"]),
        "ctx": ctx,
        "ctxT": np.ascontiguousarray(ctx.transpose(2, 0, 1).reshape(D, B * S)),
        "mask0": np.asarray(inputs["mask_BxSxS2_if1"]),
        "mask1": np.asarray(inputs["mask_1x1xSxS2_bf1"]).reshape(S, S).view(np.uint8),
        "weights": pack_weights(inputs),
        "pick": np.tile(np.repeat(np.eye(E3, dtype=np.float32), 64, axis=1), (3, 1)),
    }
    arrays = {k: np.ascontiguousarray(a) for k, a in arrays.items()}
    args = [nc.dram_tensor(k, a.shape, mybir.dt.from_np(a.dtype), kind="ExternalInput").ap() for k, a in arrays.items()]
    out = nc.dram_tensor("out", (B, S, D), F32, kind="ExternalOutput").ap()
    build(nc, *args, out)
    r = run_bass_kernel_spmd(nc, [arrays], core_ids=[0])
    return r.results[0]["out"]
```

```python
from contextlib import ExitStack

import numpy as np
import concourse.bass as bass
from concourse import mybir

F32 = mybir.dt.float32
BF16 = mybir.dt.bfloat16
I32 = mybir.dt.int32
U8 = mybir.dt.uint8
ALU = mybir.AluOpType
ACT = mybir.ActivationFunctionType
AX = mybir.AxisListType

B, S, D = 32, 128, 128
G = 2
LANES = 2
TURNS = B // (G * LANES)
PATIENCE = 0.1
AHEAD = 3
T = G * S
H, DH = 16, 8
HQ = 4
MIXERS = ("pool", "dve", "pool")
OUT_AFTER = 6
LAG = 1
NEG = -1.0e30
LN_EPS = 1e-5
E0, F0 = 8, 2
E1, D1 = 8, 64
NH2, DH2 = 4, 32
F2 = 512
F3 = 512
E3, I3 = 16, 64
ROUND = 1.5 * 2.0 ** 23
ENGINES = ("pe", "act", "dve", "pool")


class Done:

    def __init__(self, src, n):
        self.src, self.n = src, n


def flat(marks):
    for m in marks:
        if isinstance(m, Done):
            yield m
        elif m is not None:
            yield from flat(m)


def columns(ap):
    return int(np.prod(ap.shape[1:]))


class Clock:

    def __init__(self, eng):
        self.eng, self.us = eng, 0.0

    def vector(self, ap, share=1.0):
        n = columns(ap) * share
        self.us += 0.06 + n / 960 if self.eng == "dve" else 0.6 + n / 390

    def memset(self, out, value):
        self.us += 0.02

    def tensor_copy(self, out, a):
        self.vector(a, 0.6)

    def tensor_scalar(self, out, a, *rest):
        self.vector(a, 0.75)

    def tensor_tensor(self, out, a, *rest):
        self.vector(a)

    def scalar_tensor_tensor(self, out, a, *rest):
        self.vector(a)

    def tensor_reduce(self, out, a, *rest, **kw):
        self.vector(a)

    def reciprocal(self, out, a):
        self.vector(a)

    def bn_stats(self, out, a):
        self.vector(a)

    def bn_aggr(self, out, a):
        self.vector(a)

    def activation(self, out, a, func, bias=0.0, scale=1.0):
        self.us += 0.06 + columns(a) / 1200 + (0.0 if isinstance(bias, float) and isinstance(scale, float) else 0.09)

    def matmul(self, out, lhsT, rhs, **kw):
        n = columns(rhs)
        self.us += max(0.06, n / 2400) if rhs.dtype == BF16 else max(0.2, n / 600)

    def transpose(self, out, a, identity):
        self.us += 0.06 if a.dtype == BF16 else 0.22


class Flow:

    def __init__(self, at=0.0):
        self.at = at
        self.steps = {e: [] for e in ENGINES}
        self.waited = {e: {} for e in ENGINES}

    def put(self, eng, step, *after):
        need = {}
        for m in flat(after):
            if m.n > self.waited[eng].get(m.src, -1):
                need[m.src] = max(need.get(m.src, -1), m.n)
        self.waited[eng].update(need)
        clock = Clock(eng)
        step(clock)
        self.steps[eng].append((need, step, clock.us))
        return Done(eng, len(self.steps[eng]))


LATENCY = {("act", "pe"): 0.39, ("dve", "pe"): 0.22, ("pe", "pe"): 0.1, ("pool", "dve"): 0.06}


def interleave(flows):
    tails = [path_lengths(f) for f in flows]
    queues = {e: [] for e in ENGINES}
    value = [{e: [0] for e in ENGINES} for _ in flows]
    done = [{e: [0.0] for e in ENGINES} for _ in flows]
    free = {e: 0.0 for e in ENGINES}
    while True:
        heads = []
        for k, f in enumerate(flows):
            for e in ENGINES:
                n = len(done[k][e]) - 1
                if n == len(f.steps[e]):
                    continue
                need, step, us = f.steps[e][n]
                if any(src in ENGINES and m >= len(done[k][src]) for src, m in need.items()):
                    continue
                ready = max([done[k][src][m] + LATENCY.get((src, e), 0.15) for src, m in need.items()
                             if src in ENGINES], default=f.at)
                heads.append((max(ready, free[e]), -tails[k][e][n], k, e))
        if not heads:
            return queues, value
        first = min(heads)
        start, _, k, e = min((h for h in heads if h[3] == first[3] and h[0] <= first[0] + PATIENCE), key=lambda h: h[1])
        need, step, us = flows[k].steps[e][len(done[k][e]) - 1]
        queues[e].append((k, need, step))
        value[k][e].append(len(queues[e]))
        free[e] = start + us
        done[k][e].append(free[e])


def path_lengths(flow):
    tail = {e: [0.0] * len(flow.steps[e]) for e in ENGINES}
    users = {}
    for e in ENGINES:
        for n, (need, _, _) in enumerate(flow.steps[e]):
            for src, m in need.items():
                if src in ENGINES:
                    users.setdefault((src, m - 1), []).append((e, n))
    at = {e: len(flow.steps[e]) - 1 for e in ENGINES}
    while any(n >= 0 for n in at.values()):
        for e in ENGINES:
            n = at[e]
            if n >= 0 and all(m > at[o] for o, m in users.get((e, n), ()) if o != e):
                after = [tail[o][m] + LATENCY.get((e, o), 0.15) for o, m in users.get((e, n), ())]
                if n + 1 < len(tail[e]):
                    after.append(tail[e][n + 1])
                tail[e][n] = flow.steps[e][n][2] + max(after, default=0.0)
                at[e] -= 1
    return tail


class Slots:

    def __init__(self, items):
        self.free = [(it, ()) for it in items]

    def take(self):
        return self.free.pop(0)

    def give(self, item, *marks):
        self.free.append((item, tuple(flat(marks))))


def weight_columns():
    sizes = dict(
        ident=128, causal=128, triu=128, head16=H, rev8=8, rev4=4, rev16=16, rows=512, part3=3, pick0=E0,
        gates=8,
        wq0=128, wk0=128, wv0=128, wo0=128,
        gw0=E0, gb0=E0, w1_0=(E0 + F0) * 128, w3_0=(E0 + F0) * 128, w2_0=(E0 + F0) * 128,
        wq1=128, bq1=1, wk1=128, bk1=1, wv1=128, wo1=128,
        sq1=H * D1, sk1=H * D1, sv1=E1 * D1, sg1=2 * H * E1, so1=E1 * D1 // 128 * 128,
        gk2=3 * 2 * NH2, gb2=2 * NH2, nw2=128, cw1=F2, conv=3 * F2, cw2=F2,
        wq3=128, bq3=1, wk3=128, bk3=1, wv3=128, wo3=128,
        f1_3=F3, fb1_3=F3 // 128, f2_3=F3, g1_3=128, b1_3=128, g2_3=128, b2_3=128,
        gw3=E3, gb3=E3, up3=10 * 128, down3=10 * 128,
    )
    at, cols = 0, {}
    for name, n in sizes.items():
        cols[name] = (at, n)
        at += n
    return cols, at


COLS, NCOLS = weight_columns()
BIAS_ROWS = dict(bo0=(0, 0), bv1=(0, 128), bo1=(0, 256), bv3=(0, 384), bo3=(32, 0), fb2_3=(32, 128), convb=(64, 0))


def build(nc, x_in, ctx_in, ctxT_in, mask0_in, mask1_in, w_in, pick_in, out):
    with ExitStack() as ctx:
        def sb(name, cols, dt=F32, parts=128):
            return ctx.enter_context(nc.sbuf_tensor(name, [parts, cols], dt))

        def sem(name):
            return ctx.enter_context(nc.semaphore(name))

        sems = {e: sem("s_" + e) for e in ENGINES}
        s_w = sems["w"] = sem("s_w")
        s_w2 = sems["w2"] = sem("s_w2")
        s_step = sem("s_step")
        for k in range(LANES):
            sems["ctx", k] = sem(f"s_ctx{k}")
            sems["x", k] = sem(f"s_x{k}")
            sems["out", k] = sem(f"s_out{k}")

        bank_tensors = [ctx.enter_context(nc.psum_tensor(f"bank{i}", [128, 512], F32)) for i in range(8)]
        wt = sb("w_sb", NCOLS)

        def w(name, a=0, b=None):
            at, n = COLS[name]
            return wt[:, at + a:at + (n if b is None else b)]

        m1_ld = sb("m1_ld", 128, U8)
        identb, ones, causb = sb("identb", 128, BF16), sb("ones", 128), sb("causb", 128, BF16)
        mb1 = sb("mb1", 128, BF16)
        onesb, rowsb = sb("onesb", 128, BF16), sb("rowsb", 512, BF16, 67)
        tg = sb("tg", 8)
        bq1s = sb("bq1s", 2)
        wstat = sb("wstat", 8)
        wconv = w("conv")
        w2b = w("cw1", 0, F2 // 2).bitcast(BF16)
        ident = w("ident")
        pick0b = sb("pick0b", E0, BF16)
        pick3b = sb("pick3b", E3 // 2 * 128, BF16, 3 * E3)

        def b3(ap, n=G):
            return ap.rearrange("p (b c) -> p b c", b=n)

        def bc(ap, axis, n):
            a = ap.unsqueeze(axis)
            shape = list(a.shape)
            shape[axis] = n
            return a.broadcast_to(shape)

        def add_bias(e, acc, name):
            row, col = BIAS_ROWS[name]
            n = acc.shape[1]
            return e.matmul(acc, onesb[row:row + 3, :], rowsb[row:row + 3, col:col + n], start=False, stop=True)

        qks = [sb(f"qk_{k}", 2 * 8 * T) for k in range(LANES)]
        gparts = [sb(f"gpart_{k}", G * 128, BF16) for k in range(LANES)]
        pick_ld = qks[0][0:3 * E3, 0:E3 // 2 * 128]

        flow = Flow()
        def act(step, *after):
            return flow.put("act", step, *after)

        def dve(step, *after):
            return flow.put("dve", step, *after)

        load_w = Done("w", 48)
        load_w2 = Done("w2", 16)
        dve(lambda e: e.memset(ones[:, :], 1.0))
        dve(lambda e: e.tensor_copy(identb[:, :], ident), load_w)
        dve(lambda e: e.tensor_copy(causb[:, :], w("causal")))
        dve(lambda e: e.tensor_scalar(mb1[:, :], m1_ld[:, :], 0.0, NEG, ALU.is_equal, ALU.mult))
        act(lambda e: e.activation(tg[:, :], w("gates"), ACT.Tanh), load_w)
        dve(lambda e: e.memset(onesb[:, :], 1.0))
        rest_, part_ = w("rows")[0:67, :], qks[0][0:67, 1024:1280].bitcast(BF16)
        t = dve(lambda e: e.tensor_copy(part_, rest_))
        for i in range(3):
            pick = w("part3", i, i + 1)[0:67, :]
            if i == 0:
                t1 = dve(lambda e, p=pick: e.tensor_scalar(rowsb[:, :], part_, p, None, ALU.mult), t)
            else:
                t1 = dve(lambda e, p=pick: e.scalar_tensor_tensor(rowsb[:, :], part_, p, rowsb[:, :], ALU.mult, ALU.add), t, t1)
            if i < 2:
                t = dve(lambda e: e.tensor_tensor(rest_, rest_, part_, ALU.subtract), t1)
                t = dve(lambda e: e.tensor_copy(part_, rest_), t)
        dve(lambda e: e.tensor_scalar(bq1s[:, 0:1], w("bq1"), DH ** -0.5, None, ALU.mult))
        dve(lambda e: e.tensor_copy(pick0b[:, :], w("pick0")))
        dve(lambda e: e.tensor_copy(pick3b[:, :], pick_ld))
        for k in range(LANES):
            dve(lambda e, k=k: e.memset(gparts[k][:, :], 0.0))
        setup = flow

        def quantise():
            flow = Flow(at=60.0)
            banks = Slots([b[:, :] for b in bank_tensors[0:4]])

            def pe(step, *after):
                return flow.put("pe", step, *after)

            def dve(step, *after):
                return flow.put("dve", step, *after)

            dve(lambda e: e.tensor_scalar(bq1s[:, 1:2], w("bq3"), D ** -0.5, None, ALU.mult), load_w2)

            def ternary(name, at):
                t1 = dve(lambda e: e.tensor_reduce(wstat[:, at + 1:at + 2], w(name), AX.X, ALU.add,
                                                   apply_absolute_value=True), load_w2)
                bank, was = banks.take()
                t2 = pe(lambda e: e.matmul(bank[:, 0:1], ones[:, :], wstat[:, at + 1:at + 2], start=True, stop=True),
                        t1, was)
                t3 = dve(lambda e: e.tensor_scalar(wstat[:, at:at + 1], bank[:, 0:1], 1.0 / (D * F2), 1e-5,
                                                   ALU.mult, ALU.max), t2)
                banks.give(bank, t3)
                t4 = dve(lambda e: e.reciprocal(wstat[:, at + 2:at + 3], wstat[:, at:at + 1]), t3)
                t5 = dve(lambda e: e.tensor_scalar(w(name), w(name), wstat[:, at + 2:at + 3], ROUND,
                                                   ALU.mult, ALU.add), t4)
                t6 = dve(lambda e: e.tensor_scalar(w(name), w(name), ROUND, 1.0, ALU.subtract, ALU.min), t5)
                return dve(lambda e: e.tensor_scalar(w(name), w(name), -1.0, None, ALU.max), t6)

            t_q1 = ternary("cw1", 0)
            t_q2 = ternary("cw2", 4)
            dve(lambda e: e.tensor_scalar(wstat[:, 7:8], wstat[:, 4:5], 0.5, tg[:, 6:7], ALU.mult, ALU.mult), t_q2)
            for k in range(3):
                t_cw1 = dve(lambda e, k=k: e.scalar_tensor_tensor(wconv[:, k * F2:(k + 1) * F2], w("cw1"), wstat[:, 0:1],
                                                          w("conv", k * F2, (k + 1) * F2), ALU.mult, ALU.mult), t_q1)
            dve(lambda e: e.tensor_copy(w2b, w("cw2")), t_q2, t_cw1)
            return flow

        buffers = {}
        xs, ctxs, ctxTs, masks, ys = ({} for _ in range(5))

        def lane(k, stages):
            def sb_(name, cols, dt=F32):
                if (name, k) not in buffers:
                    buffers[name, k] = sb(f"{name}_{k}", cols, dt)
                return buffers[name, k]

            flow = Flow()
            banks = Slots([b[:, :] for b in bank_tensors[4 * k:4 * k + 4]])
            m_ld = sb_("m_ld", T, I32)
            y_st = w("cw2", k * T, (k + 1) * T)
            x, ctxN, ctxT = sb_("x", T), sb_("ctxN", T), sb_("ctxT", T)
            xs[k] = x[:, :]
            ctxs[k] = ctxN[:, :]
            ctxTs[k] = ctxT[:, :]
            masks[k] = m_ld[:, :]
            ys[k] = y_st
            mb0 = sb_("mb0", T, BF16)
            xn, xnT = sb_("xn", T), sb_("xnT", T)
            qk = qks[k]
            qA, kA = qk[:, 0:8 * T], qk[:, 8 * T:16 * T]
            va = sb_("va", G * H * (D1 + 1))
            oa = sb_("oa", G * H * D1)
            oT = xnT
            pv1 = sb_("pv1", G * E1 * D1)
            mixed1_gs = sb_("mixed1_gs", E1 * D1 + G * 256)
            mixed1 = mixed1_gs[:, 0:E1 * D1]
            prod_mem = sb_("prods", 2 * 1024)
            prods = Slots([prod_mem[:, i * 1024:(i + 1) * 1024] for i in range(2)])
            tmps = Slots([prod_mem[:, i * 512:(i + 1) * 512] for i in range(4)])
            P_mem, PT_mem = sb_("P", 2 * 512), sb_("PT", 2 * 512)
            Ps = Slots([P_mem[:, i * 512:(i + 1) * 512] for i in range(2)])
            PTs = Slots([PT_mem[:, i * 512:(i + 1) * 512] for i in range(2)])
            gs = mixed1_gs[:, E1 * D1:]
            gm, gt = (sb_(n, G * 256) for n in ("gm", "gt"))
            gw1_, gw2_ = oa[:, 0:G * 256], oa[:, G * 256:2 * G * 256]
            smalls = Slots([sb_(f"small{i}", 32)[:, :] for i in range(8)])
            shifts = Slots([sb_(f"nm{i}", 8)[:, :] for i in range(3)])
            tops = Slots([sb_(f"top{i}", 64)[:, :] for i in range(1)])
            gpart, gateT = gparts[k], sb_("gateT", T, BF16)
            r2 = va[:, 0:G * F2 // 2].bitcast(BF16)
            r2T = va[:, G * F2 // 2:G * F2].bitcast(BF16)
            xqT = gt[:, 0:G * 130]

            def pe(step, *after):
                return flow.put("pe", step, *after)

            def act(step, *after):
                return flow.put("act", step, *after)

            def dve(step, *after):
                return flow.put("dve", step, *after)

            def pool(step, *after):
                return flow.put("pool", step, *after)

            load_x, load_c = Done(("x", k), 16), Done(("ctx", k), 48)
            stored = Done(("out", k), 16)
            marks = {}

            def rstd(ve, eps_div, n, *after):
                t1_, w1 = smalls.take()
                y_, w2 = smalls.take()
                t1, y = t1_[:, 0:n], y_[:, 0:n]
                m = dve(lambda e: e.memset(t1, -0.5), w1, w2, *after)
                a = dve(lambda e: e.tensor_scalar(ve, ve, eps_div[0], eps_div[1], ALU.mult, ALU.add))
                p = pool(lambda e: e.tensor_tensor(y, ve, t1, ALU.pow), a, m)
                c = dve(lambda e: e.scalar_tensor_tensor(t1, y, -0.5, y, ALU.mult, ALU.mult), p)
                c = dve(lambda e: e.tensor_tensor(t1, t1, ve, ALU.mult), c)
                c = dve(lambda e: e.scalar_tensor_tensor(ve, t1, 1.5, y, ALU.add, ALU.mult), c)
                smalls.give(t1_, c)
                smalls.give(y_, c)
                return c

            def layernorm(src, dst, *after):
                st_, w1 = smalls.take()
                mv_, w2 = smalls.take()
                st, mv = b3(st_[:, 0:6 * G]), mv_[:, 0:2 * G].rearrange("p (b c) -> p b c", c=2)
                s3, d3 = b3(src), b3(dst)
                for b in range(G):
                    t = dve(lambda e, b=b: e.bn_stats(st[:, b, :], s3[:, b, :]), *after, w1, w2)
                dve(lambda e: e.memset(st_[:, 28:32], 1.0), t)
                for b in range(G):
                    t2 = dve(lambda e, b=b: e.bn_aggr(mv[:, b, :], st[:, b, :]))
                t3 = rstd(mv[:, :, 1], (1.0, LN_EPS), G, t2)
                for b in range(G):
                    t4 = dve(lambda e, b=b: e.tensor_scalar(d3[:, b, :], s3[:, b, :], mv[:, b, 0:1], mv[:, b, 1:2],
                                                            ALU.subtract, ALU.mult), t3)
                smalls.give(st_, t4)
                smalls.give(mv_, t4)
                return t4

            def turn(src, dst, *after):
                bank, was = banks.take()

                def step(e):
                    for b in range(G):
                        r = e.transpose(bank[:, b * 128:(b + 1) * 128], src[:, b * 128:(b + 1) * 128], ident)
                    return r
                t = pe(step, *after, was)
                t = act(lambda e: e.activation(dst, bank[:, 0:T], ACT.Copy), t)
                banks.give(bank, t)
                return t

            def gated_add(layer, bank, *after):
                t = dve(lambda e: e.scalar_tensor_tensor(x[:, :], bank[:, 0:T], tg[:, layer:layer + 1], x[:, :],
                                                         ALU.mult, ALU.add), *after)
                banks.give(bank, t)
                return t

            def project(weight, src, *after):
                bank, was = banks.take()
                return bank, pe(lambda e: e.matmul(bank[:, 0:T], weight, src, start=True, stop=True), *after, was)

            def attend(n, maps, scores, clamp, values, between=None):
                live = {}
                cols = maps * 128

                def start(u):
                    bank, was = banks.take()
                    nm, was_m = shifts.take()
                    P, was_P = Ps.take()
                    t = scores(u, bank, was)
                    t = dve(lambda e: e.tensor_reduce(nm[:, 0:maps], b3(bank[:, 0:cols], maps), AX.X, ALU.max,
                                                      negate=True), t, was_m)
                    if clamp:
                        t = dve(lambda e: e.tensor_scalar(nm[:, 0:maps], nm[:, 0:maps], -NEG / 10, None, ALU.min),
                                t)

                    def step(e):
                        for j in range(maps):
                            c = slice(j * 128, (j + 1) * 128)
                            r = e.activation(P[:, c], bank[:, c], ACT.Exp, bias=nm[:, j:j + 1])
                        return r
                    t = act(step, t, was_P)
                    shifts.give(nm, t)
                    banks.give(bank, t)
                    live[u] = P, t

                def turn_map(u):
                    P, t = live[u]
                    bank, was = banks.take()
                    PT, was_PT = PTs.take()

                    def step(e):
                        for j in range(maps):
                            r = e.transpose(bank[:, j * 128:(j + 1) * 128], P[:, j * 128:(j + 1) * 128], ident)
                        return r
                    t = pe(step, t, was)
                    Ps.give(P, t)
                    t = act(lambda e: e.activation(PT[:, 0:cols], bank[:, 0:cols], ACT.Copy), t, was_PT)
                    banks.give(bank, t)
                    live[u] = PT, t

                def finish(u):
                    PT, t = live.pop(u)
                    PTs.give(PT, values(u, PT, t))

                for s in range(n + 2):
                    if s < n:
                        start(s)
                    if 0 <= s - 1 < n:
                        turn_map(s - 1)
                    if 0 <= s - 2 < n:
                        finish(s - 2)
                    if between and s < n:
                        between(s)

            def small_head_attention(layer, wq, bq, wk, bk, wv, bv, wo, bo, mask, clamp, t_mask, t_x):
                t_n = layernorm(x[:, :], xn[:, :], t_x)
                kb, t_k = project(w(wk), ctxT[:, :], t_x)
                kT_, was = tmps.take()
                kT = kT_[:, 0:T]
                t_k = act(lambda e: e.activation(kT, kb[:, 0:T], ACT.Identity, bias=0.0 if bk is None else bk), t_k, was)
                banks.give(kb, t_k)
                km = qk[:, :].rearrange("p (b h t) -> p b h t", b=G, h=H)
                t_km = []
                for r in range(H // HQ):
                    def keep(e, r=r):
                        for h in range(HQ * r, HQ * r + HQ):
                            m = e.tensor_scalar(km[:, :, h, :], b3(kT), w("head16", h, h + 1), None, ALU.mult)
                        return m
                    t_km.append(dve(keep, t_k))
                tmps.give(kT_, t_km)
                t_nT = turn(xn, xnT[:, :], t_n)
                qT = gs[:, 0:T]
                vb, was = banks.take()

                def v_step(e):
                    for b in range(G):
                        o = vb[:, b * 128:(b + 1) * 128]
                        r = e.matmul(o, ctxT[:, b * 128:(b + 1) * 128], w(wv), start=True, stop=bv is None)
                        if bv is not None:
                            r = add_bias(e, o, bv)
                    return r
                t_v = pe(v_step, was, t_x)
                v4 = va[:, 0:G * H * (DH + 1)].rearrange("p (b h d) -> p b h d", b=G, h=H)
                t_va = [dve(lambda e: e.memset(v4[:, :, :, DH], 1.0), t_x),
                        dve(lambda e: e.tensor_copy(v4[:, :, :, 0:DH].rearrange("p b h d -> p (b h) d"),
                                                    vb[:, 0:T].rearrange("p (n d) -> p n d", d=DH)), t_v)]
                banks.give(vb, t_va)
                qb, t_q = project(w(wq), xnT[:, :], t_nT)
                t_qT = act(lambda e: e.activation(qT, qb[:, 0:T], ACT.Identity, scale=DH ** -0.5,
                                                        bias=0.0 if bq is None else bq), t_q)
                banks.give(qb, t_qT)

                def scores(u, bank, was):
                    b, r = divmod(u, 4)

                    def step(e):
                        e.matmul(bank, qT[:, b * 128:(b + 1) * 128], km[:, b, HQ * r:HQ * r + HQ, :], start=True, stop=False,
                                 skip_group_check=True)
                        return e.matmul(bank, identb[:, :], bc(mask(b), 1, HQ), start=False, stop=True,
                                        skip_group_check=True)
                    return pe(step, t_qT, t_km[r], t_mask, was)

                per = {}
                y_bank = {}

                def values(u, PT, t):
                    b, r = divmod(u, 4)
                    if r == 0:
                        per["O"], per["was"] = banks.take()
                    O = per["O"]

                    def step(e):
                        for j in range(HQ):
                            h = HQ * r + j
                            m = e.matmul(O[:, h * 9:h * 9 + 9], PT[:, j * 128:(j + 1) * 128], v4[:, b, h, :],
                                         start=True, stop=True)
                        return m
                    t_pv = pe(step, t, t_va, per["was"])
                    if r == 3:
                        o3 = O[:, 0:H * 9].rearrange("p (h d) -> p h d", h=H)
                        rec, was = smalls.take()
                        t1 = dve(lambda e: e.reciprocal(rec[:, 0:H], o3[:, :, DH]), t_pv, was)
                        on = oa[:, b * 128:(b + 1) * 128].rearrange("p (h d) -> p h d", h=H)
                        t2 = dve(lambda e: e.tensor_tensor(on, o3[:, :, 0:DH], bc(rec[:, 0:H], 2, DH), ALU.mult), t1)
                        smalls.give(rec, t2)
                        banks.give(O, t2)
                        y_bank["t"] = t2
                    return t_pv

                attend(G * H // HQ, HQ, scores, clamp, values)
                t_oT = turn(oa, oT[:, :], y_bank["t"])
                yb, was = banks.take()

                def y_step(e):
                    for b in range(G):
                        o = yb[:, b * 128:(b + 1) * 128]
                        e.matmul(o, oT[:, b * 128:(b + 1) * 128], w(wo), start=True, stop=False)
                        r = add_bias(e, o, bo)
                    return r
                return gated_add(layer, yb, pe(y_step, t_oT, was))

            def top(src, work1, work2, mask, n, width, k, rev, *after, meanwhile=None):
                meanwhile = meanwhile or (lambda: None)
                s3 = src.rearrange("p (n e) -> p n e", e=width)
                a3 = work1.rearrange("p (n e) -> p n e", e=width)
                r_, wr = tops.take()
                r = r_[:, 0:n]
                cur, t = s3, list(after) + [wr]
                cur_flat = src
                for i in range(k):
                    t1 = dve(lambda e, c=cur: e.tensor_reduce(r, c, AX.X, ALU.max), t)
                    t2 = dve(lambda e, c=cur: e.tensor_tensor(a3, c, bc(r, 2, width), ALU.is_equal), t1)
                    meanwhile()
                    t3 = dve(lambda e: e.tensor_tensor(a3, a3, bc(rev, 1, n), ALU.mult), t2)
                    t4 = dve(lambda e: e.tensor_reduce(r, a3, AX.X, ALU.max), t3)
                    meanwhile()
                    t5 = dve(lambda e: e.tensor_tensor(a3, a3, bc(r, 2, width), ALU.is_equal), t4)
                    if i < k - 1:
                        t = dve(lambda e, c=cur_flat: e.scalar_tensor_tensor(work2, work1, -3.0e38, c, ALU.mult, ALU.add), t5)
                    if i == 0:
                        t_m = dve(lambda e: e.tensor_copy(mask, work1), t5)
                    else:
                        t_m = dve(lambda e: e.tensor_tensor(mask, mask, work1, ALU.add), t5)
                    t = [t, t_m]
                    cur, cur_flat = work2.rearrange("p (n e) -> p n e", e=width), work2
                tops.give(r_, t_m)
                return t_m

            def attention0(t_x):
                t_m = marks["mask"] = dve(lambda e: e.tensor_scalar(mb0[:, :], m_ld[:, :], 0.0, NEG,
                                                                    ALU.is_equal, ALU.mult), load_c)
                return small_head_attention(0, "wq0", None, "wk0", None, "wv0", None, "wo0", "bo0",
                                            lambda b: mb0[:, b * 128:(b + 1) * 128], True, t_m, [t_x, load_x, load_c])

            def widen(sel, gT, *after):
                bank, was = banks.take()
                return bank, pe(lambda e: e.matmul(bank[:, 0:T], sel, gT, start=True, stop=True), *after, was)

            def turn_gates(src, width, *after):
                n = 3 * width
                parts = b3(gpart[:, :])[:, :, 0:n].rearrange("p b (k e) -> p b k e", k=3)
                s3 = src.rearrange("p (b e) -> p b e", b=G)
                t = after
                for i in range(3):
                    t = dve(lambda e, i=i: e.tensor_copy(parts[:, :, i, :], s3), t)
                    if i < 2:
                        t = dve(lambda e, i=i: e.tensor_tensor(s3, s3, parts[:, :, i, :], ALU.subtract), t)
                bank, was = banks.take()
                bb = bank[:, 0:T // 2].bitcast(BF16)

                def step(e):
                    for b in range(G):
                        c = slice(b * 128, (b + 1) * 128)
                        r = e.transpose(bb[:, c], gpart[:, c], identb[:, :])
                    return r
                t = pe(step, t, was)
                t = act(lambda e: e.activation(gateT[0:n, :], bb[0:n, :], ACT.Copy), t)
                banks.give(bank, t)
                return t

            def sum_tiles(layer, tiles, hT, weight, *after):
                yb, was = banks.take()

                def step(e):
                    for b in range(G):
                        for n in range(tiles):
                            r = e.matmul(yb[:, b * 128:(b + 1) * 128], hT[:, n * T + b * 128:n * T + (b + 1) * 128],
                                         w(weight, n * 128, (n + 1) * 128), start=(n == 0), stop=(n == tiles - 1))
                    return r
                return gated_add(layer, yb, pe(step, *after, was))

            def mixture0(t_x):
                t_n = layernorm(x[:, :], xn[:, :], t_x)
                t_nT = turn(xn, xnT[:, :], t_n)
                lb, was = banks.take()

                def l_step(e):
                    for b in range(G):
                        r = e.matmul(lb[:, b * E0:(b + 1) * E0], xnT[:, b * 128:(b + 1) * 128], w("gw0"),
                                     start=True, stop=True)
                    return r
                t_l = pe(l_step, t_nT, was)
                ne = G * E0
                l3 = lb[:, 0:ne].rearrange("p (b e) -> p b e", b=G)
                sc, sb_ = gs[:, 0:ne], gs[:, ne:2 * ne]
                sc3, sb3 = (a.rearrange("p (b e) -> p b e", b=G) for a in (sc, sb_))
                experts, t_h = list(range(E0 + F0)), {}

                def hidden():
                    if not experts:
                        return
                    n = experts.pop(0)
                    a_, t_a = project(w("w1_0", n * 128, (n + 1) * 128), xnT[:, :], t_nT)
                    c_, t_c = project(w("w3_0", n * 128, (n + 1) * 128), xnT[:, :], t_nT)
                    th_, was = tmps.take()
                    a, c, th = a_[:, 0:T], c_[:, 0:T], th_[:, 0:T]
                    t = act(lambda e: e.activation(th, a, ACT.Tanh, scale=0.5), t_a, was)
                    t = dve(lambda e: e.scalar_tensor_tensor(th, th, 1.0, a, ALU.add, ALU.mult), t)
                    banks.give(a_, t)
                    h = qk[:, n * T:(n + 1) * T]
                    t = dve(lambda e: e.scalar_tensor_tensor(h, th, 0.5 if n >= E0 else 1.0, c, ALU.mult, ALU.mult), t, t_c)
                    banks.give(c_, t)
                    tmps.give(th_, t)
                    t_h[n] = t

                mx, was = smalls.take()
                t = dve(lambda e: e.tensor_reduce(mx[:, 0:G], l3, AX.X, ALU.max), t_l, was)
                t = dve(lambda e: e.tensor_tensor(sc3, l3, bc(mx[:, 0:G], 2, E0), ALU.subtract), t)
                banks.give(lb, t)
                t = act(lambda e: e.activation(sc, sc, ACT.Exp), t)
                hidden()
                t = dve(lambda e: e.tensor_reduce(mx[:, 0:G], sc3, AX.X, ALU.add), t)
                hidden()
                t = dve(lambda e: e.reciprocal(mx[:, 0:G], mx[:, 0:G]), t)
                hidden()
                t = dve(lambda e: e.tensor_tensor(sc3, sc3, bc(mx[:, 0:G], 2, E0), ALU.mult), t)
                hidden()
                smalls.give(mx, t)
                t = dve(lambda e: e.tensor_tensor(sb3, sc3, bc(w("gb0"), 1, G), ALU.add), t)
                t = top(sb_, gw1_[:, 0:ne], gw2_[:, 0:ne], gm[:, 0:ne], G, E0, 2, w("rev8"), t,
                        meanwhile=hidden)
                t = dve(lambda e: e.scalar_tensor_tensor(sc, sc, 0.5, gm[:, 0:ne], ALU.mult, ALU.mult), t)
                t_g = turn_gates(sc, E0, t)
                while experts:
                    hidden()
                for n in range(E0):
                    h = qk[:, n * T:(n + 1) * T]
                    g_, t_w = widen(pick0b[0:3 * E0, n:n + 1].broadcast_to((3 * E0, 128)), gateT[0:3 * E0, :], t_g)
                    t_h[n] = dve(lambda e, g=g_[:, 0:T], h=h: e.tensor_tensor(h, h, g, ALU.mult), t_h[n], t_w)
                    banks.give(g_, t_h[n])
                t_h = list(t_h.values())
                return sum_tiles(4, E0 + F0, qk, "w2_0", t_h)

            def attention1(t_x):
                return small_head_attention(1, "wq1", bq1s[:, 0:1], "wk1", w("bk1"), "wv1", "bv1", "wo1", "bo1",
                                            lambda b: mb1[:, :], False, None, t_x)

            def switched_attention(t_x):
                t_n = layernorm(x[:, :], xn[:, :], t_x)
                t_nT = turn(xn, xnT[:, :], t_n)
                NGATE = 2 * H * E1
                for half in range(G // 2):
                    gb, was = banks.take()

                    def g_step(e, gb=gb, half=half):
                        for i in range(2):
                            b = 2 * half + i
                            r = e.matmul(gb[:, i * NGATE:(i + 1) * NGATE], xnT[:, b * 128:(b + 1) * 128], w("sg1"),
                                         start=True, stop=True)
                        return r
                    t = pe(g_step, t_nT, was)
                    t_g = act(lambda e, gb=gb, half=half: e.activation(gs[:, half * 512:half * 512 + 512], gb, ACT.Copy), t)
                    banks.give(gb, t_g)
                for b in range(G):
                    pb_, was = banks.take()
                    t = pe(lambda e, b=b, o=pb_: e.matmul(o, xnT[:, b * 128:(b + 1) * 128], w("sv1"), start=True, stop=True),
                           t_nT, was)
                    t_pv = act(lambda e, b=b, o=pb_: e.activation(pv1[:, b * 512:(b + 1) * 512], o, ACT.Copy, scale=0.5), t)
                    banks.give(pb_, t_pv)
                t_top = top(gs[:, :], gw1_[:, :], gw2_[:, :], gm[:, :], 2 * G * H, E1, 2, w("rev8"), t_g)
                t = act(lambda e: e.activation(gt[:, :], gs[:, :], ACT.Tanh, scale=0.5), t_g)
                t_mix = dve(lambda e: e.scalar_tensor_tensor(gt[:, :], gt[:, :], 1.0, gm[:, :], ALU.add, ALU.mult), t, t_top)
                mix = gt[:, :].rearrange("p (b s h e) -> p b s h e", b=G, s=2, h=H)
                sel = gm[:, :].rearrange("p (b s h e) -> p b s h e", b=G, s=2, h=H)
                t_qk = []
                for n in range(8):
                    for wn, dst in (("sq1", qA), ("sk1", kA)):
                        bank, t = project(w(wn, n * 128, (n + 1) * 128), xnT[:, :], t_nT)
                        t = act(lambda e, n=n, dst=dst, bank=bank: e.activation(
                            dst[:, n * T:(n + 1) * T], bank[:, 0:T], ACT.Copy, scale=D1 ** -0.5 if dst is qA else 1.0), t)
                        banks.give(bank, t)
                        t_qk.append(t)
                v4 = va[:, :].rearrange("p (b h d) -> p b h d", b=G, h=H)
                t_one = dve(lambda e: e.memset(v4[:, :, :, D1], 1.0), t_x)
                t_v = {b: [] for b in range(G)}
                pending, made = [], [0]

                def flush(lag):
                    while len(pending) > lag:
                        pr, p4, out_, t, mark, sink = pending.pop(0)
                        mark = dve(lambda e, o=out_, p4=p4: e.tensor_reduce(o, p4, AX.X, ALU.add), t, mark)
                        prods.give(pr, mark)
                        sink.append(mark)

                def mixed(out_, in0, in1, shape, sink, out_free, *after):
                    flush(min(LAG, len(prods.free) + len(pending) - 1))
                    pr, was = prods.take()
                    p4 = pr.rearrange(*shape[0], **shape[1])
                    who = dict(dve=dve, pool=pool)[MIXERS[made[0] % len(MIXERS)]]
                    made[0] += 1
                    t = who(lambda e: e.tensor_tensor(p4, in0, in1, ALU.mult), *after, was)
                    pending.append((pr, p4, out_, t, out_free, sink))

                pv4 = pv1[:, :].rearrange("p (b e d) -> p b d e", b=G, e=E1)

                def mix_values(b, h):
                    mixed(v4[:, b, h:h + 2, 0:D1], bc(mix[:, b, 0, h:h + 2, :], 2, D1),
                          bc(pv4[:, b, :, :], 1, 2), (("p (h d e) -> p h d e",), dict(h=2, e=E1)), t_v[b], None,
                          t_mix, t_pv)

                o4 = oa[:, :].rearrange("p (b h d) -> p b d h", b=G, h=H)
                t_o = {b: [] for b in range(G)}
                U = mixed1[:, :]
                u3 = U.rearrange("p (e d) -> p e d", e=E1)
                t_u = []
                t_U = []
                uT = pv1[:, :]
                t_uT = []

                def mix_outputs(b, ex):
                    mixed(u3[:, ex, :], o4[:, b, :, :], bc(sel[:, b, 1, :, ex], 1, D1),
                          (("p (d h) -> p d h",), dict(h=H)), t_U, t_u, t_o[b])

                def turn_outputs(b):
                    flush(0)
                    bank, was = banks.take()

                    def step(e):
                        for n in range(4):
                            r = e.transpose(bank[:, n * 128:(n + 1) * 128], U[:, n * 128:(n + 1) * 128], ident)
                        return r
                    t_u[:] = [pe(step, t_U, was)]
                    t = act(lambda e: e.activation(uT[:, b * 512:(b + 1) * 512], bank, ACT.Copy), t_u, [t_v[i] for i in range(G)])
                    banks.give(bank, t)
                    t_uT.append(t)

                def scores(u, bank, was):
                    b, g = divmod(u, 4)
                    rows = slice(64 * (g % 2), 64 * (g % 2) + 64)

                    def step(e):
                        for j in range(HQ):
                            c = (HQ * (g // 2) + j) * T + b * 128
                            r = e.matmul(bank[:, j * 128:(j + 1) * 128], qA[rows, c:c + 128], kA[rows, c:c + 128],
                                         start=(j == 0), stop=True, skip_group_check=True)
                        return r
                    return pe(step, t_qk, was)

                def values(u, PT, t):
                    b, g = divmod(u, 4)
                    O, was = banks.take()

                    def step(e):
                        for j in range(HQ):
                            r = e.matmul(O[:, j * 65:j * 65 + 65], PT[:, j * 128:(j + 1) * 128], v4[:, b, 8 * (g // 2) + 2 * j + g % 2, :],
                                         start=True, stop=True)
                        return r
                    assert len(t_v[b]) >= 4 * (g // 2 + 1)
                    t_p = pe(step, t, t_one, t_v[b][:4 * (g // 2 + 1)], was)
                    o3 = O[:, 0:HQ * 65].rearrange("p (h d) -> p h d", h=HQ)
                    rec, was = smalls.take()
                    t1 = dve(lambda e: e.reciprocal(rec[:, 0:HQ], o3[:, :, D1]), t_p, was)
                    dst = oa[:, :].rearrange("p (b g j r d) -> p b g j r d", b=G, g=2, j=HQ, r=2)[:, b, g // 2, :, g % 2, :]
                    m4 = gm[:, :].rearrange("p (b s g j r e) -> p b s g j r e", b=G, s=2, g=2, j=HQ, r=2)[:, b, 1, g // 2, :, g % 2, :]
                    t2 = act(lambda e: e.activation(dst, o3[:, :, 0:D1], ACT.Copy), t1)
                    t1 = dve(lambda e: e.tensor_tensor(m4, m4, bc(rec[:, 0:HQ], 2, E1), ALU.mult), t1, t_top)
                    smalls.give(rec, t1)
                    banks.give(O, t1, t2)
                    t_o[b] += [t1, t2]
                    return t_p

                extra = mixed1_gs[:, 0:1024]
                prods.give(extra, t_mix)
                for h in range(0, H, 2):
                    mix_values(0, h)
                    if h == 6 or h == 14:
                        flush(0)

                def between(s):
                    b, g = divmod(s - OUT_AFTER, 4)
                    if s < 4 * (G - 1):
                        mix_values(s // 4 + 1, s % 4 * 4)
                        mix_values(s // 4 + 1, s % 4 * 4 + 2)
                        if s + 1 == 4 * (G - 1):
                            flush(0)
                            prods.free[:] = [(pr, t) for pr, t in prods.free if pr is not extra]
                    elif b >= 0:
                        mix_outputs(b, 2 * g)
                        mix_outputs(b, 2 * g + 1)
                        if g == 3:
                            turn_outputs(b)

                attend(G * H // HQ, HQ, scores, False, values, between)
                more = [P_mem[:, :], PT_mem[:, :]]
                for mem, ring in zip(more, (Ps, PTs)):
                    prods.give(mem, [t for _, t in ring.free])
                for s in range(4 * G - OUT_AFTER, 4 * G):
                    b, g = divmod(s, 4)
                    mix_outputs(b, 2 * g)
                    mix_outputs(b, 2 * g + 1)
                    if g == 3:
                        turn_outputs(b)
                for mem, ring in zip(more, (Ps, PTs)):
                    t = [t for pr, t in prods.free if pr is mem]
                    ring.free[:] = [(half, tuple(flat([t, was]))) for half, was in ring.free]
                prods.free[:] = [(pr, t) for pr, t in prods.free if all(pr is not mem for mem in more)]
                yb, was = banks.take()

                def y_step(e):
                    for b in range(G):
                        for n in range(4):
                            r = e.matmul(yb[:, b * 128:(b + 1) * 128], uT[:, b * 512 + n * 128:b * 512 + (n + 1) * 128],
                                         w("so1", n * 128, (n + 1) * 128), start=(n == 0), stop=(n == 3))
                    return r
                return gated_add(5, yb, pe(y_step, t_uT, was))

            def mlstm(t_x):
                t_n = layernorm(x[:, :], xn[:, :], t_x)
                t_nT = turn(xn, xnT[:, :], t_n)
                gb, was = banks.take()
                NGK = 2 * NH2

                def g_step(e):
                    for b in range(G):
                        o = gb[:, b * NGK:(b + 1) * NGK]
                        e.matmul(o, xnT[:, b * 128:(b + 1) * 128], w("gk2", 0, NGK), start=True, stop=False)
                        for part in (1, 2):
                            e.matmul(o, ctxT[:, b * 128:(b + 1) * 128], w("gk2", part * NGK, (part + 1) * NGK),
                                     start=False, stop=False)
                        r = e.matmul(o, ones[0:1, :], w("gb2")[0:1, :], start=False, stop=True)
                    return r
                t_g = pe(g_step, t_nT, was)
                n = G * NH2
                g4 = gb[:, 0:G * NGK].rearrange("p (b k h) -> p b k h", b=G, k=2)
                ab, lf, ig, cum, av, mneg = (gs[:, i * n:(i + 1) * n] for i in range(6))
                v3 = {k: a.rearrange("p (b h) -> p b h", b=G) for k, a in
                      dict(ab=ab, lf=lf, ig=ig, cum=cum, av=av).items()}
                t = act(lambda e: e.activation(v3["ab"], g4[:, :, 1, :], ACT.Abs), t_g)
                t = act(lambda e: e.activation(ab, ab, ACT.Exp, scale=-1.0), t)
                t_s = act(lambda e: e.activation(ab, ab, ACT.Ln, bias=1.0), t)
                t = dve(lambda e: e.tensor_copy(v3["ig"], g4[:, :, 0, :]), t_g, t_s)
                t = dve(lambda e: e.tensor_scalar(v3["lf"], g4[:, :, 1, :], 0.0, None, ALU.min), t)
                banks.give(gb, t)
                t = dve(lambda e: e.tensor_tensor(lf, lf, ab, ALU.subtract), t, t_s)
                cb, was = banks.take()
                t = pe(lambda e: e.matmul(cb[:, 0:n], w("triu"), lf, start=True, stop=True), t, was)
                t = dve(lambda e: e.tensor_copy(cum, cb[:, 0:n]), t)
                banks.give(cb, t)
                t_a = dve(lambda e: e.tensor_tensor(av, ig, cum, ALU.subtract), t)
                v4 = va[:, 0:G * NH2 * (DH2 + 1)].rearrange("p (b h d) -> p b h d", b=G, h=NH2)
                t_va = [dve(lambda e: e.memset(v4[:, :, :, DH2], 1.0), t_x),
                        act(lambda e: e.activation(v4[:, :, :, 0:DH2].rearrange("p b h d -> p (b h) d"),
                                                   ctxN[:, :].rearrange("p (n d) -> p n d", d=DH2), ACT.Copy), t_x)]
                hn = oa[:, 0:T]
                t_h = []
                live = {}

                def decay(h):
                    m = live[h] = {}
                    dg, was = tmps.take()
                    for b in range(G):
                        t = dve(lambda e, b=b: e.tensor_scalar(dg[:, b * 128:(b + 1) * 128], ident,
                                                               av[:, b * NH2 + h:b * NH2 + h + 1], None, ALU.mult), t_a, was)
                    A_, was = banks.take()
                    A = A_[:, 0:T]

                    def a_step(e):
                        e.matmul(A, ones[:, :], dg[:, 0:T], start=True, stop=False, skip_group_check=True)
                        return e.matmul(A, identb[:, :], bc(causb[:, :], 1, G), start=False, stop=True,
                                        skip_group_check=True)
                    t = pe(a_step, t, was)
                    tmps.give(dg, t)
                    nm = mneg[:, h * G:(h + 1) * G]
                    t = dve(lambda e: e.tensor_reduce(nm, b3(A), AX.X, ALU.max, negate=True), t)
                    m.update(A=A_, t=t, nm=nm)

                def decay2(h):
                    m = live[h]
                    A_, nm = m["A"], m["nm"]
                    A = A_[:, 0:T]
                    Pd, was = Ps.take()

                    def e_step(e):
                        for b in range(G):
                            c = slice(b * 128, (b + 1) * 128)
                            r = e.activation(Pd[:, c], A[:, c], ACT.Exp, bias=nm[:, b:b + 1])
                        return r
                    t_D = act(e_step, m["t"], was)
                    banks.give(A_, t_D)
                    Q, was = banks.take()

                    def q_step(e):
                        rows = slice(32 * h, 32 * h + 32)
                        for b in range(G):
                            r = e.matmul(Q[:, b * 128:(b + 1) * 128], xnT[rows, b * 128:(b + 1) * 128],
                                         ctxT[rows, b * 128:(b + 1) * 128], start=True, stop=True)
                        return r
                    t = pe(q_step, t_nT, was)
                    t = dve(lambda e: e.scalar_tensor_tensor(Pd[:, 0:T], Q[:, 0:T], DH2 ** -0.5, Pd[:, 0:T], ALU.mult, ALU.mult), t, t_D)
                    banks.give(Q, t)
                    m.update(P=Pd, t=t)

                def weigh(h):
                    m = live.pop(h)
                    Pd = m["P"]
                    bank, was = banks.take()

                    def t_step(e):
                        for b in range(G):
                            r = e.transpose(bank[:, b * 128:(b + 1) * 128], Pd[:, b * 128:(b + 1) * 128], ident)
                        return r
                    t = pe(t_step, m["t"], was)
                    Ps.give(Pd, t)
                    PT, was = PTs.take()
                    t = act(lambda e: e.activation(PT[:, 0:T], bank[:, 0:T], ACT.Copy), t, was)
                    banks.give(bank, t)
                    O, was = banks.take()

                    def o_step(e):
                        for b in range(G):
                            r = e.matmul(O[:, b * 33:b * 33 + 33], PT[:, b * 128:(b + 1) * 128], v4[:, b, h, :],
                                         start=True, stop=True)
                        return r
                    t = pe(o_step, t, t_va, was)
                    PTs.give(PT, t)
                    o3 = O[:, 0:G * 33].rearrange("p (b d) -> p b d", b=G)
                    nr, was = smalls.take()
                    e4, s4 = nr[:, 0:G], nr[:, G:2 * G]
                    cu = v3["cum"][:, :, h]
                    t1 = dve(lambda e: e.tensor_tensor(e4, m["nm"], cu, ALU.subtract), was)
                    t1 = act(lambda e: e.activation(e4, e4, ACT.Exp), t1)
                    t2 = dve(lambda e: e.tensor_scalar(s4, o3[:, :, DH2], -1.0, None, ALU.mult), t)
                    t2 = dve(lambda e: e.tensor_tensor(s4, s4, o3[:, :, DH2], ALU.max), t2)
                    t2 = dve(lambda e: e.tensor_tensor(s4, s4, e4, ALU.max), t2, t1)
                    t2 = dve(lambda e: e.tensor_scalar(s4, s4, 1e-6, None, ALU.add), t2)
                    t2 = dve(lambda e: e.reciprocal(s4, s4), t2)
                    t2 = dve(lambda e: e.tensor_tensor(hn.rearrange("p (b h d) -> p b h d", b=G, h=NH2)[:, :, h, :],
                                                       o3[:, :, 0:DH2], bc(s4, 2, DH2), ALU.mult), t2)
                    smalls.give(nr, t2)
                    banks.give(O, t2)
                    t_h.append(t2)

                for s in range(NH2 + 2):
                    if s < NH2:
                        decay(s)
                    if 0 <= s - 1 < NH2:
                        decay2(s - 1)
                    if 0 <= s - 2 < NH2:
                        weigh(s - 2)
                h3 = hn.rearrange("p (n d) -> p n d", d=DH2)
                mn, was = smalls.take()
                vr, was2 = smalls.take()
                sq_, was3 = tmps.take()
                sq = sq_[:, 0:T]
                t = dve(lambda e: e.tensor_reduce(mn[:, 0:n], h3, AX.X, ALU.add), t_h, was, was2, was3)
                t = dve(lambda e: e.tensor_scalar(mn[:, 0:n], mn[:, 0:n], 1.0 / DH2, None, ALU.mult), t)
                t = dve(lambda e: e.tensor_tensor(h3, h3, bc(mn[:, 0:n], 2, DH2), ALU.subtract), t)
                t = dve(lambda e: e.tensor_tensor(sq, hn, hn, ALU.mult), t)
                t = dve(lambda e: e.tensor_reduce(vr[:, 0:n], sq.rearrange("p (n d) -> p n d", d=DH2), AX.X, ALU.add), t)
                tmps.give(sq_, t)
                t = rstd(vr[:, 0:n], (1.0 / DH2, 1e-6), n, t)
                t = dve(lambda e: e.tensor_tensor(h3, h3, bc(vr[:, 0:n], 2, DH2), ALU.mult), t)
                smalls.give(mn, t)
                smalls.give(vr, t)
                t = dve(lambda e: e.tensor_tensor(b3(hn), b3(hn), bc(w("nw2"), 1, G), ALU.mult), t)
                return dve(lambda e: e.scalar_tensor_tensor(x[:, :], hn, tg[:, 2:3], x[:, :], ALU.mult, ALU.add), t)

            def conv_ffn(t_x):
                q3 = xqT.rearrange("p (b t) -> p b t", t=130)
                t_pad = dve(lambda e: e.memset(q3[:, :, 0:130:129], 0.0), t_x)
                t_n = layernorm(x[:, :], xn[:, :], t_x)
                am_, was = smalls.take()
                am, sc = am_[:, 0:G], am_[:, G:2 * G]
                t = dve(lambda e: e.tensor_reduce(am, b3(xn[:, :]), AX.X, ALU.max, apply_absolute_value=True), t_n, was)
                t = dve(lambda e: e.tensor_scalar(am, am, 1e-5, 1.0 / 127.0, ALU.max, ALU.mult), t)
                t = dve(lambda e: e.reciprocal(sc, am), t)
                x3 = b3(xn[:, :])
                for b in range(G):
                    t1 = dve(lambda e, b=b: e.tensor_scalar(x3[:, b, :], x3[:, b, :], sc[:, b:b + 1], ROUND,
                                                            ALU.mult, ALU.add), t)
                t1 = dve(lambda e: e.tensor_scalar(xn[:, :], xn[:, :], ROUND, 127.0, ALU.subtract, ALU.min), t1)
                for b in range(G):
                    t2 = dve(lambda e, b=b: e.tensor_scalar(x3[:, b, :], x3[:, b, :], -128.0, am[:, b:b + 1],
                                                            ALU.max, ALU.mult), t1)
                smalls.give(am_, t2)
                bank, was = banks.take()

                def t_step(e):
                    for b in range(G):
                        r = e.transpose(bank[:, b * 128:(b + 1) * 128], xn[:, b * 128:(b + 1) * 128], ident)
                    return r
                t = pe(t_step, t2, was)
                t_q = act(lambda e: e.activation(q3[:, :, 1:129], b3(bank[:, 0:T]), ACT.Copy), t)
                banks.give(bank, t_q)
                yb, yw = banks.take()
                live = {}
                h2 = oa[:, 0:G * F2]
                sc2_, was_s = smalls.take()
                t_y = []

                def hidden(b):
                    hb, was = banks.take()

                    def step(e):
                        for k in range(3):
                            e.matmul(hb, q3[:, b, k:k + 128], wconv[:, k * F2:(k + 1) * F2], start=(k == 0), stop=False)
                        return add_bias(e, hb, "convb")
                    t = pe(step, t_q, t_pad, was)
                    h = h2[:, b * F2:(b + 1) * F2]
                    th, was = tmps.take()
                    t = act(lambda e: e.activation(th, hb, ACT.Tanh, scale=0.5), t, was)
                    t = dve(lambda e: e.scalar_tensor_tensor(h, th, 1.0, hb, ALU.add, ALU.mult), t)
                    banks.give(hb, t)
                    tmps.give(th, t)
                    a, s, o = (sc2_[:, k * G + b:k * G + b + 1] for k in range(3))
                    t = dve(lambda e: e.tensor_reduce(a, h, AX.X, ALU.max, apply_absolute_value=True), t, was_s)
                    t = dve(lambda e: e.tensor_scalar(a, a, 2e-5, 1.0 / 127.0, ALU.max, ALU.mult), t)
                    t = dve(lambda e: e.reciprocal(s, a), t)
                    live[b, "o"] = dve(lambda e: e.tensor_scalar(o, a, wstat[:, 7:8], None, ALU.mult), t)
                    t = dve(lambda e: e.tensor_scalar(h, h, s, ROUND, ALU.mult, ALU.add), t)
                    t = dve(lambda e: e.tensor_scalar(h, h, ROUND, 127.0, ALU.subtract, ALU.min), t)
                    live[b] = dve(lambda e: e.tensor_scalar(r2[:, b * F2:(b + 1) * F2], h, -128.0, None, ALU.max), t)

                def second(b):
                    bank, was = banks.take()
                    bb = bank[:, 0:256].bitcast(BF16)

                    def step(e):
                        for n in range(4):
                            r = e.transpose(bb[:, n * 128:(n + 1) * 128], r2[:, b * F2 + n * 128:b * F2 + (n + 1) * 128],
                                            identb[:, :])
                        return r
                    t = pe(step, live[b], was)
                    t = act(lambda e: e.activation(r2T[:, b * F2:(b + 1) * F2], bb, ACT.Copy), t)
                    banks.give(bank, t)

                    def y_step(e):
                        for n in range(4):
                            r = e.matmul(yb[:, b * 128:(b + 1) * 128], r2T[:, b * F2 + n * 128:b * F2 + (n + 1) * 128],
                                         w2b[:, n * 128:(n + 1) * 128], start=(n == 0), stop=(n == 3))
                        return r
                    t_y.append(pe(y_step, t, yw))

                for s in range(G + 1):
                    if s < G:
                        hidden(s)
                    if s >= 1:
                        second(s - 1)
                xx = b3(x[:, :])
                for b in range(G):
                    t = dve(lambda e, b=b: e.scalar_tensor_tensor(xx[:, b, :], yb[:, b * 128:(b + 1) * 128],
                                                                  sc2_[:, 2 * G + b:2 * G + b + 1], xx[:, b, :],
                                                                  ALU.mult, ALU.add), t_y, live[b, "o"])
                banks.give(yb, t)
                smalls.give(sc2_, t)
                return t

            def wide_attention(t_x):
                t_n = layernorm(x[:, :], xn[:, :], t_x)
                t_nT = turn(xn, xnT[:, :], t_n)
                kb, t = project(w("wk3"), ctxT[:, :], t_x)
                t_kp = t
                t_k = act(lambda e: e.activation(kA[:, 0:T], kb[:, 0:T], ACT.Identity, bias=w("bk3")), t)
                banks.give(kb, t_k)
                qb, t = project(w("wq3"), xnT[:, :], t_nT)
                t_q = act(lambda e: e.activation(qA[:, 0:T], qb[:, 0:T], ACT.Identity, scale=D ** -0.5,
                                                        bias=bq1s[:, 1:2]), t)
                banks.give(qb, t_q)
                vb, was = banks.take()

                def v_step(e):
                    for b in range(G):
                        o = vb[:, b * 128:(b + 1) * 128]
                        e.matmul(o, ctxT[:, b * 128:(b + 1) * 128], w("wv3"), start=True, stop=False)
                        r = add_bias(e, o, "bv3")
                    return r
                t_vp = t = pe(v_step, was)
                v3 = va[:, 0:G * (D + 1)].rearrange("p (b d) -> p b d", b=G)
                t_va = [dve(lambda e: e.memset(v3[:, :, D], 1.0), t_x),
                        dve(lambda e: e.tensor_copy(v3[:, :, 0:D], b3(vb[:, 0:T])), t)]
                banks.give(vb, t_va)

                def scores(u, bank, was):
                    def step(e):
                        for b in range(G):
                            c = slice(b * 128, (b + 1) * 128)
                            r = e.matmul(bank[:, c], qA[:, c], kA[:, c], start=(b == 0), stop=True, skip_group_check=True)
                        return r
                    return pe(step, t_q, t_k, was)

                res = {}

                def values(u, PT, t):
                    t_on = []
                    for half in range(G // 2):
                        O, was = banks.take()

                        def step(e, O=O, half=half):
                            for i in range(2):
                                b = 2 * half + i
                                r = e.matmul(O[:, i * 129:i * 129 + 129], PT[:, b * 128:(b + 1) * 128], v3[:, b, :],
                                             start=True, stop=True)
                            return r
                        t_p = pe(step, t, t_va, was)
                        o3 = O[:, 0:258].rearrange("p (b d) -> p b d", b=2)
                        rec, was = smalls.take()
                        t1 = dve(lambda e, o3=o3, rec=rec: e.reciprocal(rec[:, 0:2], o3[:, :, D]), t_p, was)
                        t2 = dve(lambda e, o3=o3, rec=rec, half=half: e.tensor_tensor(
                            oa[:, half * 256:half * 256 + 256].rearrange("p (b d) -> p b d", b=2), o3[:, :, 0:D],
                            bc(rec[:, 0:2], 2, D), ALU.mult), t1)
                        smalls.give(rec, t2)
                        banks.give(O, t2)
                        t_on.append(t2)
                    res["t"] = t_on
                    return t_p

                attend(1, G, scores, False, values)
                t_oT = turn(oa, oT[:, :], res["t"])
                yb, was = banks.take()

                def y_step(e):
                    for b in range(G):
                        o = yb[:, b * 128:(b + 1) * 128]
                        e.matmul(o, oT[:, b * 128:(b + 1) * 128], w("wo3"), start=True, stop=False)
                        r = add_bias(e, o, "bo3")
                    return r
                t_y = pe(y_step, t_oT, was)
                t = t_cn = dve(lambda e: e.scalar_tensor_tensor(xn[:, :], ctxN[:, :], 2.0, xn[:, :], ALU.mult, ALU.add), t_nT)
                t = dve(lambda e: e.tensor_tensor(xn[:, :], xn[:, :], yb[:, 0:T], ALU.add), t, t_y)
                banks.give(yb, t)
                t = layernorm(xn[:, :], xn[:, :], t)
                t = dve(lambda e: e.tensor_tensor(b3(xn[:, :]), b3(xn[:, :]), bc(w("g1_3"), 1, G), ALU.mult), t)
                t = dve(lambda e: e.tensor_tensor(b3(xn[:, :]), b3(xn[:, :]), bc(w("b1_3"), 1, G), ALU.add), t)
                t_nT = turn(xn, xnT[:, :], t)
                t_h = []
                for n in range(F3 // 128):
                    bank, t = project(w("f1_3", n * 128, (n + 1) * 128), xnT[:, :], t_nT)
                    t = act(lambda e, n=n, bank=bank: e.activation(qk[:, (2 + n) * T:(3 + n) * T], bank[:, 0:T], ACT.Relu,
                                                                   bias=w("fb1_3", n, n + 1)), t)
                    banks.give(bank, t)
                    t_h.append(t)
                zb, was = banks.take()

                def f_step(e, zb=zb):
                    for b in range(G):
                        o = zb[:, b * 128:(b + 1) * 128]
                        for n in range(F3 // 128):
                            e.matmul(o, qk[:, (2 + n) * T + b * 128:(2 + n) * T + (b + 1) * 128],
                                     w("f2_3", n * 128, (n + 1) * 128), start=(n == 0), stop=False)
                        r = add_bias(e, o, "fb2_3")
                    return r
                t_y = pe(f_step, t_h, was)
                t = dve(lambda e, zb=zb: e.tensor_tensor(xn[:, :], xn[:, :], zb[:, 0:T], ALU.add), t_y)
                banks.give(zb, t)
                t = layernorm(xn[:, :], xn[:, :], t)
                t = dve(lambda e: e.tensor_tensor(b3(xn[:, :]), b3(xn[:, :]), bc(w("g2_3"), 1, G), ALU.mult), t)
                t = dve(lambda e: e.tensor_tensor(b3(xn[:, :]), b3(xn[:, :]), bc(w("b2_3"), 1, G), ALU.add), t)
                marks["ctx"] = [t_vp, t_kp, t_cn]
                return dve(lambda e: e.scalar_tensor_tensor(x[:, :], xn[:, :], tg[:, 3:4], x[:, :], ALU.mult, ALU.add), t)

            def mixture3(t_x):
                t_n = layernorm(x[:, :], xn[:, :], t_x)
                t_nT = turn(xn, xnT[:, :], t_n)
                lb, was = banks.take()

                def l_step(e):
                    for b in range(G):
                        r = e.matmul(lb[:, b * E3:(b + 1) * E3], xnT[:, b * 128:(b + 1) * 128], w("gw3"),
                                     start=True, stop=True)
                    return r
                t_l = pe(l_step, t_nT, was)
                ne, ng = G * E3, G * 4
                sc, sb_, mk, pr, w1_, w2_, gmk, gw = (gs[:, i * ne:(i + 1) * ne] for i in range(8))
                t = act(lambda e: e.activation(sc, lb[:, 0:ne], ACT.Exp, scale=-1.0), t_l)
                banks.give(lb, t)
                t_h = []
                for n in range(10):
                    a, t_a = project(w("up3", n * 128, (n + 1) * 128), xnT[:, :], t_nT)
                    h = qk[:, n * T:(n + 1) * T]
                    t_r = act(lambda e, a=a, h=h: e.activation(h, a[:, 0:T], ACT.Relu), t_a)
                    banks.give(a, t_r)
                    t_h.append(act(lambda e, h=h: e.activation(h, h, ACT.Square), t_r))
                t = dve(lambda e: e.tensor_scalar(sc, sc, 1.0, None, ALU.add), t)
                t = dve(lambda e: e.reciprocal(sc, sc), t)
                t = dve(lambda e: e.tensor_tensor(sb_.rearrange("p (b e) -> p b e", b=G),
                                                  sc.rearrange("p (b e) -> p b e", b=G), bc(w("gb3"), 1, G), ALU.add), t)
                t = top(sb_, w1_, w2_, mk, ng, 4, 2, w("rev4"), t)
                t = dve(lambda e: e.tensor_tensor(pr, mk, sb_, ALU.mult), t)
                r1, was = smalls.take()
                t = dve(lambda e: e.tensor_reduce(r1[:, 0:ng], pr.rearrange("p (g e) -> p g e", e=4), AX.X, ALU.add), t, was)
                t = top(r1[:, 0:ng], w1_[:, 0:ng], w2_[:, 0:ng], gmk[:, 0:ng], G, 4, 2, w("rev4"), t)
                smalls.give(r1, t)
                t = dve(lambda e: e.tensor_tensor(sb_.rearrange("p (g e) -> p g e", e=4),
                                                  sb_.rearrange("p (g e) -> p g e", e=4), bc(gmk[:, 0:ng], 2, 4), ALU.mult), t)
                t = top(sb_, w1_, w2_, mk, G, E3, 4, w("rev16"), t)
                t = dve(lambda e: e.tensor_tensor(sc, sc, mk, ALU.mult), t)
                r2_, was = smalls.take()
                sc3 = sc.rearrange("p (b e) -> p b e", b=G)
                t = dve(lambda e: e.tensor_reduce(r2_[:, 0:G], sc3, AX.X, ALU.add), t, was)
                t = dve(lambda e: e.tensor_scalar(r2_[:, 0:G], r2_[:, 0:G], 1e-20, None, ALU.add), t)
                t = dve(lambda e: e.reciprocal(r2_[:, 0:G], r2_[:, 0:G]), t)
                t = dve(lambda e: e.tensor_scalar(r2_[:, 0:G], r2_[:, 0:G], 2.5, None, ALU.mult), t)
                t = dve(lambda e: e.tensor_tensor(sc3, sc3, bc(r2_[:, 0:G], 2, E3), ALU.mult), t)
                smalls.give(r2_, t)
                t_g = turn_gates(sc, E3, t)
                for n in range(8):
                    h = qk[:, n * T:(n + 1) * T]
                    g_, t_w = widen(pick3b[:, n * 128:(n + 1) * 128], gateT[0:3 * E3, :], t_g)
                    t_h[n] = dve(lambda e, g=g_[:, 0:T], h=h: e.tensor_tensor(h, h, g, ALU.mult), t_h[n], t_w)
                    banks.give(g_, t_h[n])
                yb, was = banks.take()

                def step(e):
                    for b in range(G):
                        for n in range(10):
                            r = e.matmul(yb[:, b * 128:(b + 1) * 128], qk[:, n * T + b * 128:n * T + (b + 1) * 128],
                                         w("down3", n * 128, (n + 1) * 128), start=(n == 0), stop=(n == 9))
                    return r
                t = pe(step, t_h, was)
                t_y = dve(lambda e: e.scalar_tensor_tensor(y_st, yb[:, 0:T], tg[:, 7:8], x[:, :], ALU.mult, ALU.add),
                          t, stored)
                banks.give(yb, t_y)
                marks["y"] = t_y
                return t_y

            by_number = (attention0, mixture0, attention1, switched_attention, mlstm, conv_ffn, wide_attention, mixture3)
            t_x = None
            for n in stages:
                t_x = by_number[n](t_x)
            return flow, marks

        lead, rest = range(AHEAD), range(AHEAD, 8)

        def part(*lanes_):
            queues, values = interleave([f for f, _ in lanes_])
            return queues, values, [m for _, m in lanes_]

        before = part((quantise(), None), lane(1, lead))
        turn_part = part(lane(0, range(8)), lane(1, [*rest, *lead]))
        after = part(lane(0, range(8)), lane(1, rest))
        base = {e: len(setup.steps[e]) + len(before[0][e]) for e in ENGINES}
        per_turn = {e: len(turn_part[0][e]) for e in ENGINES}
        for k in range(LANES):
            for what, n in (("ctx", 48), ("x", 16), ("out", 16)):
                base[what, k], per_turn[what, k] = 0 if k == 0 or what == "out" else n, n

        def value(src, n, i):
            return i * per_turn[src] + (base[src] + n)

        def program(name):
            def run(eng):
                def steps(part, value_of, before_=None):
                    queues, values, _ = part
                    waited, begun = {}, set()
                    for k, need, step in queues[name]:
                        if before_ and k not in begun:
                            begun.add(k)
                            for src in ENGINES:
                                if src not in waited:
                                    eng.wait_ge(sems[src], value_of(src, before_[k][src]))
                        for src, n in need.items():
                            m = values[k][src][n] if src in ENGINES else n
                            if m > waited.get(src, 0):
                                waited[src] = m
                                eng.wait_ge(sems[src], value_of(src, m))
                        step(eng).then_inc(sems[name], 1)

                def all_done(value_of):
                    for src in ENGINES:
                        if value_of(src) is not None:
                            eng.wait_ge(sems[src], value_of(src))

                for need, step, _ in setup.steps[name]:
                    for src, n in need.items():
                        eng.wait_ge(sems[src], n)
                    step(eng).then_inc(sems[name], 1)
                made = {e: len(setup.steps[e]) for e in ENGINES}
                all_done(lambda src: made[src] or None)
                steps(before, lambda src, m: made.get(src, 0) + m)
                all_done(lambda src: base[src])
                before_ = {k: {src: turn_part[1][k][src][-1] - per_turn[src] for src in ENGINES} for k in range(LANES)}
                assert all(base[src] + n > 0 for b in before_.values() for src, n in b.items())
                with eng.Fori(0, TURNS - 1) as i:
                    steps(turn_part, lambda src, m: value(src, m, i), before_)
                steps(after, lambda src, m: value(src, m, TURNS - 1), before_)
            return run

        block = ctx.enter_context(nc.Block())
        block.tensor(program("pe"))
        block.scalar(program("act"))
        block.vector(program("dve"))
        block.gpsimd(program("pool"))

        @block.sync
        def _(sp):
            def seqs(i, k):
                return bass.ds((i * LANES + k) * G, G)

            def wait(part, k, t, i):
                sp.wait_ge(sems[t.src], value(t.src, part[1][k][t.src][t.n], i))
                sp.sem_inc(s_step, 1)

            def load_ctx(i, k):
                for dst, src in ((ctxs[k], ctx_in), (masks[k], mask0_in)):
                    sp.dma_start(b3(dst), src[seqs(i, k), :, :].rearrange("b t c -> t b c"))\
                      .then_inc(sems["ctx", k], 16)
                sp.dma_start(ctxTs[k], ctxT_in[:, bass.ds((i * LANES + k) * T, T)]).then_inc(sems["ctx", k], 16)

            def load_x(i, k):
                sp.dma_start(b3(xs[k]), x_in[seqs(i, k), :, :].rearrange("b t c -> t b c"))\
                  .then_inc(sems["x", k], 16)

            first = COLS["sq1"][0]
            load_x(0, 1)
            load_ctx(0, 1)
            sp.dma_start(pick_ld, pick_in).then_inc(s_w, 16)
            sp.dma_start(m1_ld[:, :], mask1_in).then_inc(s_w, 16)
            sp.dma_start(wt[:, 0:first], w_in[:, 0:first]).then_inc(s_w, 16)
            load_x(0, 0)
            load_ctx(0, 0)
            for k in range(LANES):
                sp.sem_inc(sems["out", k], 16)
            sp.dma_start(wt[:, first:NCOLS], w_in[:, first:NCOLS]).then_inc(s_w2, 16)

            def turn_(part, i, last):
                for k in (1, 0):
                    marks = part[2][k]
                    if not last:
                        for t in flat([marks["ctx"], marks["mask"] if k == 0 else None]):
                            wait(part, k, t, i)
                        load_ctx(i + 1, k)
                    wait(part, k, marks["y"], i)
                    if not last:
                        load_x(i + 1, k)
                    sp.dma_start(out[seqs(i, k), :, :].rearrange("b t c -> t b c"), b3(ys[k]))\
                      .then_inc(sems["out", k], 16)

            with sp.Fori(0, TURNS - 1) as i:
                turn_(turn_part, i, False)
            turn_(after, TURNS - 1, True)
            for k in range(LANES):
                sp.wait_ge(sems["out", k], 16 * (TURNS + 1))


def pack_weights(v):
    def row(a):
        return np.broadcast_to(np.asarray(a).reshape(1, -1), (128, np.asarray(a).size))

    def col(a):
        a = np.asarray(a)
        return a.reshape(-1, 128).T

    def tiles(a):
        a = np.asarray(a)
        return a.reshape(-1, 128, a.shape[1]).transpose(1, 0, 2).reshape(128, -1)

    p = np.arange(128)
    f = {k: np.asarray(a) for k, a in v.items()}
    parts = dict(
        ident=np.eye(128, dtype=np.float32),
        causal=np.where(p[None, :] <= p[:, None], 0.0, NEG).astype(np.float32),
        triu=(p[:, None] <= p[None, :]).astype(np.float32),
        head16=(p[:, None] // DH == np.arange(H)[None, :]).astype(np.float32),
        rev8=row(np.arange(8, 0, -1, dtype=np.float32)), rev4=row(np.arange(4, 0, -1, dtype=np.float32)),
        rev16=row(np.arange(16, 0, -1, dtype=np.float32)),
        rows=np.zeros((128, 512), np.float32), part3=(p[:, None] % 32 == np.arange(3)[None, :]).astype(np.float32),
        pick0=np.tile(np.eye(E0, dtype=np.float32), (128 // E0, 1)),
        gates=row(np.concatenate([f["g_xattn"], f["g_ffn"]])),
        wq0=f["L0_xattn_w_q"].T, wk0=f["L0_xattn_w_k"].T, wv0=f["L0_xattn_w_v"].T, wo0=f["L0_xattn_w_o"].T,
        gw0=f["L0_ffn_gate_w"].T, gb0=row(f["L0_ffn_gate_bias"]),
        w1_0=np.concatenate([f["L0_ffn_w1"].reshape(-1, D), f["L0_ffn_sw1"]]).T,
        w3_0=np.concatenate([f["L0_ffn_w3"].reshape(-1, D), f["L0_ffn_sw3"]]).T,
        w2_0=tiles(np.concatenate([f["L0_ffn_w2"].transpose(0, 2, 1).reshape(-1, D), f["L0_ffn_sw2"].T])),
        wq1=f["L1_xattn_Wq"].T, bq1=col(f["L1_xattn_bq"]), wk1=f["L1_xattn_Wk"].T, bk1=col(f["L1_xattn_bk"]),
        wv1=f["L1_xattn_Wv"].T, wo1=f["L1_xattn_Wo"].T,
        sq1=f["L1_ffn_Wq"].reshape(-1, D).T, sk1=f["L1_ffn_Wk"].reshape(-1, D).T,
        sv1=f["L1_ffn_Wv"].reshape(-1, D).T,
        sg1=np.concatenate([f["L1_ffn_Ws"].reshape(-1, D), f["L1_ffn_Wd"].reshape(-1, D)]).T,
        so1=tiles(f["L1_ffn_Wo"].transpose(0, 2, 1).reshape(-1, D)),
        gk2=np.stack([np.concatenate([f["L2_xattn_ig_kernel"][k * 128:(k + 1) * 128],
                                      f["L2_xattn_fg_kernel"][k * 128:(k + 1) * 128]], axis=1)
                      for k in range(3)], axis=1).reshape(128, -1),
        gb2=row(np.concatenate([f["L2_xattn_ig_bias"], f["L2_xattn_fg_bias"]])),
        nw2=row(f["L2_xattn_outnorm_weight"]),
        cw1=f["L2_ffn_w1"].T, conv=row(f["L2_ffn_conv_w"].reshape(F2, 3).T),
        cw2=tiles(f["L2_ffn_w2"].T),
        wq3=f["L3_xattn_Wq"], bq3=col(f["L3_xattn_bq"]), wk3=f["L3_xattn_Wk"], bk3=col(f["L3_xattn_bk"]),
        wv3=f["L3_xattn_Wv"], wo3=f["L3_xattn_Wo"],
        f1_3=f["L3_xattn_W1"], fb1_3=col(f["L3_xattn_b1"]), f2_3=tiles(f["L3_xattn_W2"]),
        g1_3=row(f["L3_xattn_ln1_g"]), b1_3=row(f["L3_xattn_ln1_b"]),
        g2_3=row(f["L3_xattn_ln2_g"]), b2_3=row(f["L3_xattn_ln2_b"]),
        gw3=f["L3_ffn_gate_w"].T, gb3=row(f["L3_ffn_bias_e"]),
        up3=np.concatenate([f["L3_ffn_up_w"].reshape(-1, D), f["L3_ffn_shared_up"]]).T,
        down3=tiles(np.concatenate([f["L3_ffn_down_w"].transpose(0, 2, 1).reshape(-1, D), f["L3_ffn_shared_down"].T])),
    )
    packed = np.empty((128, NCOLS), np.float32)
    for name, (at, n) in COLS.items():
        packed[:, at:at + n] = parts[name]
    rows = dict(bo0=f["L0_xattn_b_o"], bv1=f["L1_xattn_bv"], bo1=f["L1_xattn_bo"], bv3=f["L3_xattn_bv"],
                bo3=f["L3_xattn_bo"], fb2_3=f["L3_xattn_b2"], convb=f["L2_ffn_conv_b"])
    for name, (r, c) in BIAS_ROWS.items():
        at = COLS["rows"][0] + c
        packed[r:r + 3, at:at + rows[name].size] = rows[name]
    return packed


def kernel(**inputs):
    import concourse.bacc as bacc
    from concourse.bass_utils import run_bass_kernel_spmd

    nc = bacc.Bacc("TRN2", target_bir_lowering=False, num_devices=1)
    ctx = np.asarray(inputs["ctx_1024"])
    arrays = {
        "x": np.asarray(inputs["x"]),
        "ctx": ctx,
        "ctxT": np.ascontiguousarray(ctx.transpose(2, 0, 1).reshape(D, B * S)),
        "mask0": np.asarray(inputs["mask_BxSxS2_if1"]),
        "mask1": np.asarray(inputs["mask_1x1xSxS2_bf1"]).reshape(S, S).view(np.uint8),
        "weights": pack_weights(inputs),
        "pick": np.tile(np.repeat(np.eye(E3, dtype=np.float32), 64, axis=1), (3, 1)),
    }
    arrays = {k: np.ascontiguousarray(a) for k, a in arrays.items()}
    args = [nc.dram_tensor(k, a.shape, mybir.dt.from_np(a.dtype), kind="ExternalInput").ap() for k, a in arrays.items()]
    out = nc.dram_tensor("out", (B, S, D), F32, kind="ExternalOutput").ap()
    build(nc, *args, out)
    r = run_bass_kernel_spmd(nc, [arrays], core_ids=[0])
    return r.results[0]["out"]
```
